# Optimizing a Trainium2 kernel written in Bass

```python
import numpy as np
import jax
import jax.numpy as jnp

def _softmax(x, axis=-1):
    return jax.nn.softmax(x, axis=axis)

def _gelu(x):
    return jax.nn.gelu(x, approximate=True)

def _silu(x):
    return jax.nn.silu(x)

def _sigmoid(x):
    return jax.nn.sigmoid(x)

def _layernorm(x, axis=-1, eps=1e-05):
    m = jnp.mean(x, axis=axis, keepdims=True)
    v = jnp.var(x, axis=axis, keepdims=True)
    return (x - m) / jnp.sqrt(v + eps)

def _scatter_add(tgt, idx, src, axis=0):
    return tgt.at[idx].add(src)

def _segment_sum(src, seg, n):
    return jax.ops.segment_sum(src, seg, n)
kernel_name = 'mk_xattn_ffn_d2_seqx_r4_3e536f'

def setup_inputs(seed: int=0):
    np.random.seed(seed)
    _w = jnp.asarray

    def _rec_inputs():
        import jax
        import jax.numpy as jnp
        _rk = jax.random.key(seed)
        x = -0.000125 + 0.9999 * jax.random.normal(jax.random.fold_in(_rk, 1), (16, 512, 256), jnp.float32)
        _lenS = 512 - jax.random.randint(jax.random.fold_in(_rk, 7), (16,), 0, max(1, 512 // 4) + 1, jnp.int32)
        _lenS2 = 64 - jax.random.randint(jax.random.fold_in(_rk, 8), (16,), 0, max(1, 64 // 4) + 1, jnp.int32)
        _ctx_768P = jax.random.normal(jax.random.fold_in(_rk, 11), (16, 16, 192), jnp.float32)
        _ctx_768c = jax.random.dirichlet(jax.random.fold_in(_rk, 511), 0.3 * jnp.ones((16,), jnp.float32), (16, 64))
        _ctx_768t = jnp.einsum('bsk,bkd->bsd', _ctx_768c, _ctx_768P)
        _ctx_768t = _ctx_768t * jax.lax.rsqrt(jnp.mean(jnp.square(_ctx_768t)) + 1e-12) * 0.953939
        ctx_768 = -5.15168e-05 + 0.999825 * (_ctx_768t + 0.3 * jax.random.normal(jax.random.fold_in(_rk, 611), (16, 64, 192), jnp.float32))
        return (x, ctx_768)
    x, ctx_768 = _rec_inputs()

    def _L0_xattn_setup():
        import jax, jax.numpy as jnp
        import numpy as np
        Q_DIM, K_DIM, V_DIM, OUT_DIM = (256, 192, 192, 256)
        key = jax.random.key(seed)
        ks = jax.random.split(key, 9)
        s = lambda d: 1.0 / np.sqrt(d)
        return {'query': jax.random.normal(ks[0], (16, 512, Q_DIM), jnp.float32), 'key': jax.random.normal(ks[1], (16, 512, K_DIM), jnp.float32), 'value': jax.random.normal(ks[2], (16, 512, V_DIM), jnp.float32), 'Wq': jax.random.uniform(ks[3], (OUT_DIM, Q_DIM), jnp.float32, -s(Q_DIM), s(Q_DIM)), 'bq': jax.random.uniform(ks[4], (OUT_DIM,), jnp.float32, -s(Q_DIM), s(Q_DIM)), 'Wk': jax.random.uniform(ks[5], (OUT_DIM, K_DIM), jnp.float32, -s(K_DIM), s(K_DIM)), 'bk': jax.random.uniform(ks[6], (OUT_DIM,), jnp.float32, -s(K_DIM), s(K_DIM)), 'Wv': jax.random.uniform(ks[7], (OUT_DIM, V_DIM), jnp.float32, -s(V_DIM), s(V_DIM)), 'bv': jax.random.uniform(ks[8], (OUT_DIM,), jnp.float32, -s(V_DIM), s(V_DIM))}
    _L0_xattn_all = _L0_xattn_setup()
    _L0_xattn_in = {k: v for k, v in _L0_xattn_all.items() if k in ('Wq', 'bq', 'Wk', 'bk', 'Wv', 'bv')}
    del _L0_xattn_all

    def _L0_ffn_setup():
        import jax, jax.numpy as jnp
        import numpy as np

        def _ln(x, w, b):
            m = jnp.mean(x, axis=-1, keepdims=True)
            v = jnp.var(x, axis=-1, keepdims=True)
            return (x - m) / jnp.sqrt(v + 1e-05) * w + b
        B, T, C = (4, 512, 256)
        E_RWKV, E = (2, 3)
        H = 4 * C
        S = 0.02
        key = jax.random.key(seed)
        ks = jax.random.split(key, 20)
        d = {}
        d['x'] = jax.random.normal(ks[0], (B, T, C), jnp.float32)
        d['v_first'] = jax.random.normal(ks[1], (B, T, C), jnp.float32)
        d['capital_shares'] = jax.random.uniform(ks[2], (E,), jnp.float32)
        d['ln1_w'] = jnp.ones((C,), jnp.float32)
        d['ln1_b'] = jnp.zeros((C,), jnp.float32)
        d['ln2_w'] = jnp.ones((C,), jnp.float32)
        d['ln2_b'] = jnp.zeros((C,), jnp.float32)
        d['Wr'] = S * jax.random.normal(ks[3], (C, C), jnp.float32)
        d['Wv'] = S * jax.random.normal(ks[4], (C, C), jnp.float32)
        d['Wo'] = S * jax.random.normal(ks[5], (C, C), jnp.float32)
        d['Ws'] = S * jax.random.normal(ks[6], (C, C), jnp.float32)
        d['K_rwkv'] = S * jax.random.normal(ks[7], (E_RWKV, C, H), jnp.float32)
        d['V_rwkv'] = S * jax.random.normal(ks[8], (E_RWKV, H, C), jnp.float32)
        d['conf_rwkv'] = S * jax.random.normal(ks[9], (E_RWKV, C), jnp.float32)
        d['W1'] = S * jax.random.normal(ks[10], (C, C), jnp.float32)
        d['W2'] = S * jax.random.normal(ks[11], (C, C), jnp.float32)
        d['W3'] = S * jax.random.normal(ks[12], (C, C), jnp.float32)
        d['conf_trans'] = S * jax.random.normal(ks[13], (C,), jnp.float32)
        d['w_diff'] = S * jax.random.normal(ks[14], (C,), jnp.float32)
        d['W_aff'] = S * jax.random.normal(ks[15], (C, E), jnp.float32)
        d['W_bridge'] = S * jax.random.normal(ks[16], (C, C), jnp.float32)
        return d
    _L0_ffn_all = _L0_ffn_setup()
    _L0_ffn_in = {k: v for k, v in _L0_ffn_all.items() if k in ('v_first', 'capital_shares', 'ln1_w', 'ln1_b', 'ln2_w', 'ln2_b', 'Wr', 'Wv', 'Wo', 'Ws', 'K_rwkv', 'V_rwkv', 'conf_rwkv', 'W1', 'W2', 'W3', 'conf_trans', 'w_diff', 'W_aff', 'W_bridge')}
    del _L0_ffn_all

    def _L1_xattn_setup():
        import jax, jax.numpy as jnp
        import numpy as np
        import math
        E = 256
        EV = 256
        FFN = 1024
        DINO = 192
        B, S, P = (64, 128, 64)

        def bitnet_linear(x, W, b):
            w_scale = jnp.maximum(jnp.mean(jnp.abs(W)), 1e-05)
            qW = jnp.sign(W) * (jnp.abs(W) > 0.5 * w_scale).astype(W.dtype)
            i_scale = jnp.maximum(jnp.max(jnp.abs(x)), 1e-08) / 127.0
            qx = jnp.clip(jnp.round(x / i_scale), -128.0, 127.0)
            out = jnp.einsum('...i,oi->...o', qx, qW) * (w_scale * i_scale)
            return out + b
        key = jax.random.key(seed)
        ks = iter(jax.random.split(key, 32))

        def lin_w(fin, fout):
            return jax.random.normal(next(ks), (fout, fin), jnp.float32) * math.sqrt(2.0 / fin)
        return {'text_embeddings': jax.random.normal(next(ks), (B, S, E), jnp.float32), 'dinov2_features': jax.random.normal(next(ks), (B, P, DINO), jnp.float32), 'W_d2v': lin_w(DINO, EV), 'b_d2v': jnp.zeros((EV,), jnp.float32), 'W_img': lin_w(EV, E), 'b_img': jnp.zeros((E,), jnp.float32), 'W_txt': lin_w(E, E), 'b_txt': jnp.zeros((E,), jnp.float32), 'W_att0': lin_w(E, E // 2), 'b_att0': jnp.zeros((E // 2,), jnp.float32), 'W_att1': lin_w(E, E // 2), 'b_att1': jnp.zeros((E // 2,), jnp.float32), 'W_f1': lin_w(2 * E, FFN), 'b_f1': jnp.zeros((FFN,), jnp.float32), 'W_f2': lin_w(FFN, E), 'b_f2': jnp.zeros((E,), jnp.float32)}
    _L1_xattn_all = _L1_xattn_setup()
    _L1_xattn_in = {k: v for k, v in _L1_xattn_all.items() if k in ('W_d2v', 'b_d2v', 'W_img', 'b_img', 'W_txt', 'b_txt', 'W_att0', 'b_att0', 'W_att1', 'b_att1', 'W_f1', 'b_f1', 'W_f2', 'b_f2')}
    del _L1_xattn_all

    def _L1_ffn_setup():
        import jax, jax.numpy as jnp
        import numpy as np
        DIM = 256

        def _reference_tuple_inner(x, W_r, W_k, W_v, mu_r, mu_k):
            B, T, C = x.shape
            x_prev = jnp.concatenate([jnp.zeros((B, 1, C), x.dtype), x[:, :-1, :]], axis=1)
            xr = mu_r * x + (1.0 - mu_r) * x_prev
            xk = mu_k * x + (1.0 - mu_k) * x_prev
            r = jax.nn.sigmoid(jnp.einsum('btc,dc->btd', xr, W_r))
            k = jnp.einsum('btc,dc->btd', xk, W_k)
            k_act = jnp.square(jax.nn.relu(k))
            out = r * jnp.einsum('btc,dc->btd', k_act, W_v)
            new_state = x[:, -1, :]
            return (out, new_state)
        key = jax.random.key(seed)
        ks = jax.random.split(key, 6)
        B, T, C = (8, 512, DIM)
        x = jax.random.normal(ks[0], (B, T, C), dtype=jnp.float32)
        s = 1.0 / np.sqrt(C)
        W_r = jax.random.uniform(ks[1], (C, C), jnp.float32, -s, s)
        W_k = jax.random.uniform(ks[2], (C, C), jnp.float32, -s, s)
        W_v = jax.random.uniform(ks[3], (C, C), jnp.float32, -s, s)
        mu_r = jax.random.uniform(ks[4], (C,), jnp.float32)
        mu_k = jax.random.uniform(ks[5], (C,), jnp.float32)
        return {'x': x, 'W_r': W_r, 'W_k': W_k, 'W_v': W_v, 'mu_r': mu_r, 'mu_k': mu_k}
    _L1_ffn_all = _L1_ffn_setup()
    _L1_ffn_in = {k: v for k, v in _L1_ffn_all.items() if k in ('W_r', 'W_k', 'W_v', 'mu_r', 'mu_k')}
    del _L1_ffn_all
    return {'x': x, 'ctx_768': ctx_768, 'L0_xattn_Wq': _L0_xattn_in['Wq'], 'L0_xattn_bq': _L0_xattn_in['bq'], 'L0_xattn_Wk': _L0_xattn_in['Wk'], 'L0_xattn_bk': _L0_xattn_in['bk'], 'L0_xattn_Wv': _L0_xattn_in['Wv'], 'L0_xattn_bv': _L0_xattn_in['bv'], 'L0_ffn_v_first': _L0_ffn_in['v_first'], 'L0_ffn_capital_shares': _L0_ffn_in['capital_shares'], 'L0_ffn_ln1_w': _L0_ffn_in['ln1_w'], 'L0_ffn_ln1_b': _L0_ffn_in['ln1_b'], 'L0_ffn_ln2_w': _L0_ffn_in['ln2_w'], 'L0_ffn_ln2_b': _L0_ffn_in['ln2_b'], 'L0_ffn_Wr': _L0_ffn_in['Wr'], 'L0_ffn_Wv': _L0_ffn_in['Wv'], 'L0_ffn_Wo': _L0_ffn_in['Wo'], 'L0_ffn_Ws': _L0_ffn_in['Ws'], 'L0_ffn_K_rwkv': _L0_ffn_in['K_rwkv'], 'L0_ffn_V_rwkv': _L0_ffn_in['V_rwkv'], 'L0_ffn_conf_rwkv': _L0_ffn_in['conf_rwkv'], 'L0_ffn_W1': _L0_ffn_in['W1'], 'L0_ffn_W2': _L0_ffn_in['W2'], 'L0_ffn_W3': _L0_ffn_in['W3'], 'L0_ffn_conf_trans': _L0_ffn_in['conf_trans'], 'L0_ffn_w_diff': _L0_ffn_in['w_diff'], 'L0_ffn_W_aff': _L0_ffn_in['W_aff'], 'L0_ffn_W_bridge': _L0_ffn_in['W_bridge'], 'L1_xattn_W_d2v': _L1_xattn_in['W_d2v'], 'L1_xattn_b_d2v': _L1_xattn_in['b_d2v'], 'L1_xattn_W_img': _L1_xattn_in['W_img'], 'L1_xattn_b_img': _L1_xattn_in['b_img'], 'L1_xattn_W_txt': _L1_xattn_in['W_txt'], 'L1_xattn_b_txt': _L1_xattn_in['b_txt'], 'L1_xattn_W_att0': _L1_xattn_in['W_att0'], 'L1_xattn_b_att0': _L1_xattn_in['b_att0'], 'L1_xattn_W_att1': _L1_xattn_in['W_att1'], 'L1_xattn_b_att1': _L1_xattn_in['b_att1'], 'L1_xattn_W_f1': _L1_xattn_in['W_f1'], 'L1_xattn_b_f1': _L1_xattn_in['b_f1'], 'L1_xattn_W_f2': _L1_xattn_in['W_f2'], 'L1_xattn_b_f2': _L1_xattn_in['b_f2'], 'L1_ffn_W_r': _L1_ffn_in['W_r'], 'L1_ffn_W_k': _L1_ffn_in['W_k'], 'L1_ffn_W_v': _L1_ffn_in['W_v'], 'L1_ffn_mu_r': _L1_ffn_in['mu_r'], 'L1_ffn_mu_k': _L1_ffn_in['mu_k']}

def reference(x, ctx_768, L0_xattn_Wq, L0_xattn_bq, L0_xattn_Wk, L0_xattn_bk, L0_xattn_Wv, L0_xattn_bv, L0_ffn_v_first, L0_ffn_capital_shares, L0_ffn_ln1_w, L0_ffn_ln1_b, L0_ffn_ln2_w, L0_ffn_ln2_b, L0_ffn_Wr, L0_ffn_Wv, L0_ffn_Wo, L0_ffn_Ws, L0_ffn_K_rwkv, L0_ffn_V_rwkv, L0_ffn_conf_rwkv, L0_ffn_W1, L0_ffn_W2, L0_ffn_W3, L0_ffn_conf_trans, L0_ffn_w_diff, L0_ffn_W_aff, L0_ffn_W_bridge, L1_xattn_W_d2v, L1_xattn_b_d2v, L1_xattn_W_img, L1_xattn_b_img, L1_xattn_W_txt, L1_xattn_b_txt, L1_xattn_W_att0, L1_xattn_b_att0, L1_xattn_W_att1, L1_xattn_b_att1, L1_xattn_W_f1, L1_xattn_b_f1, L1_xattn_W_f2, L1_xattn_b_f2, L1_ffn_W_r, L1_ffn_W_k, L1_ffn_W_v, L1_ffn_mu_r, L1_ffn_mu_k):
    import jax
    import jax.numpy as jnp

    def _L0_xattn_ref(query, key, value, Wq, bq, Wk, bk, Wv, bv):
        import jax, jax.numpy as jnp
        import numpy as np
        Q_DIM, K_DIM, V_DIM, OUT_DIM = (256, 192, 192, 256)
        scale = OUT_DIM ** (-0.5)
        q = jnp.einsum('bsd,od->bso', query, Wq) + bq
        k = jnp.einsum('bsd,od->bso', key, Wk) + bk
        v = jnp.einsum('bsd,od->bso', value, Wv) + bv
        scores = jnp.einsum('bqo,bko->bqk', q, k) * scale
        probs = jax.nn.softmax(scores, axis=-1)
        return jnp.einsum('bqk,bko->bqo', probs, v)

    def _L0_ffn_ref(x, v_first, capital_shares, ln1_w, ln1_b, ln2_w, ln2_b, Wr, Wv, Wo, Ws, K_rwkv, V_rwkv, conf_rwkv, W1, W2, W3, conf_trans, w_diff, W_aff, W_bridge):
        import jax, jax.numpy as jnp
        import numpy as np

        def _ln(x, w, b):
            m = jnp.mean(x, axis=-1, keepdims=True)
            v = jnp.var(x, axis=-1, keepdims=True)
            return (x - m) / jnp.sqrt(v + 1e-05) * w + b
        B, T, C = x.shape
        xln = _ln(x, ln1_w, ln1_b)
        att_out = jax.nn.sigmoid(xln @ Wr) * (xln @ Wv) @ Wo
        rwkv_state = xln @ Ws
        x = x + att_out
        h = _ln(x, ln2_w, ln2_b)
        conf_r = jax.nn.sigmoid(jnp.einsum('btc,ec->bte', h, conf_rwkv))
        conf_t = jax.nn.sigmoid(h @ conf_trans)[..., None]
        confidences = jnp.concatenate([conf_r, conf_t], axis=-1)
        E = confidences.shape[-1]
        difficulty = jax.nn.sigmoid(h @ w_diff)[..., None]
        affinity = h @ W_aff
        bids = confidences * capital_shares * difficulty + affinity
        winners = jnp.argmax(bids, axis=-1)
        flat_h = h.reshape(-1, C)
        flat_state = rwkv_state.reshape(-1, C)
        flat_w = winners.reshape(-1)
        flat_conf = confidences.reshape(-1, E)
        win_conf = jnp.take_along_axis(flat_conf, flat_w[:, None], axis=1)
        scale = win_conf / (jax.lax.stop_gradient(win_conf) + 1e-06)
        hr = jnp.square(jax.nn.relu(jnp.einsum('nc,ech->enh', flat_h, K_rwkv)))
        out_rwkv = jnp.einsum('enh,ehc->enc', hr, V_rwkv)
        out_trans = flat_h @ W1 * jax.nn.sigmoid(flat_state @ W2) @ W3
        all_out = jnp.concatenate([out_rwkv, out_trans[None]], axis=0)
        onehot = jax.nn.one_hot(flat_w, E, dtype=flat_h.dtype)
        final = jnp.einsum('ne,enc->nc', onehot, all_out) * scale
        return x + final.reshape(B, T, C)

    def _L1_xattn_ref(text_embeddings, dinov2_features, W_d2v, b_d2v, W_img, b_img, W_txt, b_txt, W_att0, b_att0, W_att1, b_att1, W_f1, b_f1, W_f2, b_f2):
        import jax, jax.numpy as jnp
        import numpy as np
        import math
        E = 256
        EV = 256
        FFN = 1024
        DINO = 192
        B, S, P = (64, 128, 64)

        def bitnet_linear(x, W, b):
            w_scale = jnp.maximum(jnp.mean(jnp.abs(W)), 1e-05)
            qW = jnp.sign(W) * (jnp.abs(W) > 0.5 * w_scale).astype(W.dtype)
            i_scale = jnp.maximum(jnp.max(jnp.abs(x)), 1e-08) / 127.0
            qx = jnp.clip(jnp.round(x / i_scale), -128.0, 127.0)
            out = jnp.einsum('...i,oi->...o', qx, qW) * (w_scale * i_scale)
            return out + b
        b, s, e = text_embeddings.shape
        vis = bitnet_linear(dinov2_features, W_d2v, b_d2v)
        image_embeds = bitnet_linear(vis, W_img, b_img)
        fused = bitnet_linear(text_embeddings, W_txt, b_txt)
        inv_sqrt_e = 1.0 / math.sqrt(e)
        for Wa, ba in ((W_att0, b_att0), (W_att1, b_att1)):
            kv = bitnet_linear(image_embeds, Wa, ba)
            k = jnp.concatenate([kv, kv], axis=-1)
            scores = jnp.einsum('bse,bpe->bsp', fused, k) * inv_sqrt_e
            attn = jax.nn.softmax(scores, axis=-1)
            fused = fused + 0.1 * jnp.einsum('bsp,bpe->bse', attn, k)
        avg_img = jnp.mean(image_embeds, axis=1, keepdims=True)
        concatenated = jnp.concatenate([fused, jnp.broadcast_to(avg_img, (b, s, e))], axis=-1)
        h = jax.nn.relu(bitnet_linear(concatenated, W_f1, b_f1))
        return bitnet_linear(h, W_f2, b_f2)

    def _L1_ffn_ref(x, W_r, W_k, W_v, mu_r, mu_k):
        import jax, jax.numpy as jnp
        import numpy as np
        DIM = 256

        def _reference_tuple_inner(x, W_r, W_k, W_v, mu_r, mu_k):
            B, T, C = x.shape
            x_prev = jnp.concatenate([jnp.zeros((B, 1, C), x.dtype), x[:, :-1, :]], axis=1)
            xr = mu_r * x + (1.0 - mu_r) * x_prev
            xk = mu_k * x + (1.0 - mu_k) * x_prev
            r = jax.nn.sigmoid(jnp.einsum('btc,dc->btd', xr, W_r))
            k = jnp.einsum('btc,dc->btd', xk, W_k)
            k_act = jnp.square(jax.nn.relu(k))
            out = r * jnp.einsum('btc,dc->btd', k_act, W_v)
            new_state = x[:, -1, :]
            return (out, new_state)
        return _reference_tuple_inner(x, W_r, W_k, W_v, mu_r, mu_k)[0]
    x = x + _L0_xattn_ref(_layernorm(x, axis=-1), ctx_768, ctx_768, L0_xattn_Wq, L0_xattn_bq, L0_xattn_Wk, L0_xattn_bk, L0_xattn_Wv, L0_xattn_bv)
    x = x + _L0_ffn_ref(_layernorm(x, axis=-1), L0_ffn_v_first, L0_ffn_capital_shares, L0_ffn_ln1_w, L0_ffn_ln1_b, L0_ffn_ln2_w, L0_ffn_ln2_b, L0_ffn_Wr, L0_ffn_Wv, L0_ffn_Wo, L0_ffn_Ws, L0_ffn_K_rwkv, L0_ffn_V_rwkv, L0_ffn_conf_rwkv, L0_ffn_W1, L0_ffn_W2, L0_ffn_W3, L0_ffn_conf_trans, L0_ffn_w_diff, L0_ffn_W_aff, L0_ffn_W_bridge)
    x = x + _L1_xattn_ref(_layernorm(x, axis=-1), ctx_768, L1_xattn_W_d2v, L1_xattn_b_d2v, L1_xattn_W_img, L1_xattn_b_img, L1_xattn_W_txt, L1_xattn_b_txt, L1_xattn_W_att0, L1_xattn_b_att0, L1_xattn_W_att1, L1_xattn_b_att1, L1_xattn_W_f1, L1_xattn_b_f1, L1_xattn_W_f2, L1_xattn_b_f2)
    x = x + _L1_ffn_ref(_layernorm(x, axis=-1), L1_ffn_W_r, L1_ffn_W_k, L1_ffn_W_v, L1_ffn_mu_r, L1_ffn_mu_k)
    return x

_drawn_inputs = setup_inputs


def setup_inputs(seed=0):
    import zlib

    import numpy as np

    out = dict(_drawn_inputs(seed))
    spreads = {'L0_ffn_ln1_w': (1.0, 0.6),
     'L0_ffn_ln1_b': (0.0, 0.8),
     'L0_ffn_ln2_w': (1.0, 0.6),
     'L0_ffn_ln2_b': (0.0, 0.537),
     'L1_xattn_b_d2v': (0.0, 0.429),
     'L1_xattn_b_img': (0.0, 0.35),
     'L1_xattn_b_txt': (0.0, 0.375),
     'L1_xattn_b_att0': (0.0, 2.0),
     'L1_xattn_b_att1': (0.0, 2.0),
     'L1_xattn_b_f1': (0.0, 0.267),
     'L1_xattn_b_f2': (0.0, 0.1)}
    factors = {'L0_xattn_bq': 8.0,
     'L0_xattn_bk': 200.0,
     'L0_ffn_capital_shares': 2.982,
     'L0_ffn_Wr': 8.0,
     'L0_ffn_Ws': 8.0,
     'L0_ffn_conf_rwkv': 5.478,
     'L0_ffn_W1': 4.124,
     'L0_ffn_W2': 8.0,
     'L0_ffn_W3': 4.113,
     'L0_ffn_conf_trans': 8.0,
     'L0_ffn_w_diff': 8.0,
     'L1_xattn_W_att0': 5.457,
     'L1_xattn_W_att1': 5.33,
     'L1_ffn_W_r': 6.273,
     'L1_ffn_mu_r': 8.0,
     'L1_ffn_mu_k': 2.691}
    for name, (base, spread) in spreads.items():
        noise = np.random.default_rng([zlib.crc32(name.encode()), seed]).standard_normal(out[name].shape)
        drawn = base * np.exp(spread * noise) if base else spread * noise
        out[name] = jnp.asarray(drawn.astype(out[name].dtype))
    for name, factor in factors.items():
        out[name] = (out[name] * factor).astype(out[name].dtype)
    return out
```

```python
from contextlib import ExitStack

import concourse.bass as bass
from concourse import mybir

F32, F32R, BF16 = mybir.dt.float32, mybir.dt.float32r, mybir.dt.bfloat16
ALU = mybir.AluOpType
ACT = mybir.ActivationFunctionType
X, XY = mybir.AxisListType.X, mybir.AxisListType.XY
RED = bass.bass_isa.ReduceOp

P = 128
B, T, C = 16, 512, 256
NT = T // P
KC = C // P
S, D = 64, 192
H = 1024
HC = H // P
NCTX = B * S
EPS = 1e-5
ROUND = 12582912.0
INV_SQRT = 1.0 / 16.0
NCHUNK = 2 + 2 * HC
GROUP_END = {1: 0, 1 + HC: 1, 1 + 2 * HC: 2}
GROUP_EXPERT = (2, 0, 1)

COLS = {}
for _name, _n in (("bq", 2), ("bk", 2), ("ln1_w", 2), ("ln1_b", 2), ("ln2_w", 2), ("ln2_b", 2), ("b_d2v", 2),
                  ("b_img", 2), ("b_txt", 2), ("b_att0", 1), ("b_att1", 1), ("b_f1", 8), ("mu_r", 2), ("mu_k", 2)):
    COLS[_name] = (sum(n for _, n in COLS.values()), _n)
NCOLS = sum(n for _, n in COLS.values())


class Steps:

    def __init__(self, eng, sem, base=0):
        self.eng, self.sem, self.base, self.n = eng, sem, base, 0

    def add(self, ins):
        ins.then_inc(self.sem, 1)
        self.n += 1

    def wait(self):
        self.eng.wait_ge(self.sem, self.base + self.n)

    def link(self, ins):
        self.add(ins)
        self.wait()


def after(eng, sem, value):
    if not isinstance(value, int) or value > 0:
        eng.wait_ge(sem, value)


def build(nc, a, out):
    x3_dram = nc.dram_tensor("x3_scratch", [B, T, C], F32, kind="Internal").ap()
    text_dram = nc.dram_tensor("text_scratch", [B, T, C], F32, kind="Internal").ap()
    ms_dram = nc.dram_tensor("ms_scratch", [B, P, KC * S], F32, kind="Internal").ap()
    vs_dram = nc.dram_tensor("vs_scratch", [B, S, C], F32, kind="Internal").ap()
    cs_dram = nc.dram_tensor("cs_scratch", [B, 1, S], F32, kind="Internal").ap()
    kv_dram = nc.dram_tensor("kv_scratch", [B, P, 2 * S], F32, kind="Internal").ap()
    kvt_dram = nc.dram_tensor("kvt_scratch", [B, S, 2 * P], F32, kind="Internal").ap()

    with ExitStack() as top:
        stack = [top]

        def sb(name, shape, dt=F32):
            return stack[-1].enter_context(nc.sbuf_tensor(name, shape, dt))

        def sem(name):
            return top.enter_context(nc.semaphore(name))

        psum = [top.enter_context(nc.psum_tensor(f"pair{k}", [P, 1024], F32)) for k in range(4)]
        up_ps, out_ps, tp_ps, g_ps = psum

        cols = sb("cols", [P, NCOLS])

        def col(name, k=0):
            at, n = COLS[name]
            assert k < n
            return cols[:, at + k:at + k + 1]

        rows = sb("rows", [P, 2 * C + 3])
        bv_row, bf2_row, cap = rows[:, 0:C], rows[:, C:2 * C], rows[:, 2 * C:2 * C + 3]
        ident = sb("ident", [P, P])
        ident_b = sb("ident_b", [P, P], BF16)
        ones = sb("ones", [1, P])
        neg_half = sb("neg_half", [P, NT])
        wtxt = sb("wtxt", [P, KC, C], BF16)
        watt = sb("watt", [P, KC, 2, P], BF16)
        wf1 = sb("wf1", [P, 2 * KC, H], BF16)
        wf2 = sb("wf2", [P, HC, C], BF16)
        q_img = sb("q_img", [P, KC, NCTX], BF16)
        avg = sb("avg", [P, KC, B])
        NW = 7
        W_D2V, W_IMG, W_TXT, W_A0, W_A1, W_F1, W_F2 = range(NW)
        wabs = sb("wabs", [P, NW])
        wsum = sb("wsum", [P, NW])
        wscale = sb("wscale", [P, NW])
        thr = sb("thr", [P, 2, NW])
        NA_ = 6
        A_CTX, A_VIS, A_IMG, A_TXT, A_CAT, A_H = range(NA_)
        amax = sb("amax", [P, NA_])
        gmax = sb("gmax", [P, NA_])
        iscale = sb("iscale", [P, NA_])
        inv = sb("inv", [P, NA_])
        oscale = sb("oscale", [P, 8])
        tmax = sb("tmax", [P, 1])
        tcur = sb("tcur", [P, 1])
        small = sb("small", [P, 64])

        v_set, p_set = sem("setup_dve"), sem("setup_pool")

        kv_scope = ExitStack()
        stack.append(kv_scope)
        names = ("Wr", "W2s", "Wv", "Wo", "W1", "W3")
        w = {n: (sb(n + "_hi", [P, KC, C], F32R), sb(n + "_lo", [P, KC, C], F32R)) for n in names}
        kexp = (sb("kexp_hi", [P, 2 * KC, H], F32R), sb("kexp_lo", [P, 2 * KC, H], F32R))
        vexp = (sb("vexp_hi", [P, 2 * HC, C], F32R), sb("vexp_lo", [P, 2 * HC, C], F32R))
        wb = sb("wb", [P, KC, 7])

        def mm3(pe, dst, st, mv, start, stop):
            pe.matmul(dst, st[1], mv[0], start=start, stop=False, skip_group_check=True)
            pe.matmul(dst, st[0], mv[1], start=False, stop=False, skip_group_check=True)
            return pe.matmul(dst, st[0], mv[0], start=False, stop=stop, skip_group_check=True)

        def stats(st, src, stat, mean, var, tmp, ready):
            for t in range(NT):
                st.add(st.eng.bn_stats(stat[:, t, :], src[:, t, :]))
            st.wait()
            e = lambda q: stat[:, :, q:q + 1].rearrange("p t o -> p (t o)")
            st.add(st.eng.tensor_tensor(mean[:, :], e(1), e(4), ALU.add))
            st.add(st.eng.tensor_tensor(tmp[:, :], e(1), e(4), ALU.subtract))
            st.link(st.eng.tensor_tensor(var[:, :], e(2), e(5), ALU.add))
            st.add(st.eng.tensor_scalar(mean[:, :], mean[:, :], 0.5, None, ALU.mult))
            st.add(st.eng.tensor_tensor(tmp[:, :], tmp[:, :], tmp[:, :], ALU.mult))
            st.link(st.eng.tensor_scalar(var[:, :], var[:, :], 1.0 / C, EPS, ALU.mult, ALU.add))
            st.eng.scalar_tensor_tensor(out=var[:, :], in0=tmp[:, :], scalar=0.25, in1=var[:, :],
                                   op0=ALU.mult, op1=ALU.add).then_inc(ready, 1)

        def pair(t, *ix):
            return (t[0][ix], t[1][ix])

        with ExitStack() as scope:
            stack.append(scope)
            stg = [sb(f"stg{k}", [P, 4096]) for k in range(2)]
            ctx = sb("ctx", [P, 2, NCTX])
            act = sb("act", [P, KC, NCTX])
            qa = sb("qa", [P, KC, NCTX], BF16)
            ms_all = act
            cs_all = sb("cs_all", [1, NCTX])
            v_all = sb("v_all", [S, B, C])
            stored = sem("setup_stored")

            ternary = [("d2v", W_D2V), ("img", W_IMG), ("txt", W_TXT), ("att", W_A0), ("f1", W_F1), ("f2", W_F2)]
            wd2v = sb("wd2v", [P, 2, C], BF16)
            wimg = sb("wimg", [P, KC, C], BF16)
            tern_dst = {"d2v": wd2v, "img": wimg, "txt": wtxt, "att": watt, "f1": wf1, "f2": wf2}
            tern_n = {"d2v": 2 * C, "img": KC * C, "txt": KC * C, "att": KC * C, "f1": 4 * H, "f2": HC * C}
            ta = sb("ta", [P, 2048], BF16)
            tb_ = sb("tb_", [P, 2048], BF16)

            with nc.Block() as block:
                loads = []
                kpn = lambda ap: ap.rearrange("(k p) n -> p k n", p=P)

                def view(k, chunks, n):
                    return stg[k][:, 0:chunks * n].rearrange("p (k n) -> p k n", k=chunks)

                v0 = view(0, 2, C)
                loads.append((0, [(v0[:, 0, :], a["d2v"][0:P, :]), (v0[0:D - P, 1, :], a["d2v"][P:D, :])]))
                loads.append((1, [(view(1, 2, C), kpn(a["img"]))]))
                loads.append((0, [(view(0, 2, C), kpn(a["txt"]))]))
                loads.append((1, [(view(1, 2, C), kpn(a["att"]))]))
                loads.append((0, [(view(0, 4, H), kpn(a["f1"]))]))
                loads.append((1, [(view(1, 8, C), kpn(a["f2"]))]))
                loads.append((0, [(view(0, 2, C), kpn(a["Wr"]))]))
                loads.append((1, [(view(1, 2, C), kpn(a["Wv"]))]))
                loads.append((0, [(view(0, 2, C), kpn(a["Wo"]))]))
                loads.append((1, [(view(1, 2, C), kpn(a["W1"]))]))
                loads.append((0, [(view(0, 2, C), kpn(a["W3"]))]))
                loads.append((1, [(view(1, 4, H), kpn(a["K"]))]))
                loads.append((0, [(view(0, 16, C), kpn(a["V"]))]))
                loads.append((1, [(stg[1][:, 0:512].rearrange("p (k n) -> p k n", k=2), kpn(a["WsT"])),
                                  (stg[1][:, 512:1024].rearrange("p (k n) -> p k n", k=2), kpn(a["W2"]))]))
                loads.append((0, [(stg[0][:, 0:512].rearrange("p (k n) -> p k n", k=2), kpn(a["Wq"])),
                                  (stg[0][:, 512:768], a["WkT"][0:P, :]), (stg[0][0:D - P, 768:1024], a["WkT"][P:D, :]),
                                  (stg[0][:, 1024:1280], a["WvT"][0:P, :]), (stg[0][0:D - P, 1280:1536], a["WvT"][P:D, :])]))
                ctx_k = stg[1][:, 2048:4096].rearrange("p (k n) -> p k n", k=2)
                stg_loaded, stg_used = sem("stg_loaded"), sem("stg_used")
                n_loaded = []
                for k, parts in loads:
                    n_loaded.append((n_loaded[-1] if n_loaded else 0) + 16 * len(parts))
                consts_loaded, ctx_zeroed = sem("consts_loaded"), sem("ctx_zeroed")

                @block.sync
                def _(sp):
                    sp.dma_start(cols[:, :], a["cols"]).then_inc(consts_loaded, 16)
                    sp.dma_start(rows[:, :], a["rows"].partition_broadcast(P)).then_inc(consts_loaded, 16)
                    sp.dma_start(wb[:, :, :], kpn(a["wb"])).then_inc(consts_loaded, 16)
                    sp.wait_ge(ctx_zeroed, 3)
                    sp.dma_start(ctx[:, 0, :], a["ctxT"][0:P, :]).then_inc(consts_loaded, 16)
                    sp.dma_start(ctx[0:D - P, 1, :], a["ctxT"][P:D, :]).then_inc(consts_loaded, 16)
                    for n, (k, parts) in enumerate(loads):
                        if n >= 2:
                            sp.wait_ge(stg_used, n - 1)
                        for dst, src in parts:
                            sp.dma_start(dst, src).then_inc(stg_loaded, 16)
                        sp.wait_ge(stg_loaded, n_loaded[n])

                sw_w = sem("weight_sums"), sem("weight_sums_all")
                am_s, gm_s = sem("act_max"), sem("act_max_all")
                q_ready, lin_done, f32_ready = sem("q_ready"), sem("lin_done"), sem("lin_f32")

                @block.gpsimd
                def _(g):
                    g.memset(ident[:, :], 0.0).then_inc(p_set, 1)
                    g.memset(ident_b[:, :], 0.0).then_inc(p_set, 1)
                    g.memset(ones[:, :], 1.0).then_inc(p_set, 1)
                    g.memset(neg_half[:, :], -0.5).then_inc(p_set, 1)
                    g.wait_ge(p_set, 4)
                    for m in (ident, ident_b):
                        g.affine_select(out=m[:, :], in_=m[:, :], compare_op=ALU.not_equal, fill=1.0, base=0,
                                        pattern=[[-1, P]], channel_multiplier=1).then_inc(p_set, 1)
                    for k in range(NW):
                        g.wait_ge(sw_w[0], k + 1)
                        g.partition_all_reduce(wsum[:, k:k + 1], wabs[:, k:k + 1], P, RED.add).then_inc(sw_w[1], 1)
                        if k == W_D2V:
                            g.wait_ge(am_s, 1)
                            g.partition_all_reduce(gmax[:, 0:1], amax[:, 0:1], P, RED.max).then_inc(gm_s, 1)
                    for k in (1, 2):
                        g.wait_ge(am_s, k + 1)
                        g.partition_all_reduce(gmax[:, k:k + 1], amax[:, k:k + 1], P, RED.max).then_inc(gm_s, 1)

                w2s_split = sem("w2s_split")
                kx_done, kx_ready = sem("kx_done"), sem("kx_ready")

                @block.vector
                def _(v):
                    st = Steps(v, v_set)
                    v.memset(ctx[:, 1, :], 0.0).then_inc(ctx_zeroed, 1)
                    v.memset(stg[0][:, 0:512], 0.0).then_inc(ctx_zeroed, 1)
                    v.memset(tmax[:, :], 0.0).then_inc(ctx_zeroed, 1)

                    def act_max(k, src):
                        v.tensor_reduce(amax[:, k:k + 1], src, XY, ALU.max, apply_absolute_value=True).then_inc(am_s, 1)

                    def act_scale(k):
                        v.wait_ge(gm_s, k + 1)
                        st.link(v.tensor_scalar(iscale[:, k:k + 1], gmax[:, k:k + 1], 1e-8, 1.0 / 127.0, ALU.max, ALU.mult))
                        st.link(v.reciprocal(inv[:, k:k + 1], iscale[:, k:k + 1]))

                    def quantise(k, src, dst):
                        for c in range(2):
                            y = stg[1][:, 2048 + 1024 * c:3072 + 1024 * c]
                            st.link(v.tensor_scalar(y, src[:, c, :], inv[:, k:k + 1], ROUND, ALU.mult, ALU.add))
                            last = v.tensor_scalar(dst[:, c, :], y, ROUND, None, ALU.subtract)
                        last.then_inc(q_ready, 1)

                    v.wait_ge(consts_loaded, 80)
                    act_max(A_CTX, ctx[:, :, :])
                    for n, (name, k0) in enumerate(ternary):
                        v.wait_ge(stg_loaded, n_loaded[n])
                        size = tern_n[name]
                        flat = stg[loads[n][0]][:, 0:size]
                        if name == "att":
                            f3 = flat.rearrange("p (k a n) -> p k a n", k=KC, a=2)
                            for j in range(2):
                                v.tensor_reduce(wabs[:, k0 + j:k0 + j + 1], f3[:, :, j, :], XY, ALU.add,
                                                apply_absolute_value=True).then_inc(sw_w[0], 1)
                            jobs = [(k0 + j, f3[:, :, j, :], watt[:, :, j, :], C * P) for j in range(2)]
                        else:
                            v.tensor_reduce(wabs[:, k0:k0 + 1], flat, X, ALU.add,
                                            apply_absolute_value=True).then_inc(sw_w[0], 1)
                            dst = tern_dst[name][:, :, :].rearrange("p k n -> p (k n)")
                            total = {"d2v": D * C, "img": C * C, "txt": C * C, "f1": 2 * C * H, "f2": H * C}[name]
                            half = min(size, 2048)
                            jobs = [(k0, flat[:, o:o + half], dst[:, o:o + half], total) for o in range(0, size, half)]
                        for j, (k, src, dst, total) in enumerate(jobs):
                            if name == "att" or j == 0:
                                v.wait_ge(sw_w[1], k + 1)
                                st.link(v.tensor_scalar(wscale[:, k:k + 1], wsum[:, k:k + 1], 1.0 / total, 1e-5, ALU.mult, ALU.max))
                                st.add(v.tensor_scalar(thr[:, 0, k:k + 1], wscale[:, k:k + 1], 0.5, None, ALU.mult))
                                st.link(v.tensor_scalar(thr[:, 1, k:k + 1], wscale[:, k:k + 1], -0.5, None, ALU.mult))
                            if name == "att":
                                up = ta[:, 0:C].rearrange("p (k n) -> p k n", k=KC)
                                dn = tb_[:, 0:C].rearrange("p (k n) -> p k n", k=KC)
                            else:
                                up, dn = ta[:, 0:src.shape[1]], tb_[:, 0:src.shape[1]]
                            st.add(v.tensor_scalar(up, src, thr[:, 0, k:k + 1], None, ALU.is_gt))
                            st.link(v.tensor_scalar(dn, src, thr[:, 1, k:k + 1], None, ALU.is_lt))
                            st.link(v.tensor_tensor(dst, up, dn, ALU.subtract))
                        v.sem_inc(stg_used, 1)
                        if name == "d2v":
                            act_scale(A_CTX)
                            st.link(v.tensor_tensor(oscale[:, 0:1], wscale[:, 0:1], iscale[:, 0:1], ALU.mult))
                            quantise(A_CTX, ctx, qa)
                    for k, wk in ((A_VIS, W_IMG), (A_IMG, None)):
                        v.wait_ge(f32_ready, 4 * k)
                        act_max(k, act[:, :, :])
                        act_scale(k)
                        if wk is not None:
                            st.link(v.tensor_tensor(oscale[:, k:k + 1], wscale[:, wk:wk + 1], iscale[:, k:k + 1], ALU.mult))
                        v.wait_ge(lin_done, 4 * k)
                        v.wait_ge(stg_loaded, n_loaded[7])
                        quantise(k, act, qa if k == A_VIS else q_img)
                    av = act[:, :, :].rearrange("p k (b s) -> p (k b) s", s=S)
                    st.link(v.tensor_reduce(avg[:, :, :].rearrange("p k b -> p (k b)"), av, X, ALU.add))
                    st.link(v.tensor_scalar(avg[:, :, :], avg[:, :, :], 1.0 / S, None, ALU.mult))

                    def split(dst, src):
                        hi, lo = dst
                        n = src.shape[1]
                        st.link(v.tensor_copy(hi, src))
                        st.link(v.tensor_tensor(lo, src, hi.bitcast(F32), ALU.subtract))

                    fl = lambda t: tuple(u[:, :, :].rearrange("p k n -> p (k n)") for u in t)
                    for n, name in ((6, "Wr"), (7, "Wv"), (8, "Wo"), (9, "W1"), (10, "W3"), (11, "K"), (12, "V")):
                        v.wait_ge(stg_loaded, n_loaded[n])
                        t = {"K": kexp, "V": vexp}.get(name) or w[name]
                        size = 4096 if name in "KV" else 512
                        src = stg[loads[n][0]][:, 0:size]
                        if name in ("Wo", "W3"):
                            st.link(v.tensor_scalar(src, src, 0.5, None, ALU.mult))
                        split(fl(t), src)
                        v.sem_inc(stg_used, 1)
                    v.wait_ge(kx_done, 1)
                    st.link(v.tensor_copy(stg[1][:, 2048:2560], tp_ps[:, 0:512]))
                    split(fl(w["W2s"]), stg[1][:, 2048:2560])
                    v.sem_inc(w2s_split, 1)
                    v.wait_ge(kx_done, 2)
                    for c, ps in ((0, tp_ps), (1, g_ps)):
                        last = v.tensor_scalar(ctx_k[:, c, :], ps[:, :], col("bk", c), None, ALU.add)
                    last.then_inc(kx_ready, 1)
                    v.wait_ge(kx_done, 3)
                    for c, ps in ((0, tp_ps), (1, g_ps)):
                        v.tensor_scalar(ms_all[:, c, :], ps[:, :], INV_SQRT, None, ALU.mult)
                    v.tensor_scalar(cs_all[:, :], up_ps[0:1, :], INV_SQRT, None, ALU.mult).then_inc(kx_ready, 1)
                    for q in range(B // 4):
                        v.wait_ge(kx_done, 4 + q)
                        for b in range(4):
                            last = v.tensor_tensor(v_all[:, 4 * q + b, :], (out_ps, up_ps)[q % 2][0:S, b * C:(b + 1) * C],
                                                   bv_row[0:S, :], ALU.add)
                        last.then_inc(kx_ready, 1)


                @block.scalar
                def _(s):
                    for k, bias in ((0, "b_d2v"), (1, "b_img")):
                        for c in range(2):
                            for h in range(2):
                                s.wait_ge(lin_done, 4 * k + 2 * c + h + 1)
                                s.activation(act[:, c, h * 512:(h + 1) * 512], (tp_ps, g_ps)[c][:, h * 512:(h + 1) * 512],
                                             ACT.Identity, bias=col(bias, c), scale=oscale[:, k:k + 1]).then_inc(f32_ready, 1)
                    s.wait_ge(kx_ready, 2)
                    s.dma_start(ms_dram.rearrange("b p (k s) -> p k b s", k=KC)[:, 0], ms_all[:, 0, :].rearrange("p (b s) -> p b s", s=S)).then_inc(stored, 16)
                    s.dma_start(ms_dram.rearrange("b p (k s) -> p k b s", k=KC)[:, 1], ms_all[:, 1, :].rearrange("p (b s) -> p b s", s=S)).then_inc(stored, 16)
                    s.dma_start(cs_dram.rearrange("b o s -> o b s"), cs_all[:, :].rearrange("p (b s) -> p b s", s=S)).then_inc(stored, 16)
                    s.wait_ge(kx_ready, 2 + B // 4)
                    s.dma_start(vs_dram.rearrange("b s c -> s b c"), v_all[:, :, :]).then_inc(stored, 16)
                    s.wait_ge(stored, 64)

                @block.tensor
                def _(pe):
                    for k, wt in ((0, wd2v), (1, wimg)):
                        pe.wait_ge(q_ready, k + 1)
                        for c in range(2):
                            for h in range(2):
                                for j in range(2):
                                    m = pe.matmul((tp_ps, g_ps)[c][:, h * 512:(h + 1) * 512], wt[:, j, c * P:(c + 1) * P],
                                                  qa[:, j, h * 512:(h + 1) * 512], start=(j == 0), stop=(j == 1))
                                m.then_inc(lin_done, 1)
                    pe.wait_ge(stg_loaded, n_loaded[13])
                    pe.wait_ge(f32_ready, 8)
                    wst, w2 = stg[1][:, 0:512].rearrange("p (k n) -> p k n", k=2), stg[1][:, 512:1024].rearrange("p (k n) -> p k n", k=2)
                    for c in range(2):
                        for j in range(2):
                            m = pe.matmul(tp_ps[:, c * C:(c + 1) * C], wst[:, j, c * P:(c + 1) * P], w2[:, j, :],
                                          start=(j == 0), stop=(j == 1))
                    m.then_inc(kx_done, 1)
                    pe.wait_ge(stg_loaded, n_loaded[14])
                    pe.wait_ge(w2s_split, 1)
                    wq = stg[0][:, 0:512].rearrange("p (k n) -> p k n", k=2)
                    wk = stg[0][:, 512:1024].rearrange("p (k n) -> p k n", k=2)
                    wv = stg[0][:, 1024:1536].rearrange("p (k n) -> p k n", k=2)
                    for c, ps in ((0, tp_ps), (1, g_ps)):
                        for h in range(2):
                            hs = slice(h * 512, (h + 1) * 512)
                            pe.matmul(ps[:, hs], wk[:, 0, c * P:(c + 1) * P], ctx[:, 0, hs], start=True, stop=False)
                            m = pe.matmul(ps[:, hs], wk[0:D - P, 1, c * P:(c + 1) * P], ctx[0:D - P, 1, hs], start=False, stop=True)
                    m.then_inc(kx_done, 1)
                    pe.wait_ge(kx_ready, 1)
                    for c, ps in ((0, tp_ps), (1, g_ps)):
                        for h in range(2):
                            hs = slice(h * 512, (h + 1) * 512)
                            for j in range(2):
                                pe.matmul(ps[:, hs], wq[:, j, c * P:(c + 1) * P], ctx_k[:, j, hs], start=(j == 0), stop=(j == 1))
                    for h in range(2):
                        hs = slice(h * 512, (h + 1) * 512)
                        for j in range(2):
                            m = pe.matmul(up_ps[0:1, hs], col("bq", j), ctx_k[:, j, hs], start=(j == 0), stop=(j == 1))
                    m.then_inc(kx_done, 1)
                    for q in range(B // 4):
                        pe.wait_ge(kx_ready, max(2, q + 1))
                        for b in range(4):
                            n = 4 * q + b
                            dst = (out_ps, up_ps)[q % 2][0:S, b * C:(b + 1) * C]
                            pe.matmul(dst, ctx[:, 0, n * S:(n + 1) * S], wv[:, 0, :], start=True, stop=False)
                            m = pe.matmul(dst, ctx[0:D - P, 1, n * S:(n + 1) * S], wv[0:D - P, 1, :], start=False, stop=True)
                        m.then_inc(kx_done, 1)
            stack.pop()

        with ExitStack() as scope:
            stack.append(scope)
            x_in = sb("x_in", [P, NT, C])
            x1 = sb("x1", [P, NT, C])
            x2 = sb("x2", [P, NT, C])
            xacc = sb("xacc", [P, NT, C])
            x3 = sb("x3", [P, NT, C])
            text = sb("text", [P, NT, C])
            xn = sb("xn", [P, NT, C])
            fm = sb("fm", [P, KC, T])
            act_p = (sb("act_hi", [P, KC, T], F32R), sb("act_lo", [P, KC, T], F32R))
            h_p = (sb("h_hi", [P, KC, T], F32R), sb("h_lo", [P, KC, T], F32R))
            t1 = sb("t1", [P, KC, T])
            t2 = sb("t2", [P, KC, T])
            probs = sb("probs", [P, NT // 2, 2, S])
            probs_t = sb("probs_t", [P, NT // 2, P])
            ms, vs, cs = sb("ms", [P, KC, S]), sb("vs", [P, C]), sb("cs", [1, S])
            hr_r = sb("hr_r", [P, 2, T])
            hr_sq = sb("hr_sq", [P, 2, T])
            hr_p = (sb("hr_hi", [P, 3, T], F32R), sb("hr_lo", [P, 3, T], F32R))
            stat = sb("stat", [P, NT, 6])
            mean, var, vtmp, rs, r2 = (sb(n, [P, NT]) for n in ("mean", "var", "vtmp", "rs", "r2"))
            stat3 = sb("stat3", [P, NT, 6])
            mean3, var3, vtmp3, rs3 = (sb(n, [P, NT]) for n in ("mean3", "var3", "vtmp3", "rs3"))
            smax, ssum = sb("smax", [P, NT]), sb("ssum", [P, NT])
            sig = sb("sig", [P, NT, 4])
            bid = sb("bid", [P, NT, 3])
            hot = sb("hot", [P, NT, 3])
            btmp = sb("btmp", [P, NT, 3])
            coef = sb("coef", [P, NT, 3])
            cap4 = sb("cap4", [P, NT, 3])

            x_loaded, small_loaded = sem("x_loaded"), sem("small_loaded")
            x3_stored, text_stored = sem("x3_stored"), sem("text_stored")
            ve_ready, rs_ready, ve3_ready, rs3_ready = (sem(n) for n in ("ve_ready", "rs_ready", "ve3_ready", "rs3_ready"))
            xn_ready, turned, turned_out = sem("xn_ready"), sem("turned"), sem("turned_out")
            scores_done, shifted, exp_done, probs_turned, probs_t_ready = (sem(n) for n in (
                "scores_done", "scores_shifted", "exp_done", "probs_turned", "probs_t_ready"))
            pv_done, x1_ready, x2_ready, xacc_ready = (sem(n) for n in ("pv_done", "x1_ready", "x2_ready", "xacc_ready"))
            hi_ready, lo_ready = sem("act_hi_ready"), sem("act_lo_ready")
            wr_done, w2s_done, wv_done, wo_done = (sem(n) for n in ("wr_done", "w2s_done", "wv_done", "wo_done"))
            t1_ready, t2_ready, g_ready = sem("t1_ready"), sem("t2_ready"), sem("gated_ready")
            h_hi_ready, h_ready = sem("h_hi_ready"), sem("h_ready")
            bids_done, bexp_done, coef_ready = sem("bids_done"), sem("bid_exp_done"), sem("coef_ready")
            up_done, relu_done, sq_done, hr_hi_done, hr_lo_done, evac_done = (sem(n) for n in (
                "up_done", "relu_done", "sq_done", "hr_hi_done", "hr_lo_done", "evac_done"))
            down_done = sem("down_done")
            v_front, v_tail, a_front = sem("dve_front"), sem("dve_tail"), sem("act_front")
            KF, KT = 52, 13

            NSLOT = NCHUNK + 2
            x_v = a["x"].rearrange("b (t p) c -> b p t c", p=P)
            x3_v = x3_dram.rearrange("b (t p) c -> b p t c", p=P)
            text_v = text_dram.rearrange("b (t p) c -> b p t c", p=P)

            def one(ap, n):
                return ap[bass.ds(n, 1)].rearrange("o p t c -> p (o t) c")

            def one2(ap, n):
                return ap[bass.ds(n, 1)].rearrange("o p c -> (o p) c")

            def pipeline(eng, iteration):
                iteration(None, 0)
                iteration(0, 1)
                with eng.Fori(1, B - 1) as i:
                    iteration(i, i + 1)
                iteration(B - 1, None)

            with nc.Block() as block:
                @block.sync
                def _(sp):
                    def load(n):
                        after(sp, x1_ready, n)
                        sp.dma_start(x_in[:, :, :], one(x_v, n)).then_inc(x_loaded, 16)
                        after(sp, pv_done, n)
                        sp.dma_start(ms[:, :, :].rearrange("p k s -> p (k s)"), one2(ms_dram, n)).then_inc(small_loaded, 16)
                        for h in range(2):
                            sp.dma_start(vs[h * S:(h + 1) * S, :], one2(vs_dram, n)).then_inc(small_loaded, 16)
                        sp.dma_start(cs[:, :], one2(cs_dram, n)).then_inc(small_loaded, 16)

                    def store(i):
                        sp.wait_ge(evac_done, 3 * i + 3)
                        sp.dma_start(one(x3_v, i), x3[:, :, :]).then_inc(x3_stored, 16)
                        sp.wait_ge(v_tail, KT * i + KT)
                        sp.dma_start(one(text_v, i), text[:, :, :]).then_inc(text_stored, 16)

                    load(0)
                    load(1)
                    load(2)
                    store(0)
                    with sp.Fori(1, B - 2) as i:
                        load(i + 2)
                        store(i)
                    store(B - 2)
                    store(B - 1)
                    sp.wait_ge(x3_stored, 16 * B)
                    sp.wait_ge(text_stored, 16 * B)

                @block.gpsimd
                def _(g):
                    def iteration(i, n):
                        if i is not None:
                            g.wait_ge(x2_ready, i + 1)
                            after(g, evac_done, 3 * i)
                            g.tensor_tensor(xacc[:, :, :], x1[:, :, :], x2[:, :, :], ALU.add).then_inc(xacc_ready, 1)
                        if n is not None:
                            for k in range(4):
                                g.wait_ge(ve_ready, 4 * n + k + 1)
                                g.tensor_tensor((rs, rs, r2, rs)[k][:, :], var[:, :], neg_half[:, :], ALU.pow).then_inc(rs_ready, 1)
                        if i is not None:
                            g.wait_ge(ve3_ready, i + 1)
                            g.tensor_tensor(rs3[:, :], var3[:, :], neg_half[:, :], ALU.pow).then_inc(rs3_ready, 1)
                    pipeline(g, iteration)

                @block.scalar
                def _(s_):
                    s = s_

                    def chunk(c, i):
                        up = up_ps[:, (c % 2) * T:(c % 2 + 1) * T]
                        hi = hr_p[0][:, c % 3, :]
                        if c < 2:
                            s.wait_ge(sq_done, NCHUNK * i + c + 1)
                            after(s, down_done, NCHUNK * i)
                            s.activation(hi, hr_sq[:, c % 2, :], ACT.Copy).then_inc(hr_hi_done, 1)
                            return
                        s.wait_ge(up_done, NCHUNK * i + c + 1)
                        s.activation(hr_r[:, c % 2, :], up, ACT.Relu).then_inc(relu_done, 1)
                        s.wait_ge(relu_done, (NCHUNK - 2) * i + c - 1)
                        after(s, down_done, NCHUNK * i + c - 2)
                        s.activation(hi, hr_r[:, c % 2, :], ACT.Square).then_inc(hr_hi_done, 1)

                    def front(k, n):
                        if k == 2:
                            s.wait_ge(turned, 3 * n + 1)
                            after(s, bids_done, n)
                            after(s, h_ready, n)
                            s.activation(fm[:, :, :].rearrange("p k t -> p (k t)"), tp_ps[:, :], ACT.Copy).then_inc(turned_out, 1)
                        if k == 4:
                            s.wait_ge(shifted, n + 1)
                            s.activation(probs[:, :, :, :], probs[:, :, :, :], ACT.Exp).then_inc(exp_done, 1)
                        if k == 5:
                            s.wait_ge(probs_turned, n + 1)
                            after(s, pv_done, n)
                            s.activation(probs_t[:, :, :].rearrange("p j t -> p (j t)"), tp_ps[:, 0:T // 2], ACT.Copy).then_inc(probs_t_ready, 1)
                        if k == 9:
                            s.wait_ge(turned, 3 * n + 2)
                            for c in range(KC):
                                s.activation(fm[:, c, :], tp_ps[:, c * T:(c + 1) * T], ACT.Identity,
                                             bias=col("ln1_b", c), scale=col("ln1_w", c)).then_inc(a_front, 1)
                            s.wait_ge(a_front, 2 * KC * n + KC)
                            after(s, wo_done, n)
                            s.activation(act_p[0][:, :, :], fm[:, :, :], ACT.Copy).then_inc(hi_ready, 1)
                        if k == 11:
                            s.wait_ge(wr_done, n + 1)
                            s.activation(t1[:, :, :].rearrange("p k t -> p (k t)"), g_ps[:, :], ACT.Tanh, scale=0.5).then_inc(t1_ready, 1)
                            s.wait_ge(w2s_done, n + 1)
                            if not isinstance(n, int) or n > 0:
                                s.wait_ge(sq_done, NCHUNK * n - NCHUNK + 2)
                            s.activation(t2[:, :, :].rearrange("p k t -> p (k t)"), tp_ps[:, :], ACT.Tanh, scale=0.5).then_inc(t2_ready, 1)
                        if k == 12:
                            s.wait_ge(g_ready, n + 1)
                            s.activation(act_p[0][:, :, :], fm[:, :, :], ACT.Copy).then_inc(hi_ready, 1)
                        if k == 16:
                            s.wait_ge(turned, 3 * n + 3)
                            s.wait_ge(lo_ready, 2 * n + 2)
                            for c in range(KC):
                                s.activation(fm[:, c, :], tp_ps[:, c * T:(c + 1) * T], ACT.Identity,
                                             bias=col("ln2_b", c), scale=col("ln2_w", c)).then_inc(a_front, 1)
                        if k == 18:
                            s.wait_ge(a_front, 2 * KC * n + 2 * KC)
                            after(s, up_done, NCHUNK * n)
                            s.activation(h_p[0][:, :, :], fm[:, :, :], ACT.Copy).then_inc(h_hi_ready, 1)
                            s.wait_ge(bids_done, n + 1)
                            s.activation(sig[:, :, :], g_ps[:, 0:8 * NT].rearrange("p (t e) -> p t e", e=8)[:, :, 0:4],
                                         ACT.Exp, scale=-1.0).then_inc(bexp_done, 1)

                    def iteration(i, n):
                        for k in range(NSLOT):
                            if i is not None and k < NCHUNK:
                                chunk(k, i)
                            if n is not None:
                                front(k, n)
                    pipeline(s, iteration)

                @block.tensor
                def _(pe):
                    def up(c, i):
                        dst = up_ps[:, (c % 2) * T:(c % 2 + 1) * T]
                        if c == 0:
                            pe.wait_ge(h_ready, i + 1)
                        after(pe, sq_done, NCHUNK * i + max(c - 1, 0))
                        for k in range(KC):
                            if c < 2:
                                st = pair(w["W1"], slice(None), k, slice(c * P, (c + 1) * P))
                            else:
                                e, cc = divmod(c - 2, HC)
                                st = pair(kexp, slice(None), e * KC + k, slice(cc * P, (cc + 1) * P))
                            last = mm3(pe, dst, st, pair(h_p, slice(None), k, slice(None)), k == 0, k == KC - 1)
                        last.then_inc(up_done, 1)

                    def down(c, i):
                        first = c in (0, 2, 2 + HC)
                        pe.wait_ge(hr_lo_done, NCHUNK * i + c + 1)
                        if first:
                            after(pe, evac_done, 3 * i + (0, 2, 2 + HC).index(c))
                        for t in range(NT):
                            st = pair(hr_p, slice(None), c % 3, slice(t * P, (t + 1) * P))
                            mv = pair(w["W3"], slice(None), c, slice(None)) if c < 2 else pair(vexp, slice(None), c - 2, slice(None))
                            last = mm3(pe, out_ps[:, t * C:(t + 1) * C], st, mv, first and t % 2 == 0, c in GROUP_END)
                        last.then_inc(down_done, 1)

                    def turn():
                        for c in range(KC):
                            for t in range(NT):
                                last = pe.transpose(tp_ps[:, c * T + t * P:c * T + (t + 1) * P], xn[:, t, c * P:(c + 1) * P], ident[:, :])
                        last.then_inc(turned, 1)

                    def project(dst, name, done):
                        for c in range(KC):
                            for k in range(KC):
                                last = mm3(pe, dst[:, c * T:(c + 1) * T], pair(w[name], slice(None), k, slice(c * P, (c + 1) * P)),
                                           pair(act_p, slice(None), k, slice(None)), k == 0, k == KC - 1)
                        last.then_inc(done, 1)

                    def front(k, n):
                        if k == 2:
                            pe.wait_ge(xn_ready, 3 * n + 1)
                            after(pe, a_front, 2 * KC * n)
                            turn()
                        if k == 3:
                            pe.wait_ge(turned_out, n + 1)
                            pe.wait_ge(small_loaded, 64 * n + 64)
                            after(pe, coef_ready, n)
                            for t in range(NT):
                                dst = g_ps[:, t * S:(t + 1) * S]
                                for c in range(KC):
                                    pe.matmul(dst, fm[:, c, t * P:(t + 1) * P], ms[:, c, :], start=(c == 0), stop=False)
                                last = pe.matmul(dst, ones[:, :], cs[:, :], start=False, stop=True)
                            last.then_inc(scores_done, 1)
                        if k == 5:
                            pe.wait_ge(exp_done, n + 1)
                            for j in range(NT // 2):
                                last = pe.transpose(tp_ps[:, j * P:(j + 1) * P], probs[:, j, :, :].rearrange("p h s -> p (h s)"), ident[:, :])
                            last.then_inc(probs_turned, 1)
                        if k == 6:
                            pe.wait_ge(probs_t_ready, n + 1)
                            for j in range(NT // 2):
                                for h in range(2):
                                    t, half = 2 * h + j, slice(h * S, (h + 1) * S)
                                    last = pe.matmul(g_ps[:, t * C:(t + 1) * C], probs_t[half, j, :], vs[half, :], start=True, stop=True)
                            last.then_inc(pv_done, 1)
                        if k == 9:
                            pe.wait_ge(xn_ready, 3 * n + 2)
                            turn()
                        if k == 11:
                            pe.wait_ge(lo_ready, 2 * n + 1)
                            project(g_ps, "Wr", wr_done)
                            project(tp_ps, "W2s", w2s_done)
                        if k == 12:
                            pe.wait_ge(t1_ready, n + 1)
                            project(g_ps, "Wv", wv_done)
                        if k == 13:
                            pe.wait_ge(lo_ready, 2 * n + 2)
                            pe.wait_ge(t2_ready, n + 1)
                            for t in range(NT):
                                for c in range(KC):
                                    last = mm3(pe, tp_ps[:, t * C:(t + 1) * C], pair(act_p, slice(None), c, slice(t * P, (t + 1) * P)),
                                               pair(w["Wo"], slice(None), c, slice(None)), c == 0, c == KC - 1)
                            last.then_inc(wo_done, 1)
                        if k == 16:
                            pe.wait_ge(xn_ready, 3 * n + 3)
                            turn()
                        if k == 18:
                            pe.wait_ge(a_front, 2 * KC * n + 2 * KC)
                            for t in range(NT):
                                for c in range(KC):
                                    last = pe.matmul(g_ps[:, 8 * t:8 * t + 7], fm[:, c, t * P:(t + 1) * P], wb[:, c, :],
                                                     start=(c == 0), stop=(c == KC - 1))
                            last.then_inc(bids_done, 1)

                    def iteration(i, n):
                        for k in range(NSLOT):
                            if i is not None and k < NCHUNK:
                                up(k, i)
                            if n is not None:
                                front(k, n)
                            if i is not None and k >= 2:
                                down(k - 2, i)
                    pipeline(pe, iteration)

                @block.vector
                def _(v):
                    for t in range(NT):
                        v.tensor_copy(cap4[:, t, :], cap)
                    v.memset(tmax[:, :], 0.0)

                    def chunk(c, i):
                        up = up_ps[:, (c % 2) * T:(c % 2 + 1) * T]
                        sq = hr_sq[:, c % 2, :]
                        if c < 2:
                            v.wait_ge(up_done, NCHUNK * i + c + 1)
                            v.wait_ge(t2_ready, i + 1)
                            v.scalar_tensor_tensor(out=sq, in0=t2[:, c, :], scalar=1.0, in1=up, op0=ALU.add, op1=ALU.mult).then_inc(sq_done, 1)
                        else:
                            v.wait_ge(relu_done, (NCHUNK - 2) * i + c - 1)
                            v.tensor_tensor(sq, hr_r[:, c % 2, :], hr_r[:, c % 2, :], ALU.mult).then_inc(sq_done, 1)
                        v.wait_ge(hr_hi_done, NCHUNK * i + c + 1)
                        v.wait_ge(sq_done, NCHUNK * i + c + 1)
                        v.tensor_tensor(hr_p[1][:, c % 3, :], sq, hr_p[0][:, c % 3, :].bitcast(F32), ALU.subtract).then_inc(hr_lo_done, 1)

                    def evacuate(c, i):
                        order = GROUP_END[c]
                        e = GROUP_EXPERT[order]
                        v.wait_ge(down_done, NCHUNK * i + c + 1)
                        v.wait_ge(xacc_ready, i + 1)
                        if order == 0:
                            v.wait_ge(coef_ready, i + 1)
                        else:
                            v.wait_ge(evac_done, 3 * i + order)
                        if order == 2:
                            after(v, x3_stored, 16 * i)
                        dst = x3 if order == 2 else xacc
                        for t in range(NT):
                            last = v.scalar_tensor_tensor(out=dst[:, t, :], in0=out_ps[:, t * C:(t + 1) * C], scalar=coef[:, t, e:e + 1],
                                                          in1=xacc[:, t, :], op0=ALU.mult, op1=ALU.add)
                        last.then_inc(evac_done, 1)

                    def front(k, n, st):
                        if k == 0:
                            v.wait_ge(x_loaded, 16 * n + 16)
                            stats(st, x_in, stat, mean, var, vtmp, ve_ready)
                        if k == 1:
                            v.wait_ge(rs_ready, 4 * n + 1)
                            after(v, turned, 3 * n)
                            for t in range(NT):
                                last = v.tensor_scalar(xn[:, t, :], x_in[:, t, :], mean[:, t:t + 1], rs[:, t:t + 1], ALU.subtract, ALU.mult)
                            last.then_inc(xn_ready, 1)
                        if k == 3:
                            v.wait_ge(scores_done, n + 1)
                            sc = g_ps[:, 0:NT * S].rearrange("p (t s) -> p t s", s=S)
                            sc4 = g_ps[:, 0:NT * S].rearrange("p (h j s) -> p h j s", h=2, s=S)
                            mx4 = smax[:, :].rearrange("p (h j) -> p h j", h=2).unsqueeze(3).broadcast_to([P, 2, NT // 2, S])
                            st.link(v.tensor_reduce(smax[:, :], sc, X, ALU.max))
                            after(v, probs_turned, n)
                            v.tensor_tensor(probs[:, :, :, :].rearrange("p j h s -> p h j s"), sc4, mx4, ALU.subtract).then_inc(shifted, 1)
                        if k == 4:
                            v.wait_ge(exp_done, n + 1)
                            st.link(v.tensor_reduce(ssum[:, :].rearrange("p (h j) -> p h j", h=2), probs[:, :, :, :].rearrange("p j h s -> p h j s"), X, ALU.add))
                            st.link(v.reciprocal(ssum[:, :], ssum[:, :]))
                        if k == 6:
                            v.wait_ge(pv_done, n + 1)
                            after(v, xacc_ready, n)
                            for t in range(NT):
                                last = v.scalar_tensor_tensor(out=x1[:, t, :], in0=g_ps[:, t * C:(t + 1) * C], scalar=ssum[:, t:t + 1],
                                                              in1=x_in[:, t, :], op0=ALU.mult, op1=ALU.add)
                            last.then_inc(x1_ready, 1)
                            v.wait_ge(x1_ready, n + 1)
                            stats(st, x1, stat, mean, var, vtmp, ve_ready)
                        if k == 7:
                            v.wait_ge(rs_ready, 4 * n + 2)
                            st.add(v.tensor_scalar(vtmp[:, :], var[:, :], EPS, None, ALU.subtract))
                            st.link(v.tensor_tensor(r2[:, :], rs[:, :], rs[:, :], ALU.mult))
                            st.link(v.tensor_tensor(var[:, :], vtmp[:, :], r2[:, :], ALU.mult))
                            v.tensor_scalar(var[:, :], var[:, :], EPS, None, ALU.add).then_inc(ve_ready, 1)
                        if k == 8:
                            v.wait_ge(rs_ready, 4 * n + 3)
                            st.link(v.tensor_tensor(r2[:, :], rs[:, :], r2[:, :], ALU.mult))
                            for t in range(NT):
                                last = v.tensor_scalar(xn[:, t, :], x1[:, t, :], mean[:, t:t + 1], r2[:, t:t + 1], ALU.subtract, ALU.mult)
                            last.then_inc(xn_ready, 1)
                            for t in range(NT):
                                last = v.tensor_scalar(x2[:, t, :], x1[:, t, :], mean[:, t:t + 1], rs[:, t:t + 1], ALU.subtract, ALU.mult)
                            st.add(last)
                        if k == 10:
                            v.wait_ge(hi_ready, 2 * n + 1)
                            v.tensor_tensor(act_p[1][:, :, :], fm[:, :, :], act_p[0][:, :, :].bitcast(F32), ALU.subtract).then_inc(lo_ready, 1)
                        if k == 12:
                            v.wait_ge(wv_done, n + 1)
                            v.scalar_tensor_tensor(out=fm[:, :, :].rearrange("p k t -> p (k t)"), in0=t1[:, :, :].rearrange("p k t -> p (k t)"),
                                                   scalar=1.0, in1=g_ps[:, :], op0=ALU.add, op1=ALU.mult).then_inc(g_ready, 1)
                            v.wait_ge(hi_ready, 2 * n + 2)
                            v.tensor_tensor(act_p[1][:, :, :], fm[:, :, :], act_p[0][:, :, :].bitcast(F32), ALU.subtract).then_inc(lo_ready, 1)
                        if k == 13:
                            v.wait_ge(wo_done, n + 1)
                            st.wait()
                            f2 = x2[:, :, :].rearrange("p t c -> p (t c)")
                            v.tensor_tensor(f2, f2, tp_ps[:, :], ALU.add).then_inc(x2_ready, 1)
                            v.wait_ge(x2_ready, n + 1)
                            stats(st, x2, stat, mean, var, vtmp, ve_ready)
                        if k == 15:
                            v.wait_ge(rs_ready, 4 * n + 4)
                            for t in range(NT):
                                last = v.tensor_scalar(xn[:, t, :], x2[:, t, :], mean[:, t:t + 1], rs[:, t:t + 1], ALU.subtract, ALU.mult)
                            last.then_inc(xn_ready, 1)
                        if k == 18:
                            v.wait_ge(h_hi_ready, n + 1)
                            v.tensor_tensor(h_p[1][:, :, :], fm[:, :, :], h_p[0][:, :, :].bitcast(F32), ALU.subtract).then_inc(h_ready, 1)

                    def bids(n, st):
                        v.wait_ge(bexp_done, n + 1)
                        conf = sig[:, :, 0:3]
                        ee = lambda m, q: m[:, :, q:q + 1]
                        st.link(v.tensor_scalar(sig[:, :, :], sig[:, :, :], 1.0, None, ALU.add))
                        st.link(v.reciprocal(sig[:, :, :], sig[:, :, :]))
                        st.add(v.tensor_tensor(bid[:, :, :], conf, cap4[:, :, :], ALU.mult))
                        st.link(v.tensor_scalar(btmp[:, :, :], conf, 1e-6, None, ALU.add))
                        st.link(v.tensor_tensor(bid[:, :, :], bid[:, :, :], ee(sig, 3).broadcast_to([P, NT, 3]), ALU.mult))
                        aff = g_ps[:, 0:8 * NT].rearrange("p (t e) -> p t e", e=8)[:, :, 4:7]
                        st.add(v.tensor_tensor(bid[:, :, :], bid[:, :, :], aff, ALU.add))
                        st.link(v.reciprocal(btmp[:, :, :], btmp[:, :, :]))
                        st.add(v.tensor_tensor(btmp[:, :, :], btmp[:, :, :], conf, ALU.mult))
                        st.add(v.tensor_tensor(ee(hot, 0), ee(bid, 1), ee(bid, 2), ALU.max))
                        st.link(v.tensor_tensor(ee(hot, 2), ee(bid, 0), ee(bid, 1), ALU.max))
                        st.add(v.tensor_tensor(ee(hot, 0), ee(bid, 0), ee(hot, 0), ALU.is_ge))
                        st.link(v.tensor_tensor(ee(hot, 2), ee(bid, 2), ee(hot, 2), ALU.is_gt))
                        st.link(v.tensor_tensor(ee(hot, 1), ee(hot, 0), ee(hot, 2), ALU.add))
                        st.link(v.tensor_scalar(ee(hot, 1), ee(hot, 1), -1.0, 1.0, ALU.mult, ALU.add))
                        v.tensor_tensor(coef[:, :, :], btmp[:, :, :], hot[:, :, :], ALU.mult).then_inc(coef_ready, 1)

                    def iteration(i, n):
                        st = Steps(v, v_front, 0 if n is None else KF * n)
                        tail = Steps(v, v_tail, 0 if i is None else KT * i)
                        for k in range(NSLOT):
                            if i is not None and k < NCHUNK:
                                chunk(k, i)
                            if n is not None:
                                front(k, n, st)
                            if i is not None and k >= 2 and k - 2 in GROUP_END:
                                evacuate(k - 2, i)
                        if i is not None:
                            v.wait_ge(evac_done, 3 * i + 3)
                            stats(tail, x3, stat3, mean3, var3, vtmp3, ve3_ready)
                        if n is not None:
                            bids(n, st)
                            assert st.n == KF, st.n
                        if i is not None:
                            v.wait_ge(rs3_ready, i + 1)
                            after(v, text_stored, 16 * i)
                            for t in range(NT):
                                last = v.tensor_scalar(text[:, t, :], x3[:, t, :], mean3[:, t:t + 1], rs3[:, t:t + 1], ALU.subtract, ALU.mult)
                            tail.link(last)
                            tail.link(v.tensor_reduce(tcur[:, :], text[:, :, :], XY, ALU.max, apply_absolute_value=True))
                            tail.add(v.tensor_tensor(tmax[:, :], tmax[:, :], tcur[:, :], ALU.max))
                            assert tail.n == KT, tail.n
                    pipeline(v, iteration)
            stack.pop()

        kv_scope.close()
        stack.pop()

        def scale_step(name, which, products, extra=None):
            s_max, s_done = sem(name + "_max"), sem(name + "_scale")
            with nc.Block() as block:
                @block.gpsimd
                def _(g):
                    g.partition_all_reduce(gmax[:, which:which + 1], tmax[:, :], P, RED.max).then_inc(s_max, 1)

                @block.vector
                def _(v):
                    st = Steps(v, s_done)
                    v.wait_ge(s_max, 1)
                    st.link(v.tensor_scalar(iscale[:, which:which + 1], gmax[:, which:which + 1], 1e-8, 1.0 / 127.0, ALU.max, ALU.mult))
                    st.add(v.reciprocal(inv[:, which:which + 1], iscale[:, which:which + 1]))
                    for o, wk, ak in products:
                        st.add(v.tensor_tensor(oscale[:, o:o + 1], wscale[:, wk:wk + 1], iscale[:, ak:ak + 1], ALU.mult))
                    st.wait()
                    if extra is not None:
                        extra(v, st)
                    v.memset(tmax[:, :], 0.0)

        def first_then_loop(eng, body, n):
            body(0)
            with eng.Fori(1, n) as j:
                body(j)

        ff_scope = ExitStack()
        stack.append(ff_scope)
        ff = sb("ff", [P, B, KC, T])
        O_TXT, O_A0, O_A1, O_F1, O_F2 = 2, 3, 4, 5, 6

        scale_step("text", A_TXT, [(O_TXT, W_TXT, A_TXT), (O_A0, W_A0, A_IMG), (O_A1, W_A1, A_IMG)])
        with ExitStack() as scope:
            stack.append(scope)
            kf = sb("kf", [P, 2, NCTX])
            kt = sb("kt", [P, 2, B // 2, P])
            key_lin, key_ready, key_turned, key_t_ready, key_stored = (sem(n) for n in (
                "key_lin", "key_ready", "key_turned", "key_t_ready", "key_stored"))
            with nc.Block() as block:
                @block.tensor
                def _(pe):
                    for a_ in range(2):
                        for h in range(2):
                            for k in range(KC):
                                last = pe.matmul(psum[a_][:, h * 512:(h + 1) * 512], watt[:, k, a_, :],
                                                 q_img[:, k, h * 512:(h + 1) * 512], start=(k == 0), stop=(k == KC - 1))
                        last.then_inc(key_lin, 1)
                    for a_ in range(2):
                        pe.wait_ge(key_ready, a_ + 1)
                        for j in range(B // 2):
                            last = pe.transpose(psum[2 + a_][:, j * P:(j + 1) * P], kf[:, a_, j * P:(j + 1) * P], ident[:, :])
                        last.then_inc(key_turned, 1)

                @block.scalar
                def _(s):
                    for a_ in range(2):
                        s.wait_ge(key_lin, a_ + 1)
                        s.activation(kf[:, a_, :], psum[a_][:, :], ACT.Identity, bias=col("b_att%d" % a_),
                                     scale=oscale[:, O_A0 + a_:O_A0 + a_ + 1]).then_inc(key_ready, 1)
                    for a_ in range(2):
                        s.wait_ge(key_turned, a_ + 1)
                        s.activation(kt[:, a_, :, :].rearrange("p j f -> p (j f)"), psum[2 + a_][:, :], ACT.Copy).then_inc(key_t_ready, 1)

                @block.sync
                def _(sp):
                    sp.wait_ge(key_ready, 2)
                    for a_ in range(2):
                        sp.dma_start(kv_dram.rearrange("b p (a s) -> a p b s", a=2)[a_],
                                     kf[:, a_, :].rearrange("p (b s) -> p b s", s=S)).then_inc(key_stored, 16)
                    sp.wait_ge(key_t_ready, 2)
                    for a_ in range(2):
                        for h in range(2):
                            sp.dma_start(kvt_dram.rearrange("(j h) s (a f) -> a h s j f", h=2, a=2)[a_, h],
                                         kt[h * S:(h + 1) * S, a_, :, :]).then_inc(key_stored, 16)
                    sp.wait_ge(key_stored, 96)
            stack.pop()

        L = 4
        with ExitStack() as scope:
            stack.append(scope)
            tx = [sb(f"tx{l}", [P, NT, C]) for l in range(L)]
            qt = [sb(f"qt{l}", [P, NT, C], BF16) for l in range(L)]
            qc = [sb(f"qc{l}", [P, KC, T], BF16) for l in range(L)]
            f = [sb(f"f{l}", [P, KC, T]) for l in range(L)]
            fs = [sb(f"fs{l}", [P, T]) for l in range(L)]
            pr = [sb(f"pr{l}", [P, NT // 2, 2, S]) for l in range(L)]
            prt = [sb(f"prt{l}", [P, NT // 2, P]) for l in range(L)]
            kv = [sb(f"kv{l}", [P, 2, S]) for l in range(L)]
            kvt = [sb(f"kvt{l}", [P, 2, P]) for l in range(L)]
            mx = [sb(f"mx{l}", [P, NT]) for l in range(L)]
            sm = [sb(f"sm{l}", [P, NT]) for l in range(L)]
            cur = [sb(f"cur{l}", [P, 1]) for l in range(L)]
            tx_loaded, kv_loaded, f_stored = ([sem(f"att_{n}{l}") for l in range(L)] for n in ("tx_loaded", "kv_loaded", "f_stored"))
            (quant_done, q_turned, qc_ready, txt_done, f_ready, fs_ready, sc_done, sc_shifted,
             e_done, norm_done, e_turned, prt_ready, o_done, f_updated, v_att) = (sem("att_" + n) for n in (
                 "quant_done", "q_turned", "qc_ready", "txt_done", "f_ready", "fs_ready",
                 "scores_done", "shifted", "exp_done", "norm_done", "probs_turned", "probs_t_ready", "o_done",
                 "f_updated", "dve"))
            t_v = text_dram.rearrange("b (t p) c -> b p t c", p=P)
            NJ = B // L
            KV_ = 36

            def bank4(l):
                return psum[l][:, :].rearrange("p (h n) -> p h n", h=2)[:, :, 0:2 * P]

            def tok4(ap):
                return ap.rearrange("p (h n) -> p h n", h=2)

            with nc.Block() as block:
                @block.sync
                def _(sp):
                    def load(j):
                        for l in range(L):
                            n = L * j + l
                            after(sp, quant_done, n + 1 - L)
                            sp.dma_start(tx[l][:, :, :], one(t_v, n)).then_inc(tx_loaded[l], 16)
                        for l in range(L):
                            n = L * j + l
                            after(sp, o_done, 2 * L * j - L + l + 1)
                            sp.dma_start(kv[l][:, :, :].rearrange("p a s -> p (a s)"), one2(kv_dram, n)).then_inc(kv_loaded[l], 16)
                            for h in range(2):
                                sp.dma_start(kvt[l][h * S:(h + 1) * S, :, :].rearrange("p a f -> p (a f)"), one2(kvt_dram, n)).then_inc(kv_loaded[l], 16)

                    def store(j):
                        for l in range(L):
                            n = L * j + l
                            sp.wait_ge(f_updated, 2 * L * j + L + l + 1)
                            sp.dma_start(ff[:, bass.ds(n, 1), :, :].rearrange("p o k t -> p (o k t)"),
                                         f[l][:, :, :].rearrange("p k t -> p (k t)")).then_inc(f_stored[l], 16)
                    load(0)
                    load(1)
                    store(0)
                    with sp.Fori(1, NJ - 1) as j:
                        load(j + 1)
                        store(j)
                    store(NJ - 1)
                    for l in range(L):
                        sp.wait_ge(f_stored[l], 16 * NJ)

                @block.gpsimd
                def _(g):
                    def body(j):
                        for a_ in range(2):
                            for l in range(L):
                                if a_ == 0:
                                    g.wait_ge(f_ready, L * j + l + 1)
                                    after(g, sc_done, 2 * L * j - L + l + 1)
                                else:
                                    g.wait_ge(f_updated, 2 * L * j + l + 1)
                                g.tensor_tensor(fs[l][:, :], f[l][:, 0, :], f[l][:, 1, :], ALU.add).then_inc(fs_ready, 1)
                    first_then_loop(g, body, NJ)

                @block.scalar
                def _(s):
                    def body(j):
                        for l in range(L):
                            n = L * j + l
                            s.wait_ge(q_turned, n + 1)
                            after(s, txt_done, n + 1 - L)
                            s.activation(qc[l][:, :, :].rearrange("p k t -> p (k t)"), psum[l][:, 0:T].bitcast(BF16), ACT.Copy).then_inc(qc_ready, 1)
                        for l in range(L):
                            n = L * j + l
                            s.wait_ge(txt_done, n + 1)
                            after(s, f_stored[l], 16 * j)
                            for c in range(KC):
                                last = s.activation(f[l][:, c, :], psum[l][:, c * T:(c + 1) * T], ACT.Identity, bias=col("b_txt", c),
                                                    scale=oscale[:, O_TXT:O_TXT + 1])
                            last.then_inc(f_ready, 1)
                        for a_ in range(2):
                            for l in range(L):
                                s.wait_ge(sc_shifted, 2 * L * j + L * a_ + l + 1)
                                s.activation(pr[l][:, :, :, :], pr[l][:, :, :, :], ACT.Exp, scale=INV_SQRT).then_inc(e_done, 1)
                            for l in range(L):
                                u = 2 * L * j + L * a_ + l
                                s.wait_ge(e_turned, u + 1)
                                after(s, o_done, u + 1 - L)
                                s.activation(prt[l][:, :, :].rearrange("p j t -> p (j t)"), psum[l][:, 0:2 * P], ACT.Copy).then_inc(prt_ready, 1)
                    first_then_loop(s, body, NJ)

                @block.tensor
                def _(pe):
                    def body(j):
                        for l in range(L):
                            n = L * j + l
                            pe.wait_ge(quant_done, n + 1)
                            after(pe, f_updated, 2 * L * j - L + l + 1)
                            qp = psum[l][:, 0:T].bitcast(BF16)
                            for c in range(KC):
                                for t in range(NT):
                                    last = pe.transpose(qp[:, c * T + t * P:c * T + (t + 1) * P], qt[l][:, t, c * P:(c + 1) * P], ident_b[:, :])
                            last.then_inc(q_turned, 1)
                        for l in range(L):
                            pe.wait_ge(qc_ready, L * j + l + 1)
                            for c in range(KC):
                                for k in range(KC):
                                    last = pe.matmul(psum[l][:, c * T:(c + 1) * T], wtxt[:, k, c * P:(c + 1) * P], qc[l][:, k, :],
                                                     start=(k == 0), stop=(k == KC - 1))
                            last.then_inc(txt_done, 1)
                        for a_ in range(2):
                            for l in range(L):
                                n, u = L * j + l, 2 * L * j + L * a_ + l
                                if a_ == 0:
                                    pe.wait_ge(kv_loaded[l], 48 * j + 48)
                                pe.wait_ge(fs_ready, u + 1)
                                for t in range(NT):
                                    last = pe.matmul(psum[l][:, t * S:(t + 1) * S], fs[l][:, t * P:(t + 1) * P], kv[l][:, a_, :], start=True, stop=True)
                                last.then_inc(sc_done, 1)
                            for l in range(L):
                                u = 2 * L * j + L * a_ + l
                                pe.wait_ge(norm_done, u + 1)
                                for q in range(NT // 2):
                                    last = pe.transpose(psum[l][:, q * P:(q + 1) * P], pr[l][:, q, :, :].rearrange("p h s -> p (h s)"), ident[:, :])
                                last.then_inc(e_turned, 1)
                            for l in range(L):
                                u = 2 * L * j + L * a_ + l
                                pe.wait_ge(prt_ready, u + 1)
                                for q in range(NT // 2):
                                    for h in range(2):
                                        half = slice(h * S, (h + 1) * S)
                                        last = pe.matmul(psum[l][:, h * T + q * P:h * T + (q + 1) * P], kvt[l][half, a_, :],
                                                         prt[l][half, q, :], start=True, stop=True)
                                last.then_inc(o_done, 1)
                    first_then_loop(pe, body, NJ)

                @block.vector
                def _(v):
                    def body(j):
                        st = Steps(v, v_att, KV_ * j)
                        for l in range(L):
                            v.wait_ge(tx_loaded[l], 16 * j + 16)
                            st.add(v.tensor_scalar(tx[l][:, :, :], tx[l][:, :, :], inv[:, A_TXT:A_TXT + 1], ROUND, ALU.mult, ALU.add))
                        for l in range(L):
                            n = L * j + l
                            v.wait_ge(v_att, KV_ * j + l + 1)
                            after(v, q_turned, n + 1 - L)
                            v.tensor_scalar(qt[l][:, :, :], tx[l][:, :, :], ROUND, None, ALU.subtract).then_inc(quant_done, 1)
                        for a_ in range(2):
                            for l in range(L):
                                v.wait_ge(sc_done, 2 * L * j + L * a_ + l + 1)
                                st.add(v.tensor_reduce(mx[l][:, :], psum[l][:, 0:NT * S].rearrange("p (t s) -> p t s", s=S), X, ALU.max))
                            st.wait()
                            for l in range(L):
                                after(v, e_turned, 2 * L * j + L * a_ + l + 1 - L)
                                v.tensor_tensor(pr[l][:, :, :, :].rearrange("p j h s -> p h j s"),
                                                psum[l][:, 0:NT * S].rearrange("p (h j s) -> p h j s", h=2, s=S),
                                                mx[l][:, :].rearrange("p (h j) -> p h j", h=2).unsqueeze(3).broadcast_to([P, 2, NT // 2, S]),
                                                ALU.subtract).then_inc(sc_shifted, 1)
                            for l in range(L):
                                v.wait_ge(e_done, 2 * L * j + L * a_ + l + 1)
                                st.add(v.tensor_reduce(sm[l][:, :].rearrange("p (j h) -> p j h", h=2), pr[l][:, :, :, :], X, ALU.add))
                            st.wait()
                            for l in range(L):
                                st.add(v.reciprocal(sm[l][:, :], sm[l][:, :]))
                            st.wait()
                            for l in range(L):
                                v.tensor_tensor(pr[l][:, :, :, :], pr[l][:, :, :, :],
                                                sm[l][:, :].rearrange("p (j h) -> p j h", h=2).unsqueeze(3).broadcast_to([P, NT // 2, 2, S]),
                                                ALU.mult).then_inc(norm_done, 1)
                            for l in range(L):
                                v.wait_ge(o_done, 2 * L * j + L * a_ + l + 1)
                                for c in range(KC):
                                    last = v.scalar_tensor_tensor(out=tok4(f[l][:, c, :]), in0=bank4(l), scalar=0.1, in1=tok4(f[l][:, c, :]),
                                                                  op0=ALU.mult, op1=ALU.add)
                                last.then_inc(f_updated, 1)
                        for l in range(L):
                            v.wait_ge(f_updated, 2 * L * j + L + l + 1)
                            st.add(v.tensor_reduce(cur[l][:, :], f[l][:, :, :], XY, ALU.max, apply_absolute_value=True))
                        st.wait()
                        for l in range(L):
                            st.link(v.tensor_tensor(tmax[:, :], tmax[:, :], cur[l][:, :], ALU.max))
                        assert st.n == KV_, st.n
                    first_then_loop(v, body, NJ)
            stack.pop()

        qf = sb("qf", [P, B, KC, T], BF16)
        lw = {n: (sb(n + "_hi", [P, KC, C], F32R), sb(n + "_lo", [P, KC, C], F32R)) for n in ("rT", "kT", "vT")}
        qavg = sb("qavg", [P, KC, B], BF16)
        acc_avg = sb("acc_avg", [P, HC, B])
        hmax8, hcur = sb("hmax8", [P, HC]), sb("hcur", [P, HC])
        avg_max, avg_join = sem("avg_max"), sem("avg_join")
        with nc.Block() as block:
            @block.vector
            def _(v):
                v.tensor_reduce(tcur[:, :], avg[:, :, :], XY, ALU.max, apply_absolute_value=True).then_inc(avg_max, 1)
                v.wait_ge(avg_max, 1)
                v.tensor_tensor(tmax[:, :], tmax[:, :], tcur[:, :], ALU.max).then_inc(avg_join, 1)
        scale_step("concat", A_CAT, [(O_F1, W_F1, A_CAT)])
        qy = sb("qy", [P, KC * T])
        with ExitStack() as scope:
            stack.append(scope)
            lstg = sb("lstg", [P, 3, KC, C])
            l_loaded, qavg_ready, acc_done, acc_ready, v_hid = (sem(n) for n in ("l1_loaded", "qavg_ready", "acc_avg_done", "acc_avg_ready", "dve_hidden"))
            hq_done, h_done, h_red = sem("hid_quant"), sem("hid_f1"), sem("hid_reduced")
            KH = 3
            with nc.Block() as block:
                @block.sync
                def _(sp):
                    for k, name in enumerate(("rT", "kT", "vT")):
                        sp.dma_start(lstg[:, k, :, :], a[name].rearrange("(k p) n -> p k n", p=P)).then_inc(l_loaded, 16)

                @block.tensor
                def _(pe):
                    pe.wait_ge(qavg_ready, 1)
                    for c in range(HC):
                        for k in range(KC):
                            last = pe.matmul(psum[3][:, c * B:(c + 1) * B], wf1[:, KC + k, c * P:(c + 1) * P], qavg[:, k, :],
                                             start=(k == 0), stop=(k == KC - 1))
                    last.then_inc(acc_done, 1)
                    pe.wait_ge(acc_ready, 1)

                    def body(n):
                        for q in range(HC // 2):
                            if q == 0:
                                pe.wait_ge(hq_done, n + 1)
                            after(pe, h_red, 4 * n + q - 3)
                            for c in (2 * q, 2 * q + 1):
                                for k in range(KC):
                                    last = pe.matmul(psum[q][:, (c % 2) * T:(c % 2 + 1) * T], wf1[:, k, c * P:(c + 1) * P],
                                                     qf[:, bass.ds(n, 1), k, :].rearrange("p o t -> p (o t)"), start=(k == 0), stop=(k == KC - 1))
                            last.then_inc(h_done, 1)
                    first_then_loop(pe, body, B)

                @block.vector
                def _(v):
                    st = Steps(v, v_hid)
                    st.link(v.tensor_scalar(lstg_avg := qy[:, 0:KC * B].rearrange("p (k b) -> p k b", k=KC), avg[:, :, :], inv[:, A_CAT:A_CAT + 1], ROUND, ALU.mult, ALU.add))
                    v.tensor_scalar(qavg[:, :, :], lstg_avg, ROUND, None, ALU.subtract).then_inc(qavg_ready, 1)
                    st.add(v.memset(hmax8[:, :], -1e30))
                    v.wait_ge(l_loaded, 48)
                    for k, name in enumerate(("rT", "kT", "vT")):
                        hi, lo = lw[name]
                        if name == "vT":
                            st.link(v.tensor_scalar(lstg[:, k, :, :], lstg[:, k, :, :], 0.5, None, ALU.mult))
                        st.link(v.tensor_copy(hi[:, :, :], lstg[:, k, :, :]))
                        st.add(v.tensor_tensor(lo[:, :, :], lstg[:, k, :, :], hi[:, :, :].bitcast(F32), ALU.subtract))
                    v.wait_ge(acc_done, 1)
                    v.tensor_copy(acc_avg[:, :, :].rearrange("p c b -> p (c b)"), psum[3][:, 0:HC * B]).then_inc(acc_ready, 1)
                    v.wait_ge(acc_ready, 1)
                    base = st.n

                    def quant(n, at):
                        sel = lambda m: m[:, bass.ds(n, 1), :, :].rearrange("p o k t -> p (o k t)")
                        after(v, hq_done, n)
                        v.tensor_scalar(qy[:, :], sel(ff), inv[:, A_CAT:A_CAT + 1], ROUND, ALU.mult, ALU.add).then_inc(v_hid, 1)
                        v.wait_ge(v_hid, at + 1)
                        v.tensor_scalar(sel(qf), qy[:, :], ROUND, None, ALU.subtract).then_inc(hq_done, 1)

                    def body(n, ahead):
                        at = base + 1 + KH * n
                        if ahead:
                            quant(n + 1, at)
                        else:
                            v.wait_ge(v_hid, at)
                        for q in range(HC // 2):
                            v.wait_ge(h_done, 4 * n + q + 1)
                            v.tensor_reduce(hcur[:, 2 * q:2 * q + 2], psum[q][:, :].rearrange("p (c t) -> p c t", c=2), X, ALU.max).then_inc(h_red, 1)
                        v.wait_ge(h_red, 4 * n + 4)
                        at = at + (1 if ahead else 0)
                        v.tensor_tensor(hcur[:, :], hcur[:, :], acc_avg[:, :, bass.ds(n, 1)].rearrange("p c o -> p (c o)"), ALU.add).then_inc(v_hid, 1)
                        v.wait_ge(v_hid, at + 1)
                        v.tensor_tensor(hmax8[:, :], hmax8[:, :], hcur[:, :], ALU.max).then_inc(v_hid, 1)
                    quant(0, base)
                    body(0, True)
                    with v.Fori(1, B - 1) as n:
                        body(n, True)
                    body(B - 1, False)
                    end = base + 1 + KH * B - 1
                    v.wait_ge(v_hid, end)
                    st2 = Steps(v, v_hid, end)
                    st2.link(v.tensor_scalar(hmax8[:, :], hmax8[:, :], oscale[:, O_F1:O_F1 + 1], None, ALU.mult))
                    st2.link(v.tensor_tensor(hmax8[:, :], hmax8[:, :], cols[:, COLS["b_f1"][0]:COLS["b_f1"][0] + HC], ALU.add))
                    st2.link(v.tensor_reduce(tmax[:, :], hmax8[:, :], X, ALU.max))
                    st2.link(v.tensor_scalar(tmax[:, :], tmax[:, :], 0.0, None, ALU.max))
            stack.pop()

        hb = sb("hb", [P, HC, B])
        s1h = sb("s1h", [P, 1])

        def hidden_bias(v, st):
            st.link(v.tensor_scalar(hb[:, :, :], acc_avg[:, :, :], oscale[:, O_F1:O_F1 + 1], None, ALU.mult))
            st.add(v.tensor_tensor(s1h[:, :], oscale[:, O_F1:O_F1 + 1], inv[:, A_H:A_H + 1], ALU.mult))
            st.link(v.tensor_tensor(hb[:, :, :], hb[:, :, :],
                                    cols[:, COLS["b_f1"][0]:COLS["b_f1"][0] + HC].unsqueeze(2).broadcast_to([P, HC, B]), ALU.add))
            st.link(v.tensor_scalar(hb[:, :, :], hb[:, :, :], inv[:, A_H:A_H + 1], None, ALU.mult))

        scale_step("hidden", A_H, [(O_F2, W_F2, A_H)], hidden_bias)
        L3 = 2
        with ExitStack() as scope:
            space = ff[:, :, :, :].rearrange("p b k t -> p (b k t)")
            used = [0]

            def view(*shape):
                n = 1
                for q in shape:
                    n *= q
                at = used[0]
                used[0] += n
                assert used[0] <= B * KC * T
                flat = space[:, at:at + n]
                if len(shape) == 1:
                    return flat
                return flat.rearrange("p (a b) -> p a b", a=shape[0])

            stack.append(scope)
            xt = [view(NT, C) for _ in range(L3)]
            xnn = [view(NT, C) for _ in range(L3)]
            zd = [view(KC, T) for _ in range(L3)]
            xm = [view(KC, T) for _ in range(L3)]
            tr = [view(NT * C) for _ in range(L3)]
            kr = [view(KC, T) for _ in range(L3)]
            hr2 = [view(2, T) for _ in range(L3)]
            yo = [view(NT, C) for _ in range(L3)]
            zz = [sb(f"zz{l}", [P, KC, T + 1]) for l in range(L3)]
            hq = [sb(f"hq{l}", [P, HC, T], BF16) for l in range(L3)]
            mp = [(sb(f"mp_hi{l}", [P, KC, T], F32R), sb(f"mp_lo{l}", [P, KC, T], F32R)) for l in range(L3)]
            hbs = [sb(f"hbs{l}", [P, HC]) for l in range(L3)]
            st6 = [sb(f"st6{l}", [P, NT, 6]) for l in range(L3)]
            me, va, vt, rr = ([sb(f"{q}{l}", [P, NT]) for l in range(L3)] for q in ("me", "va", "vt", "rr"))
            fl_ = lambda ap: ap.rearrange("p a b -> p (a b)")
            xt_loaded, y_stored = ([sem(f"fin_{q}{l}") for l in range(L3)] for q in ("x_loaded", "y_stored"))
            (hbs_ready, f1_done, hrelu_done, hround_done, f2_done, xb_ready, x4_ready, ve4, rs4, xn4, z_turned, z_ready,
             zd_ready, mix_done, m_hi, m_lo, r_done, k_done, tr_ready, kr_ready, ksq_ready, v_done, y_ready, yo_used, v_fin, p_fin) = (sem("fin_" + q) for q in (
                 "hbs_ready", "f1_done", "relu_done", "round_done", "f2_done", "xb_ready", "x4_ready", "ve", "rs", "xn", "z_turned",
                 "z_ready", "zd_ready", "mix_done", "mix_hi", "mix_lo", "r_done", "k_done", "tanh_ready", "krelu_ready",
                 "ksq_ready", "v_done", "y_ready", "yo_used", "dve", "pool"))
            NJ3 = B // L3
            out_v = out.rearrange("b (t p) c -> b p t c", p=P)
            x3r_v = x3_dram.rearrange("b (t p) c -> b p t c", p=P)
            KF3 = 10 * L3
            G = lambda l: psum[2 * l]
            TT = lambda l: psum[2 * l + 1]

            def hbank(l, c):
                return psum[2 * l + (c % 4) // 2][:, (c % 2) * T:(c % 2 + 1) * T]

            with nc.Block() as block:
                @block.sync
                def _(sp):
                    def load(j):
                        for l in range(L3):
                            after(sp, y_ready, L3 * j + l + 1 - L3)
                            sp.dma_start(xt[l], one(x3r_v, L3 * j + l)).then_inc(xt_loaded[l], 16)

                    def store(j):
                        for l in range(L3):
                            sp.wait_ge(y_ready, L3 * j + l + 1)
                            sp.dma_start(one(out_v, L3 * j + l), yo[l]).then_inc(y_stored[l], 16)
                    load(0)
                    store(0)
                    with sp.Fori(1, NJ3) as j:
                        load(j)
                        store(j)
                    for l in range(L3):
                        sp.wait_ge(y_stored[l], 16 * NJ3)

                @block.gpsimd
                def _(g):
                    def body(j):
                        for l in range(L3):
                            g.wait_ge(xt_loaded[l], 16 * j + 16)
                            g.tensor_tensor(xt[l], xt[l], bf2_row.unsqueeze(1).broadcast_to([P, NT, C]), ALU.add).then_inc(xb_ready, 1)
                        for l in range(L3):
                            g.wait_ge(ve4, L3 * j + l + 1)
                            g.tensor_tensor(rr[l][:, :], va[l][:, :], neg_half[:, :], ALU.pow).then_inc(rs4, 1)
                        for l in range(L3):
                            g.wait_ge(z_ready, L3 * j + l + 1)
                            g.tensor_tensor(zd[l], zz[l][:, :, 1:T + 1], zz[l][:, :, 0:T], ALU.subtract).then_inc(zd_ready, 1)
                    first_then_loop(g, body, NJ3)

                @block.scalar
                def _(s):
                    def body(j):
                        for c in range(HC):
                            for l in range(L3):
                                u = HC * L3 * j + L3 * c + l
                                s.wait_ge(f1_done, u + 1)
                                if c == 0:
                                    s.wait_ge(hbs_ready, L3 * j + l + 1)
                                after(s, hround_done, u + 1 - 2 * L3)
                                s.activation(hr2[l][:, c % 2, :], hbank(l, c), ACT.Relu, bias=hbs[l][:, c:c + 1], scale=s1h[:, :]).then_inc(hrelu_done, 1)
                        for l in range(L3):
                            s.wait_ge(z_turned, L3 * j + l + 1)
                            after(s, mix_done, 2 * L3 * j - L3 + l + 1)
                            s.activation(zz[l][:, :, 1:T + 1], TT(l)[:, :].rearrange("p (k t) -> p k t", k=KC), ACT.Copy).then_inc(z_ready, 1)
                        for m in range(2):
                            for l in range(L3):
                                s.wait_ge(mix_done, 2 * L3 * j + L3 * m + l + 1)
                                if m == 0:
                                    after(s, v_done, L3 * j + l + 1 - L3)
                                else:
                                    s.wait_ge(r_done, L3 * j + l + 1)
                                s.activation(mp[l][0][:, :, :], xm[l], ACT.Copy).then_inc(m_hi, 1)
                            if m == 0:
                                for l in range(L3):
                                    s.wait_ge(r_done, L3 * j + l + 1)
                                    after(s, y_ready, L3 * j + l + 1 - L3)
                                    s.activation(tr[l], G(l)[:, :], ACT.Tanh, scale=0.5).then_inc(tr_ready, 1)
                        for l in range(L3):
                            s.wait_ge(k_done, L3 * j + l + 1)
                            s.activation(fl_(kr[l]), TT(l)[:, :], ACT.Relu).then_inc(kr_ready, 1)
                        for l in range(L3):
                            s.wait_ge(ksq_ready, L3 * j + l + 1)
                            s.activation(mp[l][0][:, :, :], xm[l], ACT.Copy).then_inc(m_hi, 1)
                    first_then_loop(s, body, NJ3)

                @block.tensor
                def _(pe):
                    sl = slice(None)

                    def body(j):
                        for c in range(HC):
                            for l in range(L3):
                                n = L3 * j + l
                                u = HC * L3 * j + L3 * c + l
                                if c == 0:
                                    after(pe, y_ready, n + 1 - L3)
                                if c >= 4:
                                    pe.wait_ge(hrelu_done, u + 1 - 4 * L3)
                                for k in range(KC):
                                    last = pe.matmul(hbank(l, c), wf1[:, k, c * P:(c + 1) * P],
                                                     qf[:, bass.ds(n, 1), k, :].rearrange("p o t -> p (o t)"), start=(k == 0), stop=(k == KC - 1))
                                last.then_inc(f1_done, 1)
                        for l in range(L3):
                            pe.wait_ge(hround_done, HC * L3 * j + L3 * (HC - 1) + l + 1)
                            for t in range(NT):
                                for c in range(HC):
                                    last = pe.matmul(G(l)[:, t * C:(t + 1) * C], hq[l][:, c, t * P:(t + 1) * P], wf2[:, c, :],
                                                     start=(c == 0), stop=(c == HC - 1))
                            last.then_inc(f2_done, 1)
                        for l in range(L3):
                            pe.wait_ge(xn4, L3 * j + l + 1)
                            for c in range(KC):
                                for t in range(NT):
                                    last = pe.transpose(TT(l)[:, c * T + t * P:c * T + (t + 1) * P], xnn[l][:, t, c * P:(c + 1) * P], ident[:, :])
                            last.then_inc(z_turned, 1)
                        for l in range(L3):
                            pe.wait_ge(m_lo, 3 * L3 * j + l + 1)
                            for t in range(NT):
                                for k in range(KC):
                                    last = mm3(pe, G(l)[:, t * C:(t + 1) * C], pair(mp[l], sl, k, slice(t * P, (t + 1) * P)),
                                               pair(lw["rT"], sl, k, sl), k == 0, k == KC - 1)
                            last.then_inc(r_done, 1)
                        for l in range(L3):
                            pe.wait_ge(m_lo, 3 * L3 * j + L3 + l + 1)
                            for c in range(KC):
                                for k in range(KC):
                                    last = mm3(pe, TT(l)[:, c * T:(c + 1) * T], pair(lw["kT"], sl, k, slice(c * P, (c + 1) * P)),
                                               pair(mp[l], sl, k, sl), k == 0, k == KC - 1)
                            last.then_inc(k_done, 1)
                        for l in range(L3):
                            pe.wait_ge(m_lo, 3 * L3 * j + 2 * L3 + l + 1)
                            for t in range(NT):
                                for k in range(KC):
                                    last = mm3(pe, G(l)[:, t * C:(t + 1) * C], pair(mp[l], sl, k, slice(t * P, (t + 1) * P)),
                                               pair(lw["vT"], sl, k, sl), k == 0, k == KC - 1)
                            last.then_inc(v_done, 1)
                    first_then_loop(pe, body, NJ3)

                @block.vector
                def _(v):
                    for l in range(L3):
                        v.memset(zz[l][:, :, 0:1], 0.0)

                    def body(j):
                        st = Steps(v, v_fin, KF3 * j)
                        for l in range(L3):
                            n = L3 * j + l
                            after(v, hrelu_done, HC * L3 * j)
                            v.tensor_scalar(hbs[l][:, :], hb[:, :, bass.ds(n, 1)].rearrange("p c o -> p (c o)"), 1.0, None, ALU.mult).then_inc(hbs_ready, 1)
                        for c in range(HC):
                            for l in range(L3):
                                u = HC * L3 * j + L3 * c + l
                                v.wait_ge(hrelu_done, u + 1)
                                after(v, f2_done, L3 * j)
                                v.tensor_scalar(hq[l][:, c, :], hr2[l][:, c % 2, :], ROUND, ROUND, ALU.add, ALU.subtract).then_inc(hround_done, 1)
                        for l in range(L3):
                            v.wait_ge(f2_done, L3 * j + l + 1)
                            v.wait_ge(xb_ready, L3 * j + l + 1)
                            v.scalar_tensor_tensor(out=fl_(xt[l]), in0=G(l)[:, :], scalar=oscale[:, O_F2:O_F2 + 1], in1=fl_(xt[l]),
                                                   op0=ALU.mult, op1=ALU.add).then_inc(x4_ready, 1)
                        for l in range(L3):
                            v.wait_ge(x4_ready, L3 * j + l + 1)
                            stats(st, xt[l], st6[l], me[l], va[l], vt[l], ve4)
                        for l in range(L3):
                            v.wait_ge(rs4, L3 * j + l + 1)
                            for t in range(NT):
                                last = v.tensor_scalar(xnn[l][:, t, :], xt[l][:, t, :], me[l][:, t:t + 1], rr[l][:, t:t + 1], ALU.subtract, ALU.mult)
                            last.then_inc(xn4, 1)
                        for m, mu in enumerate(("mu_r", "mu_k")):
                            for l in range(L3):
                                if m == 0:
                                    v.wait_ge(zd_ready, L3 * j + l + 1)
                                    after(v, m_lo, 3 * L3 * j - L3 + l + 1)
                                else:
                                    v.wait_ge(m_lo, 3 * L3 * j + l + 1)
                                for c in range(KC):
                                    last = v.scalar_tensor_tensor(out=xm[l][:, c, :], in0=zd[l][:, c, :], scalar=col(mu, c), in1=zz[l][:, c, 0:T],
                                                                  op0=ALU.mult, op1=ALU.add)
                                last.then_inc(mix_done, 1)
                            for l in range(L3):
                                v.wait_ge(m_hi, 3 * L3 * j + L3 * m + l + 1)
                                v.tensor_tensor(mp[l][1][:, :, :], xm[l], mp[l][0][:, :, :].bitcast(F32), ALU.subtract).then_inc(m_lo, 1)
                        for l in range(L3):
                            v.wait_ge(kr_ready, L3 * j + l + 1)
                            v.wait_ge(m_lo, 3 * L3 * j + L3 + l + 1)
                            v.tensor_tensor(xm[l], kr[l], kr[l], ALU.mult).then_inc(ksq_ready, 1)
                        for l in range(L3):
                            v.wait_ge(m_hi, 3 * L3 * j + 2 * L3 + l + 1)
                            v.tensor_tensor(mp[l][1][:, :, :], xm[l], mp[l][0][:, :, :].bitcast(F32), ALU.subtract).then_inc(m_lo, 1)
                        for l in range(L3):
                            v.wait_ge(v_done, L3 * j + l + 1)
                            v.wait_ge(tr_ready, L3 * j + l + 1)
                            after(v, y_stored[l], 16 * j)
                            v.scalar_tensor_tensor(out=fl_(yo[l]), in0=tr[l], scalar=1.0, in1=G(l)[:, :], op0=ALU.add, op1=ALU.mult).then_inc(yo_used, 1)
                        for l in range(L3):
                            v.wait_ge(yo_used, L3 * j + l + 1)
                            v.tensor_tensor(yo[l], yo[l], xt[l], ALU.add).then_inc(y_ready, 1)
                        assert st.n == KF3, st.n
                    first_then_loop(v, body, NJ3)
            stack.pop()
        ff_scope.close()
        stack.pop()
    return nc


def kernel(**inputs):
    import numpy as np
    import concourse.bacc as bacc
    from concourse.bass_utils import run_bass_kernel_spmd

    g = lambda name: np.asarray(inputs[name])
    c = np.ascontiguousarray
    chunks = lambda name: g(name).reshape(-1, P)
    arrays = {
        "x": c(g("x")),
        "ctxT": c(g("ctx_768").reshape(NCTX, D).T),
        "WkT": c(g("L0_xattn_Wk").T), "WvT": c(g("L0_xattn_Wv").T), "Wq": c(g("L0_xattn_Wq")),
        "Wr": c(g("L0_ffn_Wr")), "Wv": c(g("L0_ffn_Wv")), "Wo": c(g("L0_ffn_Wo")), "WsT": c(g("L0_ffn_Ws").T),
        "K": c(g("L0_ffn_K_rwkv").reshape(2 * C, H)), "V": c(g("L0_ffn_V_rwkv").reshape(2 * H, C)),
        "W1": c(g("L0_ffn_W1")), "W2": c(g("L0_ffn_W2")), "W3": c(g("L0_ffn_W3")),
        "wb": c(np.concatenate([g("L0_ffn_conf_rwkv").T, g("L0_ffn_conf_trans")[:, None],
                                g("L0_ffn_w_diff")[:, None], g("L0_ffn_W_aff")], axis=1)),
        "d2v": c(g("L1_xattn_W_d2v").T), "img": c(g("L1_xattn_W_img").T), "txt": c(g("L1_xattn_W_txt").T),
        "att": c(np.concatenate([g("L1_xattn_W_att0").T, g("L1_xattn_W_att1").T], axis=1)),
        "f1": c(g("L1_xattn_W_f1").T), "f2": c(g("L1_xattn_W_f2").T),
        "rT": c(g("L1_ffn_W_r").T), "kT": c(g("L1_ffn_W_k").T), "vT": c(g("L1_ffn_W_v").T),
        "rows": c(np.concatenate([g("L0_xattn_bv"), g("L1_xattn_b_f2"), g("L0_ffn_capital_shares")])),
    }
    packed = {"bq": "L0_xattn_bq", "bk": "L0_xattn_bk", "ln1_w": "L0_ffn_ln1_w", "ln1_b": "L0_ffn_ln1_b",
              "ln2_w": "L0_ffn_ln2_w", "ln2_b": "L0_ffn_ln2_b", "b_d2v": "L1_xattn_b_d2v", "b_img": "L1_xattn_b_img",
              "b_txt": "L1_xattn_b_txt", "b_att0": "L1_xattn_b_att0", "b_att1": "L1_xattn_b_att1",
              "b_f1": "L1_xattn_b_f1", "mu_r": "L1_ffn_mu_r", "mu_k": "L1_ffn_mu_k"}
    arrays["cols"] = c(np.concatenate([chunks(packed[name]) for name in COLS]).T)

    nc = bacc.Bacc("TRN2", target_bir_lowering=False, num_devices=1)
    aps = {n: nc.dram_tensor("in_" + n, v.shape, mybir.dt.from_np(v.dtype), kind="ExternalInput").ap()
           for n, v in arrays.items()}
    out = nc.dram_tensor("out_0", (B, T, C), F32, kind="ExternalOutput").ap()
    build(nc, aps, out)
    r = run_bass_kernel_spmd(nc, [{"in_" + n: v for n, v in arrays.items()}], core_ids=[0])
    return r.results[0]["out_0"]
```

```python
from contextlib import ExitStack

import concourse.bass as bass
from concourse import mybir

F32, F32R, BF16 = mybir.dt.float32, mybir.dt.float32r, mybir.dt.bfloat16
ALU = mybir.AluOpType
ACT = mybir.ActivationFunctionType
X, XY = mybir.AxisListType.X, mybir.AxisListType.XY
RED = bass.bass_isa.ReduceOp

P = 128
B, T, C = 16, 512, 256
NT = T // P
KC = C // P
S, D = 64, 192
H = 1024
HC = H // P
NCTX = B * S
EPS = 1e-5
ROUND = 12582912.0
INV_SQRT = 1.0 / 16.0
NCHUNK = 2 + 2 * HC
GROUP_END = {1: 0, 1 + HC: 1, 1 + 2 * HC: 2}
GROUP_START = (0, 2, 2 + HC)
GROUP_EXPERT = (2, 0, 1)

COLS = {}
for _name, _n in (("bq", 2), ("bk", 2), ("ln1_w", 2), ("ln1_b", 2), ("ln2_w", 2), ("ln2_b", 2), ("b_d2v", 2),
                  ("b_img", 2), ("b_txt", 2), ("b_att0", 1), ("b_att1", 1), ("b_f1", 8), ("mu_r", 2), ("mu_k", 2)):
    COLS[_name] = (sum(n for _, n in COLS.values()), _n)
NCOLS = sum(n for _, n in COLS.values())


class Steps:

    def __init__(self, eng, sem, base=0):
        self.eng, self.sem, self.base, self.n = eng, sem, base, 0

    def add(self, ins):
        ins.then_inc(self.sem, 1)
        self.n += 1

    def wait(self):
        self.eng.wait_ge(self.sem, self.base + self.n)

    def link(self, ins):
        self.add(ins)
        self.wait()


def after(eng, sem, value):
    if not isinstance(value, int) or value > 0:
        eng.wait_ge(sem, value)


def build(nc, a, out):
    x3_dram = nc.dram_tensor("x3_scratch", [B, T, C], F32, kind="Internal").ap()
    text_dram = nc.dram_tensor("text_scratch", [B, T, C], F32, kind="Internal").ap()
    ms_dram = nc.dram_tensor("ms_scratch", [B, P, KC * S], F32, kind="Internal").ap()
    vs_dram = nc.dram_tensor("vs_scratch", [B, S, C], F32, kind="Internal").ap()
    cs_dram = nc.dram_tensor("cs_scratch", [B, 1, S], F32, kind="Internal").ap()
    kv_dram = nc.dram_tensor("kv_scratch", [B, P, 2 * S], F32, kind="Internal").ap()
    kvt_dram = nc.dram_tensor("kvt_scratch", [B, S, 2 * P], F32, kind="Internal").ap()

    with ExitStack() as top:
        stack = [top]

        def sb(name, shape, dt=F32):
            return stack[-1].enter_context(nc.sbuf_tensor(name, shape, dt))

        def sem(name):
            return top.enter_context(nc.semaphore(name))

        psum = [top.enter_context(nc.psum_tensor(f"pair{k}", [P, 1024], F32)) for k in range(4)]
        up_ps, out_ps, tp_ps, g_ps = psum

        cols = sb("cols", [P, NCOLS])

        def col(name, k=0):
            at, n = COLS[name]
            assert k < n
            return cols[:, at + k:at + k + 1]

        rows = sb("rows", [P, 2 * C + 3])
        bv_row, bf2_row, cap = rows[:, 0:C], rows[:, C:2 * C], rows[:, 2 * C:2 * C + 3]
        ident = sb("ident", [P, P])
        ident_b = sb("ident_b", [P, P], BF16)
        ones = sb("ones", [1, P])
        neg_half2 = sb("neg_half", [P, 2, NT])
        neg_half = neg_half2[:, 0, :]
        wtxt = sb("wtxt", [P, KC, C], BF16)
        watt = sb("watt", [P, KC, 2, P], BF16)
        wf1 = sb("wf1", [P, 2 * KC, H], BF16)
        wf2 = sb("wf2", [P, HC, C], BF16)
        q_img = sb("q_img", [P, KC, NCTX], BF16)
        avg = sb("avg", [P, KC, B])
        NW = 7
        W_D2V, W_IMG, W_TXT, W_A0, W_A1, W_F1, W_F2 = range(NW)
        wabs = sb("wabs", [P, NW])
        wsum = sb("wsum", [P, NW])
        wscale = sb("wscale", [P, NW])
        thr = sb("thr", [P, 2, NW])
        NA_ = 6
        A_CTX, A_VIS, A_IMG, A_TXT, A_CAT, A_H = range(NA_)
        amax = sb("amax", [P, NA_])
        gmax = sb("gmax", [P, NA_])
        iscale = sb("iscale", [P, NA_])
        inv = sb("inv", [P, NA_])
        oscale = sb("oscale", [P, 8])
        tmax = sb("tmax", [P, 1])
        tcur = sb("tcur", [P, 1])

        v_set, p_set = sem("setup_dve"), sem("setup_pool")

        kv_scope = ExitStack()
        stack.append(kv_scope)
        names = ("Wr", "W2s", "Wv", "Wo", "W1", "W3")
        w = {n: (sb(n + "_hi", [P, KC, C], F32R), sb(n + "_lo", [P, KC, C], F32R)) for n in names}
        kexp = (sb("kexp_hi", [P, 2 * KC, H], F32R), sb("kexp_lo", [P, 2 * KC, H], F32R))
        vexp = (sb("vexp_hi", [P, 2 * HC, C], F32R), sb("vexp_lo", [P, 2 * HC, C], F32R))
        wb = sb("wb", [P, KC, 7])

        def mm3(pe, dst, st, mv, start, stop):
            pe.matmul(dst, st[1], mv[0], start=start, stop=False, skip_group_check=True)
            pe.matmul(dst, st[0], mv[1], start=False, stop=False, skip_group_check=True)
            return pe.matmul(dst, st[0], mv[0], start=False, stop=stop, skip_group_check=True)

        def stats(st, src, stat, mean, var, tmp, ready):
            for t in range(NT):
                st.add(st.eng.bn_stats(stat[:, t, :], src[:, t, :]))
            st.wait()
            e = lambda q: stat[:, :, q:q + 1].rearrange("p t o -> p (t o)")
            st.add(st.eng.tensor_tensor(mean[:, :], e(1), e(4), ALU.add))
            st.add(st.eng.tensor_tensor(tmp[:, :], e(1), e(4), ALU.subtract))
            st.link(st.eng.tensor_tensor(var[:, :], e(2), e(5), ALU.add))
            st.add(st.eng.tensor_scalar(mean[:, :], mean[:, :], 0.5, None, ALU.mult))
            st.add(st.eng.tensor_tensor(tmp[:, :], tmp[:, :], tmp[:, :], ALU.mult))
            st.link(st.eng.tensor_scalar(var[:, :], var[:, :], 1.0 / C, EPS, ALU.mult, ALU.add))
            last = st.eng.scalar_tensor_tensor(out=var[:, :], in0=tmp[:, :], scalar=0.25, in1=var[:, :],
                                               op0=ALU.mult, op1=ALU.add)
            if ready is None:
                st.link(last)
            else:
                last.then_inc(ready, 1)

        def pair(t, *ix):
            return (t[0][ix], t[1][ix])

        with ExitStack() as scope:
            stack.append(scope)
            stg = [sb(f"stg{k}", [P, 4096]) for k in range(2)]
            ctx = sb("ctx", [P, 2, NCTX])
            act = sb("act", [P, KC, NCTX])
            qa = sb("qa", [P, KC, NCTX], BF16)
            ms_all = act
            cs_all = sb("cs_all", [1, NCTX])
            v_all = sb("v_all", [S, B, C])
            stored = sem("setup_stored")

            ternary = [("d2v", W_D2V), ("img", W_IMG), ("txt", W_TXT), ("att", W_A0), ("f1", W_F1), ("f2", W_F2)]
            wd2v = sb("wd2v", [P, 2, C], BF16)
            wimg = sb("wimg", [P, KC, C], BF16)
            tern_dst = {"d2v": wd2v, "img": wimg, "txt": wtxt, "att": watt, "f1": wf1, "f2": wf2}
            tern_n = {"d2v": 2 * C, "img": KC * C, "txt": KC * C, "att": KC * C, "f1": 4 * H, "f2": HC * C}
            ta = sb("ta", [P, 2048], BF16)
            tb_ = sb("tb_", [P, 2048], BF16)

            with nc.Block() as block:
                loads = []
                kpn = lambda ap: ap.rearrange("(k p) n -> p k n", p=P)

                def view(k, chunks, n):
                    return stg[k][:, 0:chunks * n].rearrange("p (k n) -> p k n", k=chunks)

                v0 = view(0, 2, C)
                loads.append((0, [(v0[:, 0, :], a["d2v"][0:P, :]), (v0[0:D - P, 1, :], a["d2v"][P:D, :])]))
                loads.append((1, [(view(1, 2, C), kpn(a["img"]))]))
                loads.append((0, [(view(0, 2, C), kpn(a["txt"]))]))
                loads.append((1, [(view(1, 2, C), kpn(a["att"]))]))
                loads.append((0, [(view(0, 4, H), kpn(a["f1"]))]))
                loads.append((1, [(view(1, 8, C), kpn(a["f2"]))]))
                loads.append((0, [(view(0, 2, C), kpn(a["Wr"]))]))
                loads.append((1, [(view(1, 2, C), kpn(a["Wv"]))]))
                loads.append((0, [(view(0, 2, C), kpn(a["Wo"]))]))
                loads.append((1, [(view(1, 2, C), kpn(a["W1"]))]))
                loads.append((0, [(view(0, 2, C), kpn(a["W3"]))]))
                loads.append((1, [(view(1, 4, H), kpn(a["K"]))]))
                loads.append((0, [(view(0, 16, C), kpn(a["V"]))]))
                loads.append((1, [(stg[1][:, 0:512].rearrange("p (k n) -> p k n", k=2), kpn(a["WsT"])),
                                  (stg[1][:, 512:1024].rearrange("p (k n) -> p k n", k=2), kpn(a["W2"]))]))
                loads.append((0, [(stg[0][:, 0:512].rearrange("p (k n) -> p k n", k=2), kpn(a["Wq"])),
                                  (stg[0][:, 512:768], a["WkT"][0:P, :]), (stg[0][0:D - P, 768:1024], a["WkT"][P:D, :]),
                                  (stg[0][:, 1024:1280], a["WvT"][0:P, :]), (stg[0][0:D - P, 1280:1536], a["WvT"][P:D, :])]))
                ctx_k = stg[1][:, 2048:4096].rearrange("p (k n) -> p k n", k=2)
                stg_loaded, stg_used = sem("stg_loaded"), sem("stg_used")
                n_loaded = []
                for k, parts in loads:
                    n_loaded.append((n_loaded[-1] if n_loaded else 0) + 16 * len(parts))
                consts_loaded, ctx_zeroed = sem("consts_loaded"), sem("ctx_zeroed")

                @block.sync
                def _(sp):
                    sp.dma_start(cols[:, :], a["cols"]).then_inc(consts_loaded, 16)
                    sp.dma_start(rows[:, :], a["rows"].partition_broadcast(P)).then_inc(consts_loaded, 16)
                    sp.dma_start(wb[:, :, :], kpn(a["wb"])).then_inc(consts_loaded, 16)
                    sp.wait_ge(ctx_zeroed, 3)
                    sp.dma_start(ctx[:, 0, :], a["ctxT"][0:P, :]).then_inc(consts_loaded, 16)
                    sp.dma_start(ctx[0:D - P, 1, :], a["ctxT"][P:D, :]).then_inc(consts_loaded, 16)
                    for n, (k, parts) in enumerate(loads):
                        if n >= 2:
                            sp.wait_ge(stg_used, n - 1)
                        for dst, src in parts:
                            sp.dma_start(dst, src).then_inc(stg_loaded, 16)
                        sp.wait_ge(stg_loaded, n_loaded[n])

                sw_w = sem("weight_sums"), sem("weight_sums_all")
                am_s, gm_s = sem("act_max"), sem("act_max_all")
                q_ready, lin_done, f32_ready = sem("q_ready"), sem("lin_done"), sem("lin_f32")

                @block.gpsimd
                def _(g):
                    g.memset(ident[:, :], 0.0).then_inc(p_set, 1)
                    g.memset(ident_b[:, :], 0.0).then_inc(p_set, 1)
                    g.memset(ones[:, :], 1.0).then_inc(p_set, 1)
                    g.memset(neg_half2[:, :, :], -0.5).then_inc(p_set, 1)
                    g.wait_ge(p_set, 4)
                    for m in (ident, ident_b):
                        g.affine_select(out=m[:, :], in_=m[:, :], compare_op=ALU.not_equal, fill=1.0, base=0,
                                        pattern=[[-1, P]], channel_multiplier=1).then_inc(p_set, 1)
                    for k in range(NW):
                        g.wait_ge(sw_w[0], k + 1)
                        g.partition_all_reduce(wsum[:, k:k + 1], wabs[:, k:k + 1], P, RED.add).then_inc(sw_w[1], 1)
                        if k == W_D2V:
                            g.wait_ge(am_s, 1)
                            g.partition_all_reduce(gmax[:, 0:1], amax[:, 0:1], P, RED.max).then_inc(gm_s, 1)
                    for k in (1, 2):
                        g.wait_ge(am_s, k + 1)
                        g.partition_all_reduce(gmax[:, k:k + 1], amax[:, k:k + 1], P, RED.max).then_inc(gm_s, 1)

                w2s_split = sem("w2s_split")
                kx_done, kx_ready = sem("kx_done"), sem("kx_ready")

                @block.vector
                def _(v):
                    st = Steps(v, v_set)
                    v.memset(ctx[:, 1, :], 0.0).then_inc(ctx_zeroed, 1)
                    v.memset(stg[0][:, 0:512], 0.0).then_inc(ctx_zeroed, 1)
                    v.memset(tmax[:, :], 0.0).then_inc(ctx_zeroed, 1)

                    def act_max(k, src):
                        v.tensor_reduce(amax[:, k:k + 1], src, XY, ALU.max, apply_absolute_value=True).then_inc(am_s, 1)

                    def act_scale(k):
                        v.wait_ge(gm_s, k + 1)
                        st.link(v.tensor_scalar(iscale[:, k:k + 1], gmax[:, k:k + 1], 1e-8, 1.0 / 127.0, ALU.max, ALU.mult))
                        st.link(v.reciprocal(inv[:, k:k + 1], iscale[:, k:k + 1]))

                    def quantise(k, src, dst):
                        for c in range(2):
                            y = stg[1][:, 2048 + 1024 * c:3072 + 1024 * c]
                            st.link(v.tensor_scalar(y, src[:, c, :], inv[:, k:k + 1], ROUND, ALU.mult, ALU.add))
                            last = v.tensor_scalar(dst[:, c, :], y, ROUND, None, ALU.subtract)
                        last.then_inc(q_ready, 1)

                    v.wait_ge(consts_loaded, 80)
                    act_max(A_CTX, ctx[:, :, :])
                    for n, (name, k0) in enumerate(ternary):
                        v.wait_ge(stg_loaded, n_loaded[n])
                        size = tern_n[name]
                        flat = stg[loads[n][0]][:, 0:size]
                        if name == "att":
                            f3 = flat.rearrange("p (k a n) -> p k a n", k=KC, a=2)
                            for j in range(2):
                                v.tensor_reduce(wabs[:, k0 + j:k0 + j + 1], f3[:, :, j, :], XY, ALU.add,
                                                apply_absolute_value=True).then_inc(sw_w[0], 1)
                            jobs = [(k0 + j, f3[:, :, j, :], watt[:, :, j, :], C * P) for j in range(2)]
                        else:
                            v.tensor_reduce(wabs[:, k0:k0 + 1], flat, X, ALU.add,
                                            apply_absolute_value=True).then_inc(sw_w[0], 1)
                            dst = tern_dst[name][:, :, :].rearrange("p k n -> p (k n)")
                            total = {"d2v": D * C, "img": C * C, "txt": C * C, "f1": 2 * C * H, "f2": H * C}[name]
                            half = min(size, 2048)
                            jobs = [(k0, flat[:, o:o + half], dst[:, o:o + half], total) for o in range(0, size, half)]
                        for j, (k, src, dst, total) in enumerate(jobs):
                            if name == "att" or j == 0:
                                v.wait_ge(sw_w[1], k + 1)
                                st.link(v.tensor_scalar(wscale[:, k:k + 1], wsum[:, k:k + 1], 1.0 / total, 1e-5, ALU.mult, ALU.max))
                                st.add(v.tensor_scalar(thr[:, 0, k:k + 1], wscale[:, k:k + 1], 0.5, None, ALU.mult))
                                st.link(v.tensor_scalar(thr[:, 1, k:k + 1], wscale[:, k:k + 1], -0.5, None, ALU.mult))
                            if name == "att":
                                up = ta[:, 0:C].rearrange("p (k n) -> p k n", k=KC)
                                dn = tb_[:, 0:C].rearrange("p (k n) -> p k n", k=KC)
                            else:
                                up, dn = ta[:, 0:src.shape[1]], tb_[:, 0:src.shape[1]]
                            st.add(v.tensor_scalar(up, src, thr[:, 0, k:k + 1], None, ALU.is_gt))
                            st.link(v.tensor_scalar(dn, src, thr[:, 1, k:k + 1], None, ALU.is_lt))
                            st.link(v.tensor_tensor(dst, up, dn, ALU.subtract))
                        v.sem_inc(stg_used, 1)
                        if name == "d2v":
                            act_scale(A_CTX)
                            st.link(v.tensor_tensor(oscale[:, 0:1], wscale[:, 0:1], iscale[:, 0:1], ALU.mult))
                            quantise(A_CTX, ctx, qa)
                    for k, wk in ((A_VIS, W_IMG), (A_IMG, None)):
                        v.wait_ge(f32_ready, 4 * k)
                        act_max(k, act[:, :, :])
                        act_scale(k)
                        if wk is not None:
                            st.link(v.tensor_tensor(oscale[:, k:k + 1], wscale[:, wk:wk + 1], iscale[:, k:k + 1], ALU.mult))
                        v.wait_ge(lin_done, 4 * k)
                        v.wait_ge(stg_loaded, n_loaded[7])
                        quantise(k, act, qa if k == A_VIS else q_img)
                    av = act[:, :, :].rearrange("p k (b s) -> p (k b) s", s=S)
                    st.link(v.tensor_reduce(avg[:, :, :].rearrange("p k b -> p (k b)"), av, X, ALU.add))
                    st.link(v.tensor_scalar(avg[:, :, :], avg[:, :, :], 1.0 / S, None, ALU.mult))

                    def split(dst, src):
                        hi, lo = dst
                        n = src.shape[1]
                        st.link(v.tensor_copy(hi, src))
                        st.link(v.tensor_tensor(lo, src, hi.bitcast(F32), ALU.subtract))

                    fl = lambda t: tuple(u[:, :, :].rearrange("p k n -> p (k n)") for u in t)
                    for n, name in ((6, "Wr"), (7, "Wv"), (8, "Wo"), (9, "W1"), (10, "W3"), (11, "K"), (12, "V")):
                        v.wait_ge(stg_loaded, n_loaded[n])
                        t = {"K": kexp, "V": vexp}.get(name) or w[name]
                        size = 4096 if name in "KV" else 512
                        src = stg[loads[n][0]][:, 0:size]
                        if name in ("Wo", "W3"):
                            st.link(v.tensor_scalar(src, src, 0.5, None, ALU.mult))
                        split(fl(t), src)
                        v.sem_inc(stg_used, 1)
                    v.wait_ge(kx_done, 1)
                    st.link(v.tensor_copy(stg[1][:, 2048:2560], tp_ps[:, 0:512]))
                    split(fl(w["W2s"]), stg[1][:, 2048:2560])
                    v.sem_inc(w2s_split, 1)
                    v.wait_ge(kx_done, 2)
                    for c, ps in ((0, tp_ps), (1, g_ps)):
                        last = v.tensor_scalar(ctx_k[:, c, :], ps[:, :], col("bk", c), None, ALU.add)
                    last.then_inc(kx_ready, 1)
                    v.wait_ge(kx_done, 3)
                    for c, ps in ((0, tp_ps), (1, g_ps)):
                        v.tensor_scalar(ms_all[:, c, :], ps[:, :], INV_SQRT, None, ALU.mult)
                    v.tensor_scalar(cs_all[:, :], up_ps[0:1, :], INV_SQRT, None, ALU.mult).then_inc(kx_ready, 1)
                    for q in range(B // 4):
                        v.wait_ge(kx_done, 4 + q)
                        for b in range(4):
                            last = v.tensor_tensor(v_all[:, 4 * q + b, :], (out_ps, up_ps)[q % 2][0:S, b * C:(b + 1) * C],
                                                   bv_row[0:S, :], ALU.add)
                        last.then_inc(kx_ready, 1)


                @block.scalar
                def _(s):
                    for k, bias in ((0, "b_d2v"), (1, "b_img")):
                        for c in range(2):
                            for h in range(2):
                                s.wait_ge(lin_done, 4 * k + 2 * c + h + 1)
                                s.activation(act[:, c, h * 512:(h + 1) * 512], (tp_ps, g_ps)[c][:, h * 512:(h + 1) * 512],
                                             ACT.Identity, bias=col(bias, c), scale=oscale[:, k:k + 1]).then_inc(f32_ready, 1)
                    s.wait_ge(kx_ready, 2)
                    s.dma_start(ms_dram.rearrange("b p (k s) -> p k b s", k=KC)[:, 0], ms_all[:, 0, :].rearrange("p (b s) -> p b s", s=S)).then_inc(stored, 16)
                    s.dma_start(ms_dram.rearrange("b p (k s) -> p k b s", k=KC)[:, 1], ms_all[:, 1, :].rearrange("p (b s) -> p b s", s=S)).then_inc(stored, 16)
                    s.dma_start(cs_dram.rearrange("b o s -> o b s"), cs_all[:, :].rearrange("p (b s) -> p b s", s=S)).then_inc(stored, 16)
                    s.wait_ge(kx_ready, 2 + B // 4)
                    s.dma_start(vs_dram.rearrange("b s c -> s b c"), v_all[:, :, :]).then_inc(stored, 16)
                    s.wait_ge(stored, 64)

                @block.tensor
                def _(pe):
                    for k, wt in ((0, wd2v), (1, wimg)):
                        pe.wait_ge(q_ready, k + 1)
                        for c in range(2):
                            for h in range(2):
                                for j in range(2):
                                    m = pe.matmul((tp_ps, g_ps)[c][:, h * 512:(h + 1) * 512], wt[:, j, c * P:(c + 1) * P],
                                                  qa[:, j, h * 512:(h + 1) * 512], start=(j == 0), stop=(j == 1))
                                m.then_inc(lin_done, 1)
                    pe.wait_ge(stg_loaded, n_loaded[13])
                    pe.wait_ge(f32_ready, 8)
                    wst, w2 = stg[1][:, 0:512].rearrange("p (k n) -> p k n", k=2), stg[1][:, 512:1024].rearrange("p (k n) -> p k n", k=2)
                    for c in range(2):
                        for j in range(2):
                            m = pe.matmul(tp_ps[:, c * C:(c + 1) * C], wst[:, j, c * P:(c + 1) * P], w2[:, j, :],
                                          start=(j == 0), stop=(j == 1))
                    m.then_inc(kx_done, 1)
                    pe.wait_ge(stg_loaded, n_loaded[14])
                    pe.wait_ge(w2s_split, 1)
                    wq = stg[0][:, 0:512].rearrange("p (k n) -> p k n", k=2)
                    wk = stg[0][:, 512:1024].rearrange("p (k n) -> p k n", k=2)
                    wv = stg[0][:, 1024:1536].rearrange("p (k n) -> p k n", k=2)
                    for c, ps in ((0, tp_ps), (1, g_ps)):
                        for h in range(2):
                            hs = slice(h * 512, (h + 1) * 512)
                            pe.matmul(ps[:, hs], wk[:, 0, c * P:(c + 1) * P], ctx[:, 0, hs], start=True, stop=False)
                            m = pe.matmul(ps[:, hs], wk[0:D - P, 1, c * P:(c + 1) * P], ctx[0:D - P, 1, hs], start=False, stop=True)
                    m.then_inc(kx_done, 1)
                    pe.wait_ge(kx_ready, 1)
                    for c, ps in ((0, tp_ps), (1, g_ps)):
                        for h in range(2):
                            hs = slice(h * 512, (h + 1) * 512)
                            for j in range(2):
                                pe.matmul(ps[:, hs], wq[:, j, c * P:(c + 1) * P], ctx_k[:, j, hs], start=(j == 0), stop=(j == 1))
                    for h in range(2):
                        hs = slice(h * 512, (h + 1) * 512)
                        for j in range(2):
                            m = pe.matmul(up_ps[0:1, hs], col("bq", j), ctx_k[:, j, hs], start=(j == 0), stop=(j == 1))
                    m.then_inc(kx_done, 1)
                    for q in range(B // 4):
                        pe.wait_ge(kx_ready, max(2, q + 1))
                        for b in range(4):
                            n = 4 * q + b
                            dst = (out_ps, up_ps)[q % 2][0:S, b * C:(b + 1) * C]
                            pe.matmul(dst, ctx[:, 0, n * S:(n + 1) * S], wv[:, 0, :], start=True, stop=False)
                            m = pe.matmul(dst, ctx[0:D - P, 1, n * S:(n + 1) * S], wv[0:D - P, 1, :], start=False, stop=True)
                        m.then_inc(kx_done, 1)
            stack.pop()

        with ExitStack() as scope:
            stack.append(scope)
            x_in = sb("x_in", [P, NT, C])
            x1 = sb("x1", [P, NT, C])
            x2 = sb("x2", [P, NT, C])
            xacc = sb("xacc", [P, NT, C])
            x3 = sb("x3", [P, NT, C])
            text = sb("text", [P, NT, C])
            xn = sb("xn", [P, NT, C])
            xn0 = sb("xn0", [P, NT, C])
            fm = sb("fm", [P, KC, T])
            act_p = (sb("act_hi", [P, KC, T], F32R), sb("act_lo", [P, KC, T], F32R))
            h_p = (sb("h_hi", [P, KC, T], F32R), sb("h_lo", [P, KC, T], F32R))
            t1 = xn
            t2 = sb("t2", [P, KC, T])
            probs = sb("probs", [P, NT // 2, 2, S])
            probs_t = sb("probs_t", [P, NT // 2, P])
            ms, vs, cs = sb("ms", [P, KC, S]), sb("vs", [P, C]), sb("cs", [1, S])
            hr_r = sb("hr_r", [P, 3, T])
            hr_sq = sb("hr_sq", [P, 2, T])
            RING, LAG = 6, 3
            hr_p = (sb("hr_hi", [P, RING, T], F32R), sb("hr_lo", [P, RING, T], F32R))
            stat = sb("stat", [P, NT, 6])
            mean, var, vtmp, rs, nmr = (sb(n, [P, NT]) for n in ("mean", "var", "vtmp", "rs", "nmr"))
            stat0 = sb("stat0", [P, NT, 6])
            mean0, var0, vtmp0, rs0 = (sb(n, [P, NT]) for n in ("mean0", "var0", "vtmp0", "rs0"))
            var1, rs1 = sb("var1", [P, 2, NT]), sb("rs1", [P, 2, NT])
            stat3 = sb("stat3", [P, NT, 6])
            mean3, var3, vtmp3, rs3, nmr3 = (sb(n, [P, NT]) for n in ("mean3", "var3", "vtmp3", "rs3", "nmr3"))
            smax, ssum = sb("smax", [P, NT]), sb("ssum", [P, NT])
            sig = sb("sig", [P, NT, 4])
            bid = sb("bid", [P, NT, 3])
            hot = sb("hot", [P, NT, 3])
            btmp = sb("btmp", [P, NT, 3])
            coef = sb("coef", [P, NT, 3])
            cap4 = sb("cap4", [P, NT, 3])

            x_loaded, small_loaded = sem("x_loaded"), sem("small_loaded")
            x3_stored, text_stored = sem("x3_stored"), sem("text_stored")
            ve_ready, rs_ready, ve3_ready, rs3_ready = (sem(n) for n in ("ve_ready", "rs_ready", "ve3_ready", "rs3_ready"))
            xn_ready, turned, turned_out = sem("xn_ready"), sem("turned"), sem("turned_out")
            scores_done, shifted, exp_done, probs_turned, probs_t_ready = (sem(n) for n in (
                "scores_done", "scores_shifted", "exp_done", "probs_turned", "probs_t_ready"))
            pv_done, x1_ready, x2_ready, xacc_ready = (sem(n) for n in ("pv_done", "x1_ready", "x2_ready", "xacc_ready"))
            hi_ready, lo_ready = sem("act_hi_ready"), sem("act_lo_ready")
            wr_done, w2s_done, wv_done, wo_done = (sem(n) for n in ("wr_done", "w2s_done", "wv_done", "wo_done"))
            t1_ready, t2_ready, g_ready = sem("t1_ready"), sem("t2_ready"), sem("gated_ready")
            h_hi_ready, h_ready = sem("h_hi_ready"), sem("h_ready")
            bids_done, bexp_done, coef_ready = sem("bids_done"), sem("bid_exp_done"), sem("coef_ready")
            up_done, relu_done, sq_done, hr_hi_done, hr_lo_done, evac_done = (sem(n) for n in (
                "up_done", "relu_done", "sq_done", "hr_hi_done", "hr_lo_done", "evac_done"))
            down_done = sem("down_done")
            ve0_ready, rs0_ready, ve1_ready, rs1_ready, xn0_ready, bid_ready = (sem(n) for n in (
                "ve0_ready", "rs0_ready", "ve1_ready", "rs1_ready", "xn0_ready", "bid_ready"))
            nmr_ready, x2ln_ready, nmr3_ready, text_ready, text_seen = (sem(n) for n in (
                "nmr_ready", "x2_ln_ready", "nmr3_ready", "text_ready", "text_seen"))
            v_first, v_front, v_bids, v_tail, a_front = sem("dve_first"), sem("dve_front"), sem("dve_bids"), sem("dve_tail"), sem("act_front")
            K0, KF, KB, KT = 10, 28, 13, 11

            x_v = a["x"].rearrange("b (t p) c -> b p t c", p=P)
            x3_v = x3_dram.rearrange("b (t p) c -> b p t c", p=P)
            text_v = text_dram.rearrange("b (t p) c -> b p t c", p=P)

            def one(ap, n):
                return ap[bass.ds(n, 1)].rearrange("o p t c -> p (o t) c")

            def one2(ap, n):
                return ap[bass.ds(n, 1)].rearrange("o p c -> (o p) c")

            def pipeline(eng, iteration):
                iteration(None, None, None, 0)
                iteration(None, None, 0, 1)
                iteration(None, 0, 1, 2)
                iteration(0, 1, 2, 3)
                with eng.Fori(2, B - 2) as i:
                    iteration(i - 1, i, i + 1, i + 2)
                iteration(B - 3, B - 2, B - 1, None)
                iteration(B - 2, B - 1, None, None)
                iteration(B - 1, None, None, None)

            flat = lambda b: b[:, :, :].rearrange("p a b -> p (a b)")

            with nc.Block() as block:
                @block.sync
                def _(sp):
                    def load(n):
                        after(sp, x1_ready, n)
                        sp.dma_start(x_in[:, :, :], one(x_v, n)).then_inc(x_loaded, 16)
                        after(sp, pv_done, n)
                        sp.dma_start(flat(ms), one2(ms_dram, n)).then_inc(small_loaded, 16)
                        for h in range(2):
                            sp.dma_start(vs[h * S:(h + 1) * S, :], one2(vs_dram, n)).then_inc(small_loaded, 16)
                        sp.dma_start(cs[:, :], one2(cs_dram, n)).then_inc(small_loaded, 16)

                    def store(t):
                        sp.wait_ge(evac_done, 3 * t + 3)
                        sp.dma_start(one(x3_v, t), x3[:, :, :]).then_inc(x3_stored, 16)
                        sp.wait_ge(text_ready, t + 1)
                        sp.dma_start(one(text_v, t), text[:, :, :]).then_inc(text_stored, 16)

                    load(0)
                    load(1)
                    load(2)
                    load(3)
                    with sp.Fori(4, B) as n:
                        store(n - 4)
                        load(n)
                    for t in range(B - 4, B):
                        store(t)
                    sp.wait_ge(x3_stored, 16 * B)
                    sp.wait_ge(text_stored, 16 * B)

                @block.gpsimd
                def _(g):
                    def iteration(t, i, n, m):
                        if i is not None:
                            g.wait_ge(x2_ready, i + 1)
                            after(g, evac_done, 3 * i)
                            g.tensor_tensor(xacc[:, :, :], x1[:, :, :], x2[:, :, :], ALU.add).then_inc(xacc_ready, 1)
                        if n is not None:
                            g.wait_ge(ve1_ready, n + 1)
                            g.tensor_tensor(rs1[:, :, :], var1[:, :, :], neg_half2[:, :, :], ALU.pow).then_inc(rs1_ready, 1)
                        if m is not None:
                            g.wait_ge(ve0_ready, m + 1)
                            g.tensor_tensor(rs0[:, :], var0[:, :], neg_half[:, :], ALU.pow).then_inc(rs0_ready, 1)
                        if t is not None:
                            g.wait_ge(ve3_ready, t + 1)
                            g.tensor_tensor(rs3[:, :], var3[:, :], neg_half[:, :], ALU.pow).then_inc(rs3_ready, 1)
                        if n is not None:
                            g.wait_ge(ve_ready, n + 1)
                            g.tensor_tensor(rs[:, :], var[:, :], neg_half[:, :], ALU.pow).then_inc(rs_ready, 1)
                    pipeline(g, iteration)

                @block.scalar
                def _(s):
                    def chunk(c, i):
                        up = up_ps[:, (c % 2) * T:(c % 2 + 1) * T]
                        hi = hr_p[0][:, c % RING, :]
                        if c < 2:
                            s.wait_ge(sq_done, NCHUNK * i + c + 1)
                            after(s, down_done, NCHUNK * i + c + 1 - RING)
                            s.activation(hi, hr_sq[:, c % 2, :], ACT.Copy).then_inc(hr_hi_done, 1)
                            return
                        s.wait_ge(up_done, NCHUNK * i + c + 1)
                        if c >= 5:
                            s.wait_ge(sq_done, NCHUNK * i + c - 2)
                        s.activation(hr_r[:, c % 3, :], up, ACT.Relu).then_inc(relu_done, 1)
                        s.wait_ge(relu_done, (NCHUNK - 2) * i + c - 1)
                        after(s, down_done, NCHUNK * i + c + 1 - RING)
                        s.activation(hi, hr_r[:, c % 3, :], ACT.Square).then_inc(hr_hi_done, 1)

                    def front(k, n):
                        if k == 0:
                            s.wait_ge(turned, 3 * n + 1)
                            after(s, bids_done, n)
                            after(s, h_ready, n)
                            s.activation(flat(fm), tp_ps[:, :], ACT.Copy).then_inc(turned_out, 1)
                        if k == 2:
                            s.wait_ge(shifted, n + 1)
                            s.activation(probs[:, :, :, :], probs[:, :, :, :], ACT.Exp).then_inc(exp_done, 1)
                        if k == 3:
                            s.wait_ge(probs_turned, n + 1)
                            after(s, pv_done, n)
                            s.activation(flat(probs_t), tp_ps[:, 0:T // 2], ACT.Copy).then_inc(probs_t_ready, 1)
                        if k == 7:
                            s.wait_ge(nmr_ready, n + 1)
                            for t in range(NT):
                                last = s.activation(x2[:, t, :], x1[:, t, :], ACT.Identity, bias=nmr[:, t:t + 1], scale=rs1[:, 0, t:t + 1])
                            last.then_inc(x2ln_ready, 1)
                        if k == 8:
                            s.wait_ge(turned, 3 * n + 2)
                            for c in range(KC):
                                s.activation(fm[:, c, :], tp_ps[:, c * T:(c + 1) * T], ACT.Identity,
                                             bias=col("ln1_b", c), scale=col("ln1_w", c)).then_inc(a_front, 1)
                            s.wait_ge(a_front, 2 * KC * n + KC)
                            after(s, wo_done, n)
                            s.activation(act_p[0][:, :, :], fm[:, :, :], ACT.Copy).then_inc(hi_ready, 1)
                        if k == 10:
                            s.wait_ge(wr_done, n + 1)
                            s.activation(flat(t1), g_ps[:, :], ACT.Tanh, scale=0.5).then_inc(t1_ready, 1)
                            s.wait_ge(w2s_done, n + 1)
                            if not isinstance(n, int) or n > 0:
                                s.wait_ge(sq_done, NCHUNK * n - NCHUNK + 2)
                            s.activation(flat(t2), tp_ps[:, :], ACT.Tanh, scale=0.5).then_inc(t2_ready, 1)
                        if k == 11:
                            s.wait_ge(g_ready, n + 1)
                            s.activation(act_p[0][:, :, :], fm[:, :, :], ACT.Copy).then_inc(hi_ready, 1)
                        if k == 16:
                            s.wait_ge(turned, 3 * n + 3)
                            s.wait_ge(lo_ready, 2 * n + 2)
                            for c in range(KC):
                                s.activation(fm[:, c, :], tp_ps[:, c * T:(c + 1) * T], ACT.Identity,
                                             bias=col("ln2_b", c), scale=col("ln2_w", c)).then_inc(a_front, 1)
                        if k == 17:
                            s.wait_ge(bids_done, n + 1)
                            after(s, bid_ready, n)
                            s.activation(sig[:, :, :], g_ps[:, 0:8 * NT].rearrange("p (t e) -> p t e", e=8)[:, :, 0:4],
                                         ACT.Exp, scale=-1.0).then_inc(bexp_done, 1)
                        if k == NCHUNK:
                            s.wait_ge(a_front, 2 * KC * n + 2 * KC)
                            after(s, up_done, NCHUNK * n)
                            s.activation(h_p[0][:, :, :], fm[:, :, :], ACT.Copy).then_inc(h_hi_ready, 1)

                    def iteration(t, i, n, m):
                        for k in range(NCHUNK):
                            if k == 12 and t is not None:
                                s.wait_ge(nmr3_ready, t + 1)
                                after(s, text_seen, t)
                                after(s, text_stored, 16 * t)
                                for q in range(NT):
                                    last = s.activation(text[:, q, :], x3[:, q, :], ACT.Identity, bias=nmr3[:, q:q + 1], scale=rs3[:, q:q + 1])
                                last.then_inc(text_ready, 1)
                            if n is not None:
                                front(k, n)
                            if i is not None:
                                chunk(k, i)
                        if n is not None:
                            front(NCHUNK, n)
                    pipeline(s, iteration)

                @block.tensor
                def _(pe):
                    def up(c, i):
                        dst = up_ps[:, (c % 2) * T:(c % 2 + 1) * T]
                        if c == 0:
                            pe.wait_ge(h_ready, i + 1)
                        if c in (2, 3):
                            pe.wait_ge(sq_done, NCHUNK * i + c - 1)
                        else:
                            after(pe, relu_done, (NCHUNK - 2) * i + (c - 1 if c < 2 else c - 3))
                        for k in range(KC):
                            if c < 2:
                                st = pair(w["W1"], slice(None), k, slice(c * P, (c + 1) * P))
                            else:
                                e, cc = divmod(c - 2, HC)
                                st = pair(kexp, slice(None), e * KC + k, slice(cc * P, (cc + 1) * P))
                            last = mm3(pe, dst, st, pair(h_p, slice(None), k, slice(None)), k == 0, k == KC - 1)
                        last.then_inc(up_done, 1)

                    def down(c, i):
                        first = c in GROUP_START
                        pe.wait_ge(hr_lo_done, NCHUNK * i + c + 1)
                        if first:
                            after(pe, evac_done, 3 * i + GROUP_START.index(c))
                        for t in range(NT):
                            st = pair(hr_p, slice(None), c % RING, slice(t * P, (t + 1) * P))
                            mv = pair(w["W3"], slice(None), c, slice(None)) if c < 2 else pair(vexp, slice(None), c - 2, slice(None))
                            last = mm3(pe, out_ps[:, t * C:(t + 1) * C], st, mv, first and t % 2 == 0, c in GROUP_END)
                        last.then_inc(down_done, 1)

                    def turn(xn):
                        for c in range(KC):
                            for t in range(NT):
                                last = pe.transpose(tp_ps[:, c * T + t * P:c * T + (t + 1) * P], xn[:, t, c * P:(c + 1) * P], ident[:, :])
                        last.then_inc(turned, 1)

                    def project(dst, name, done):
                        for c in range(KC):
                            for k in range(KC):
                                last = mm3(pe, dst[:, c * T:(c + 1) * T], pair(w[name], slice(None), k, slice(c * P, (c + 1) * P)),
                                           pair(act_p, slice(None), k, slice(None)), k == 0, k == KC - 1)
                        last.then_inc(done, 1)

                    def front(k, n):
                        if k == 1:
                            pe.wait_ge(turned_out, n + 1)
                            pe.wait_ge(small_loaded, 64 * n + 64)
                            after(pe, bid_ready, n)
                            for t in range(NT):
                                dst = g_ps[:, t * S:(t + 1) * S]
                                for c in range(KC):
                                    pe.matmul(dst, fm[:, c, t * P:(t + 1) * P], ms[:, c, :], start=(c == 0), stop=False)
                                last = pe.matmul(dst, ones[:, :], cs[:, :], start=False, stop=True)
                            last.then_inc(scores_done, 1)
                        if k == 2:
                            pe.wait_ge(exp_done, n + 1)
                            for j in range(NT // 2):
                                last = pe.transpose(tp_ps[:, j * P:(j + 1) * P], probs[:, j, :, :].rearrange("p h s -> p (h s)"), ident[:, :])
                            last.then_inc(probs_turned, 1)
                        if k == 4:
                            pe.wait_ge(probs_t_ready, n + 1)
                            for j in range(NT // 2):
                                for h in range(2):
                                    t, half = 2 * h + j, slice(h * S, (h + 1) * S)
                                    last = pe.matmul(g_ps[:, t * C:(t + 1) * C], probs_t[half, j, :], vs[half, :], start=True, stop=True)
                            last.then_inc(pv_done, 1)
                        if k == 7:
                            pe.wait_ge(xn_ready, 2 * n + 1)
                            turn(xn)
                        if k == 9:
                            pe.wait_ge(lo_ready, 2 * n + 1)
                            project(g_ps, "Wr", wr_done)
                            project(tp_ps, "W2s", w2s_done)
                        if k == 10:
                            pe.wait_ge(t1_ready, n + 1)
                            project(g_ps, "Wv", wv_done)
                        if k == 12:
                            pe.wait_ge(lo_ready, 2 * n + 2)
                            pe.wait_ge(t2_ready, n + 1)
                            for t in range(NT):
                                for c in range(KC):
                                    last = mm3(pe, tp_ps[:, t * C:(t + 1) * C], pair(act_p, slice(None), c, slice(t * P, (t + 1) * P)),
                                               pair(w["Wo"], slice(None), c, slice(None)), c == 0, c == KC - 1)
                            last.then_inc(wo_done, 1)
                        if k == 15:
                            pe.wait_ge(xn_ready, 2 * n + 2)
                            turn(xn)
                        if k == 16:
                            pe.wait_ge(a_front, 2 * KC * n + 2 * KC)
                            for t in range(NT):
                                for c in range(KC):
                                    last = pe.matmul(g_ps[:, 8 * t:8 * t + 7], fm[:, c, t * P:(t + 1) * P], wb[:, c, :],
                                                     start=(c == 0), stop=(c == KC - 1))
                            last.then_inc(bids_done, 1)

                    def iteration(t, i, n, m):
                        for k in range(NCHUNK):
                            opens = k - LAG in GROUP_START
                            if t is not None and k < LAG:
                                if k != 1:
                                    down(NCHUNK - LAG + k, t)
                                if k == 0:
                                    down(NCHUNK - LAG + 1, t)
                            if n is not None and k == 0:
                                pe.wait_ge(xn0_ready, n + 1)
                                after(pe, a_front, 2 * KC * n)
                                turn(xn0)
                            if i is not None:
                                if k >= LAG and not opens:
                                    down(k - LAG, i)
                                up(k, i)
                                if opens:
                                    down(k - LAG, i)
                            if n is not None:
                                front(k, n)
                    pipeline(pe, iteration)

                @block.vector
                def _(v):
                    for t in range(NT):
                        v.tensor_copy(cap4[:, t, :], cap)
                    v.memset(tmax[:, :], 0.0)

                    def chunk(c, i):
                        up = up_ps[:, (c % 2) * T:(c % 2 + 1) * T]
                        sq = hr_sq[:, c % 2, :]
                        if c < 2:
                            v.wait_ge(up_done, NCHUNK * i + c + 1)
                            v.wait_ge(t2_ready, i + 1)
                            v.scalar_tensor_tensor(out=sq, in0=t2[:, c, :], scalar=1.0, in1=up, op0=ALU.add, op1=ALU.mult).then_inc(sq_done, 1)
                        else:
                            v.wait_ge(relu_done, (NCHUNK - 2) * i + c - 1)
                            v.tensor_tensor(sq, hr_r[:, c % 3, :], hr_r[:, c % 3, :], ALU.mult).then_inc(sq_done, 1)
                        v.wait_ge(hr_hi_done, NCHUNK * i + c + 1)
                        v.wait_ge(sq_done, NCHUNK * i + c + 1)
                        v.tensor_tensor(hr_p[1][:, c % RING, :], sq, hr_p[0][:, c % RING, :].bitcast(F32), ALU.subtract).then_inc(hr_lo_done, 1)

                    def evacuate(c, i):
                        order = GROUP_END[c]
                        e = GROUP_EXPERT[order]
                        v.wait_ge(down_done, NCHUNK * i + c + 1)
                        v.wait_ge(xacc_ready, i + 1)
                        if order == 0:
                            v.wait_ge(coef_ready, i + 1)
                        else:
                            v.wait_ge(evac_done, 3 * i + order)
                        if order == 2:
                            after(v, x3_stored, 16 * i)
                            after(v, text_ready, i)
                        dst = x3 if order == 2 else xacc
                        for t in range(NT):
                            last = v.scalar_tensor_tensor(out=dst[:, t, :], in0=out_ps[:, t * C:(t + 1) * C], scalar=coef[:, t, e:e + 1],
                                                          in1=xacc[:, t, :], op0=ALU.mult, op1=ALU.add)
                        last.then_inc(evac_done, 1)

                    def first_ln(k, m, st):
                        if k == 9:
                            v.wait_ge(x_loaded, 16 * m + 16)
                            stats(st, x_in, stat0, mean0, var0, vtmp0, ve0_ready)
                        if k == 15:
                            v.wait_ge(rs0_ready, m + 1)
                            after(v, turned, 3 * m - 2)
                            for t in range(NT):
                                last = v.tensor_scalar(xn0[:, t, :], x_in[:, t, :], mean0[:, t:t + 1], rs0[:, t:t + 1], ALU.subtract, ALU.mult)
                            last.then_inc(xn0_ready, 1)

                    def front(k, n, st):
                        if k == 2:
                            v.wait_ge(scores_done, n + 1)
                            sc = g_ps[:, 0:NT * S].rearrange("p (t s) -> p t s", s=S)
                            sc4 = g_ps[:, 0:NT * S].rearrange("p (h j s) -> p h j s", h=2, s=S)
                            mx4 = smax[:, :].rearrange("p (h j) -> p h j", h=2).unsqueeze(3).broadcast_to([P, 2, NT // 2, S])
                            st.link(v.tensor_reduce(smax[:, :], sc, X, ALU.max))
                            after(v, probs_turned, n)
                            v.tensor_tensor(probs[:, :, :, :].rearrange("p j h s -> p h j s"), sc4, mx4, ALU.subtract).then_inc(shifted, 1)
                        if k == 3:
                            v.wait_ge(exp_done, n + 1)
                            st.link(v.tensor_reduce(ssum[:, :].rearrange("p (h j) -> p h j", h=2), probs[:, :, :, :].rearrange("p j h s -> p h j s"), X, ALU.add))
                            st.link(v.reciprocal(ssum[:, :], ssum[:, :]))
                        if k == 5:
                            v.wait_ge(pv_done, n + 1)
                            after(v, xacc_ready, n)
                            for t in range(NT):
                                last = v.scalar_tensor_tensor(out=x1[:, t, :], in0=g_ps[:, t * C:(t + 1) * C], scalar=ssum[:, t:t + 1],
                                                              in1=x_in[:, t, :], op0=ALU.mult, op1=ALU.add)
                            last.then_inc(x1_ready, 1)
                            v.wait_ge(x1_ready, n + 1)
                            after(v, x2ln_ready, n)
                            stats(st, x1, stat, mean, var1[:, 0, :], vtmp, None)
                            st.add(v.tensor_scalar(vtmp[:, :], var1[:, 0, :], EPS, None, ALU.subtract))
                            st.link(v.reciprocal(nmr[:, :], var1[:, 0, :]))
                            st.link(v.tensor_tensor(var1[:, 1, :], vtmp[:, :], nmr[:, :], ALU.mult))
                            v.tensor_scalar(var1[:, 1, :], var1[:, 1, :], EPS, None, ALU.add).then_inc(ve1_ready, 1)
                        if k == 6:
                            v.wait_ge(rs1_ready, n + 1)
                            st.add(v.tensor_tensor(vtmp[:, :], rs1[:, 0, :], rs1[:, 1, :], ALU.mult))
                            v.scalar_tensor_tensor(out=nmr[:, :], in0=mean[:, :], scalar=-1.0, in1=rs1[:, 0, :], op0=ALU.mult, op1=ALU.mult).then_inc(nmr_ready, 1)
                            st.wait()
                            after(v, turned, 3 * n)
                            for t in range(NT):
                                last = v.tensor_scalar(xn[:, t, :], x1[:, t, :], mean[:, t:t + 1], vtmp[:, t:t + 1], ALU.subtract, ALU.mult)
                            last.then_inc(xn_ready, 1)
                        if k == 8:
                            v.wait_ge(hi_ready, 2 * n + 1)
                            v.tensor_tensor(act_p[1][:, :, :], fm[:, :, :], act_p[0][:, :, :].bitcast(F32), ALU.subtract).then_inc(lo_ready, 1)
                        if k == 11:
                            v.wait_ge(wv_done, n + 1)
                            v.scalar_tensor_tensor(out=flat(fm), in0=flat(t1), scalar=1.0, in1=g_ps[:, :], op0=ALU.add, op1=ALU.mult).then_inc(g_ready, 1)
                        if k == 12:
                            v.wait_ge(hi_ready, 2 * n + 2)
                            v.tensor_tensor(act_p[1][:, :, :], fm[:, :, :], act_p[0][:, :, :].bitcast(F32), ALU.subtract).then_inc(lo_ready, 1)
                        if k == 13:
                            v.wait_ge(wo_done, n + 1)
                            v.wait_ge(x2ln_ready, n + 1)
                            v.tensor_tensor(flat(x2), flat(x2), tp_ps[:, :], ALU.add).then_inc(x2_ready, 1)
                            v.wait_ge(x2_ready, n + 1)
                            v.wait_ge(xn_ready, 2 * n + 1)
                            stats(st, x2, stat, mean, var, vtmp, ve_ready)
                        if k == 14:
                            v.wait_ge(rs_ready, n + 1)
                            for t in range(NT):
                                last = v.tensor_scalar(xn[:, t, :], x2[:, t, :], mean[:, t:t + 1], rs[:, t:t + 1], ALU.subtract, ALU.mult)
                            last.then_inc(xn_ready, 1)

                    def bids(n):
                        st = Steps(v, v_bids, KB * n)
                        v.wait_ge(bexp_done, n + 1)
                        after(v, coef_ready, n)
                        conf = sig[:, :, 0:3]
                        ee = lambda m, q: m[:, :, q:q + 1]
                        st.link(v.tensor_scalar(sig[:, :, :], sig[:, :, :], 1.0, None, ALU.add))
                        st.link(v.reciprocal(sig[:, :, :], sig[:, :, :]))
                        st.add(v.tensor_tensor(bid[:, :, :], conf, cap4[:, :, :], ALU.mult))
                        st.link(v.tensor_scalar(btmp[:, :, :], conf, 1e-6, None, ALU.add))
                        st.link(v.tensor_tensor(bid[:, :, :], bid[:, :, :], ee(sig, 3).broadcast_to([P, NT, 3]), ALU.mult))
                        aff = g_ps[:, 0:8 * NT].rearrange("p (t e) -> p t e", e=8)[:, :, 4:7]
                        st.add(v.tensor_tensor(bid[:, :, :], bid[:, :, :], aff, ALU.add))
                        st.link(v.reciprocal(btmp[:, :, :], btmp[:, :, :]))
                        st.add(v.tensor_tensor(btmp[:, :, :], btmp[:, :, :], conf, ALU.mult))
                        st.add(v.tensor_tensor(ee(hot, 0), ee(bid, 1), ee(bid, 2), ALU.max))
                        st.link(v.tensor_tensor(ee(hot, 2), ee(bid, 0), ee(bid, 1), ALU.max))
                        st.add(v.tensor_tensor(ee(hot, 0), ee(bid, 0), ee(hot, 0), ALU.is_ge))
                        st.link(v.tensor_tensor(ee(hot, 2), ee(bid, 2), ee(hot, 2), ALU.is_gt))
                        st.link(v.tensor_tensor(ee(hot, 1), ee(hot, 0), ee(hot, 2), ALU.add))
                        v.tensor_scalar(ee(hot, 1), ee(hot, 1), -1.0, 1.0, ALU.mult, ALU.add).then_inc(bid_ready, 1)
                        assert st.n == KB, st.n

                    def tail(k, t, st):
                        if k == 9:
                            v.wait_ge(evac_done, 3 * t + 3)
                            stats(st, x3, stat3, mean3, var3, vtmp3, ve3_ready)
                        if k == 11:
                            v.wait_ge(rs3_ready, t + 1)
                            v.scalar_tensor_tensor(out=nmr3[:, :], in0=mean3[:, :], scalar=-1.0, in1=rs3[:, :], op0=ALU.mult, op1=ALU.mult).then_inc(nmr3_ready, 1)
                        if k == 14:
                            v.wait_ge(text_ready, t + 1)
                            v.tensor_reduce(tcur[:, :], text[:, :, :], XY, ALU.max, apply_absolute_value=True).then_inc(text_seen, 1)
                            v.wait_ge(text_seen, t + 1)
                            st.link(v.tensor_tensor(tmax[:, :], tmax[:, :], tcur[:, :], ALU.max))

                    def iteration(t, i, n, m):
                        st = Steps(v, v_front, 0 if n is None else KF * n)
                        st0 = Steps(v, v_first, 0 if m is None else K0 * m)
                        stt = Steps(v, v_tail, 0 if t is None else KT * t)
                        for k in range(NCHUNK):
                            if n is not None:
                                front(k, n, st)
                            if k == 2:
                                if t is not None:
                                    evacuate(NCHUNK - 1, t)
                                if i is not None:
                                    v.wait_ge(bid_ready, i + 1)
                                    after(v, evac_done, 3 * i)
                                    v.tensor_tensor(coef[:, :, :], btmp[:, :, :], hot[:, :, :], ALU.mult).then_inc(coef_ready, 1)
                            if i is not None and k - LAG in GROUP_END:
                                evacuate(k - LAG, i)
                            if i is not None:
                                chunk(k, i)
                            if m is not None:
                                first_ln(k, m, st0)
                            if t is not None:
                                tail(k, t, stt)
                        if n is not None:
                            v.wait_ge(h_hi_ready, n + 1)
                            v.tensor_tensor(h_p[1][:, :, :], fm[:, :, :], h_p[0][:, :, :].bitcast(F32), ALU.subtract).then_inc(h_ready, 1)
                            bids(n)
                            assert st.n == KF, st.n
                        assert (t is None or stt.n == KT) and (m is None or st0.n == K0), (stt.n, st0.n)
                    pipeline(v, iteration)
            stack.pop()

        kv_scope.close()
        stack.pop()

        scale_max, scale_steps = sem("scale_max"), sem("scale_steps")
        scales_made = [0, 0]

        def scale_step(which, products, extra=None):
            with nc.Block() as block:
                @block.gpsimd
                def _(g):
                    g.partition_all_reduce(gmax[:, which:which + 1], tmax[:, :], P, RED.max).then_inc(scale_max, 1)

                @block.vector
                def _(v):
                    st = Steps(v, scale_steps, scales_made[1])
                    scales_made[0] += 1
                    v.wait_ge(scale_max, scales_made[0])
                    st.link(v.tensor_scalar(iscale[:, which:which + 1], gmax[:, which:which + 1], 1e-8, 1.0 / 127.0, ALU.max, ALU.mult))
                    st.add(v.reciprocal(inv[:, which:which + 1], iscale[:, which:which + 1]))
                    for o, wk, ak in products:
                        st.add(v.tensor_tensor(oscale[:, o:o + 1], wscale[:, wk:wk + 1], iscale[:, ak:ak + 1], ALU.mult))
                    st.wait()
                    if extra is not None:
                        extra(v, st)
                    scales_made[1] += st.n
                    v.memset(tmax[:, :], 0.0)

        def first_then_loop(eng, body, n):
            body(0)
            with eng.Fori(1, n) as j:
                body(j)

        ff_scope = ExitStack()
        stack.append(ff_scope)
        ff = sb("ff", [P, B, KC, T])
        O_TXT, O_A0, O_A1, O_F1, O_F2 = 2, 3, 4, 5, 6

        scale_step(A_TXT, [(O_TXT, W_TXT, A_TXT), (O_A0, W_A0, A_IMG), (O_A1, W_A1, A_IMG)])
        with ExitStack() as scope:
            stack.append(scope)
            kf = sb("kf", [P, 2, NCTX])
            kt = sb("kt", [P, 2, B // 2, P])
            key_lin, key_ready, key_turned, key_t_ready, key_stored = (sem(n) for n in (
                "key_lin", "key_ready", "key_turned", "key_t_ready", "key_stored"))
            with nc.Block() as block:
                @block.tensor
                def _(pe):
                    for a_ in range(2):
                        for h in range(2):
                            for k in range(KC):
                                last = pe.matmul(psum[a_][:, h * 512:(h + 1) * 512], watt[:, k, a_, :],
                                                 q_img[:, k, h * 512:(h + 1) * 512], start=(k == 0), stop=(k == KC - 1))
                        last.then_inc(key_lin, 1)
                    for a_ in range(2):
                        pe.wait_ge(key_ready, a_ + 1)
                        for j in range(B // 2):
                            last = pe.transpose(psum[2 + a_][:, j * P:(j + 1) * P], kf[:, a_, j * P:(j + 1) * P], ident[:, :])
                        last.then_inc(key_turned, 1)

                @block.scalar
                def _(s):
                    for a_ in range(2):
                        s.wait_ge(key_lin, a_ + 1)
                        s.activation(kf[:, a_, :], psum[a_][:, :], ACT.Identity, bias=col("b_att%d" % a_),
                                     scale=oscale[:, O_A0 + a_:O_A0 + a_ + 1]).then_inc(key_ready, 1)
                    for a_ in range(2):
                        s.wait_ge(key_turned, a_ + 1)
                        s.activation(kt[:, a_, :, :].rearrange("p j f -> p (j f)"), psum[2 + a_][:, :], ACT.Copy).then_inc(key_t_ready, 1)

                @block.sync
                def _(sp):
                    sp.wait_ge(key_ready, 2)
                    for a_ in range(2):
                        sp.dma_start(kv_dram.rearrange("b p (a s) -> a p b s", a=2)[a_],
                                     kf[:, a_, :].rearrange("p (b s) -> p b s", s=S)).then_inc(key_stored, 16)
                    sp.wait_ge(key_t_ready, 2)
                    for a_ in range(2):
                        for h in range(2):
                            sp.dma_start(kvt_dram.rearrange("(j h) s (a f) -> a h s j f", h=2, a=2)[a_, h],
                                         kt[h * S:(h + 1) * S, a_, :, :]).then_inc(key_stored, 16)
                    sp.wait_ge(key_stored, 96)
            stack.pop()

        L = 4
        with ExitStack() as scope:
            stack.append(scope)
            tx = [sb(f"tx{l}", [P, NT, C]) for l in range(L)]
            qt = [sb(f"qt{l}", [P, NT, C], BF16) for l in range(L)]
            qc = [sb(f"qc{l}", [P, KC, T], BF16) for l in range(L)]
            f = [sb(f"f{l}", [P, KC, T]) for l in range(L)]
            fs = [sb(f"fs{l}", [P, T]) for l in range(L)]
            pr = [sb(f"pr{l}", [P, NT // 2, 2, S]) for l in range(L)]
            prt = [sb(f"prt{l}", [P, NT // 2, P]) for l in range(L)]
            kv = [sb(f"kv{l}", [P, 2, S]) for l in range(L)]
            kvt = [sb(f"kvt{l}", [P, 2, P]) for l in range(L)]
            mx = [sb(f"mx{l}", [P, NT]) for l in range(L)]
            sm = [sb(f"sm{l}", [P, NT]) for l in range(L)]
            cur = [sb(f"cur{l}", [P, 1]) for l in range(L)]
            tx_loaded, kv_loaded, f_stored = ([sem(f"att_{n}{l}") for l in range(L)] for n in ("tx_loaded", "kv_loaded", "f_stored"))
            (quant_done, q_turned, qc_ready, txt_done, f_ready, fs_ready, sc_done, sc_shifted,
             e_done, norm_done, e_turned, prt_ready, o_done, f_updated, v_att) = (sem("att_" + n) for n in (
                 "quant_done", "q_turned", "qc_ready", "txt_done", "f_ready", "fs_ready",
                 "scores_done", "shifted", "exp_done", "norm_done", "probs_turned", "probs_t_ready", "o_done",
                 "f_updated", "dve"))
            t_v = text_dram.rearrange("b (t p) c -> b p t c", p=P)
            NJ = B // L
            KV_ = 36

            def bank4(l):
                return psum[l][:, :].rearrange("p (h n) -> p h n", h=2)[:, :, 0:2 * P]

            def tok4(ap):
                return ap.rearrange("p (h n) -> p h n", h=2)

            with nc.Block() as block:
                @block.sync
                def _(sp):
                    def load(j):
                        for l in range(L):
                            n = L * j + l
                            after(sp, quant_done, n + 1 - L)
                            sp.dma_start(tx[l][:, :, :], one(t_v, n)).then_inc(tx_loaded[l], 16)
                        for l in range(L):
                            n = L * j + l
                            after(sp, o_done, 2 * L * j - L + l + 1)
                            sp.dma_start(kv[l][:, :, :].rearrange("p a s -> p (a s)"), one2(kv_dram, n)).then_inc(kv_loaded[l], 16)
                            for h in range(2):
                                sp.dma_start(kvt[l][h * S:(h + 1) * S, :, :].rearrange("p a f -> p (a f)"), one2(kvt_dram, n)).then_inc(kv_loaded[l], 16)

                    def store(j):
                        for l in range(L):
                            n = L * j + l
                            sp.wait_ge(f_updated, 2 * L * j + L + l + 1)
                            sp.dma_start(ff[:, bass.ds(n, 1), :, :].rearrange("p o k t -> p (o k t)"),
                                         f[l][:, :, :].rearrange("p k t -> p (k t)")).then_inc(f_stored[l], 16)
                    load(0)
                    load(1)
                    store(0)
                    with sp.Fori(1, NJ - 1) as j:
                        load(j + 1)
                        store(j)
                    store(NJ - 1)
                    for l in range(L):
                        sp.wait_ge(f_stored[l], 16 * NJ)

                @block.gpsimd
                def _(g):
                    def body(j):
                        for a_ in range(2):
                            for l in range(L):
                                if a_ == 0:
                                    g.wait_ge(f_ready, L * j + l + 1)
                                    after(g, sc_done, 2 * L * j - L + l + 1)
                                else:
                                    g.wait_ge(f_updated, 2 * L * j + l + 1)
                                g.tensor_tensor(fs[l][:, :], f[l][:, 0, :], f[l][:, 1, :], ALU.add).then_inc(fs_ready, 1)
                    first_then_loop(g, body, NJ)

                @block.scalar
                def _(s):
                    def body(j):
                        for l in range(L):
                            n = L * j + l
                            s.wait_ge(q_turned, n + 1)
                            after(s, txt_done, n + 1 - L)
                            s.activation(qc[l][:, :, :].rearrange("p k t -> p (k t)"), psum[l][:, 0:T].bitcast(BF16), ACT.Copy).then_inc(qc_ready, 1)
                        for l in range(L):
                            n = L * j + l
                            s.wait_ge(txt_done, n + 1)
                            after(s, f_stored[l], 16 * j)
                            for c in range(KC):
                                last = s.activation(f[l][:, c, :], psum[l][:, c * T:(c + 1) * T], ACT.Identity, bias=col("b_txt", c),
                                                    scale=oscale[:, O_TXT:O_TXT + 1])
                            last.then_inc(f_ready, 1)
                        for a_ in range(2):
                            for l in range(L):
                                s.wait_ge(sc_shifted, 2 * L * j + L * a_ + l + 1)
                                s.activation(pr[l][:, :, :, :], pr[l][:, :, :, :], ACT.Exp, scale=INV_SQRT).then_inc(e_done, 1)
                            for l in range(L):
                                u = 2 * L * j + L * a_ + l
                                s.wait_ge(e_turned, u + 1)
                                after(s, o_done, u + 1 - L)
                                s.activation(prt[l][:, :, :].rearrange("p j t -> p (j t)"), psum[l][:, 0:2 * P], ACT.Copy).then_inc(prt_ready, 1)
                    first_then_loop(s, body, NJ)

                @block.tensor
                def _(pe):
                    def body(j):
                        for l in range(L):
                            n = L * j + l
                            pe.wait_ge(quant_done, n + 1)
                            after(pe, f_updated, 2 * L * j - L + l + 1)
                            qp = psum[l][:, 0:T].bitcast(BF16)
                            for c in range(KC):
                                for t in range(NT):
                                    last = pe.transpose(qp[:, c * T + t * P:c * T + (t + 1) * P], qt[l][:, t, c * P:(c + 1) * P], ident_b[:, :])
                            last.then_inc(q_turned, 1)
                        for l in range(L):
                            pe.wait_ge(qc_ready, L * j + l + 1)
                            for c in range(KC):
                                for k in range(KC):
                                    last = pe.matmul(psum[l][:, c * T:(c + 1) * T], wtxt[:, k, c * P:(c + 1) * P], qc[l][:, k, :],
                                                     start=(k == 0), stop=(k == KC - 1))
                            last.then_inc(txt_done, 1)
                        for a_ in range(2):
                            for l in range(L):
                                n, u = L * j + l, 2 * L * j + L * a_ + l
                                if a_ == 0:
                                    pe.wait_ge(kv_loaded[l], 48 * j + 48)
                                pe.wait_ge(fs_ready, u + 1)
                                for t in range(NT):
                                    last = pe.matmul(psum[l][:, t * S:(t + 1) * S], fs[l][:, t * P:(t + 1) * P], kv[l][:, a_, :], start=True, stop=True)
                                last.then_inc(sc_done, 1)
                            for l in range(L):
                                u = 2 * L * j + L * a_ + l
                                pe.wait_ge(norm_done, u + 1)
                                for q in range(NT // 2):
                                    last = pe.transpose(psum[l][:, q * P:(q + 1) * P], pr[l][:, q, :, :].rearrange("p h s -> p (h s)"), ident[:, :])
                                last.then_inc(e_turned, 1)
                            for l in range(L):
                                u = 2 * L * j + L * a_ + l
                                pe.wait_ge(prt_ready, u + 1)
                                for q in range(NT // 2):
                                    for h in range(2):
                                        half = slice(h * S, (h + 1) * S)
                                        last = pe.matmul(psum[l][:, h * T + q * P:h * T + (q + 1) * P], kvt[l][half, a_, :],
                                                         prt[l][half, q, :], start=True, stop=True)
                                last.then_inc(o_done, 1)
                    first_then_loop(pe, body, NJ)

                @block.vector
                def _(v):
                    def body(j):
                        st = Steps(v, v_att, KV_ * j)
                        for l in range(L):
                            v.wait_ge(tx_loaded[l], 16 * j + 16)
                            st.add(v.tensor_scalar(tx[l][:, :, :], tx[l][:, :, :], inv[:, A_TXT:A_TXT + 1], ROUND, ALU.mult, ALU.add))
                        for l in range(L):
                            n = L * j + l
                            v.wait_ge(v_att, KV_ * j + l + 1)
                            after(v, q_turned, n + 1 - L)
                            v.tensor_scalar(qt[l][:, :, :], tx[l][:, :, :], ROUND, None, ALU.subtract).then_inc(quant_done, 1)
                        for a_ in range(2):
                            for l in range(L):
                                v.wait_ge(sc_done, 2 * L * j + L * a_ + l + 1)
                                st.add(v.tensor_reduce(mx[l][:, :], psum[l][:, 0:NT * S].rearrange("p (t s) -> p t s", s=S), X, ALU.max))
                            st.wait()
                            for l in range(L):
                                after(v, e_turned, 2 * L * j + L * a_ + l + 1 - L)
                                v.tensor_tensor(pr[l][:, :, :, :].rearrange("p j h s -> p h j s"),
                                                psum[l][:, 0:NT * S].rearrange("p (h j s) -> p h j s", h=2, s=S),
                                                mx[l][:, :].rearrange("p (h j) -> p h j", h=2).unsqueeze(3).broadcast_to([P, 2, NT // 2, S]),
                                                ALU.subtract).then_inc(sc_shifted, 1)
                            for l in range(L):
                                v.wait_ge(e_done, 2 * L * j + L * a_ + l + 1)
                                st.add(v.tensor_reduce(sm[l][:, :].rearrange("p (j h) -> p j h", h=2), pr[l][:, :, :, :], X, ALU.add))
                            st.wait()
                            for l in range(L):
                                st.add(v.reciprocal(sm[l][:, :], sm[l][:, :]))
                            st.wait()
                            for l in range(L):
                                v.tensor_tensor(pr[l][:, :, :, :], pr[l][:, :, :, :],
                                                sm[l][:, :].rearrange("p (j h) -> p j h", h=2).unsqueeze(3).broadcast_to([P, NT // 2, 2, S]),
                                                ALU.mult).then_inc(norm_done, 1)
                            for l in range(L):
                                v.wait_ge(o_done, 2 * L * j + L * a_ + l + 1)
                                for c in range(KC):
                                    last = v.scalar_tensor_tensor(out=tok4(f[l][:, c, :]), in0=bank4(l), scalar=0.1, in1=tok4(f[l][:, c, :]),
                                                                  op0=ALU.mult, op1=ALU.add)
                                last.then_inc(f_updated, 1)
                        for l in range(L):
                            v.wait_ge(f_updated, 2 * L * j + L + l + 1)
                            st.add(v.tensor_reduce(cur[l][:, :], f[l][:, :, :], XY, ALU.max, apply_absolute_value=True))
                        st.wait()
                        for l in range(L):
                            st.link(v.tensor_tensor(tmax[:, :], tmax[:, :], cur[l][:, :], ALU.max))
                        assert st.n == KV_, st.n
                    first_then_loop(v, body, NJ)
            stack.pop()

        qf = sb("qf", [P, B, KC, T], BF16)
        lw = {n: (sb(n + "_hi", [P, KC, C], F32R), sb(n + "_lo", [P, KC, C], F32R)) for n in ("rT", "kT", "vT")}
        qavg = sb("qavg", [P, KC, B], BF16)
        acc_avg = sb("acc_avg", [P, HC, B])
        hmax8, hcur = sb("hmax8", [P, HC]), sb("hcur", [P, HC])
        avg_max, avg_join = sem("avg_max"), sem("avg_join")
        with nc.Block() as block:
            @block.vector
            def _(v):
                v.tensor_reduce(tcur[:, :], avg[:, :, :], XY, ALU.max, apply_absolute_value=True).then_inc(avg_max, 1)
                v.wait_ge(avg_max, 1)
                v.tensor_tensor(tmax[:, :], tmax[:, :], tcur[:, :], ALU.max).then_inc(avg_join, 1)
        scale_step(A_CAT, [(O_F1, W_F1, A_CAT)])
        qy = sb("qy", [P, KC * T])
        with ExitStack() as scope:
            stack.append(scope)
            lstg = sb("lstg", [P, 3, KC, C])
            l_loaded, qavg_ready, acc_done, acc_ready, v_hid = (sem(n) for n in ("l1_loaded", "qavg_ready", "acc_avg_done", "acc_avg_ready", "dve_hidden"))
            hq_done, h_done, h_red = sem("hid_quant"), sem("hid_f1"), sem("hid_reduced")
            KH = 3
            with nc.Block() as block:
                @block.sync
                def _(sp):
                    for k, name in enumerate(("rT", "kT", "vT")):
                        sp.dma_start(lstg[:, k, :, :], a[name].rearrange("(k p) n -> p k n", p=P)).then_inc(l_loaded, 16)

                @block.tensor
                def _(pe):
                    pe.wait_ge(qavg_ready, 1)
                    for c in range(HC):
                        for k in range(KC):
                            last = pe.matmul(psum[3][:, c * B:(c + 1) * B], wf1[:, KC + k, c * P:(c + 1) * P], qavg[:, k, :],
                                             start=(k == 0), stop=(k == KC - 1))
                    last.then_inc(acc_done, 1)
                    pe.wait_ge(acc_ready, 1)

                    def body(n):
                        for q in range(HC // 2):
                            if q == 0:
                                pe.wait_ge(hq_done, n + 1)
                            after(pe, h_red, 4 * n + q - 3)
                            for c in (2 * q, 2 * q + 1):
                                for k in range(KC):
                                    last = pe.matmul(psum[q][:, (c % 2) * T:(c % 2 + 1) * T], wf1[:, k, c * P:(c + 1) * P],
                                                     qf[:, bass.ds(n, 1), k, :].rearrange("p o t -> p (o t)"), start=(k == 0), stop=(k == KC - 1))
                            last.then_inc(h_done, 1)
                    first_then_loop(pe, body, B)

                @block.vector
                def _(v):
                    st = Steps(v, v_hid)
                    st.link(v.tensor_scalar(lstg_avg := qy[:, 0:KC * B].rearrange("p (k b) -> p k b", k=KC), avg[:, :, :], inv[:, A_CAT:A_CAT + 1], ROUND, ALU.mult, ALU.add))
                    v.tensor_scalar(qavg[:, :, :], lstg_avg, ROUND, None, ALU.subtract).then_inc(qavg_ready, 1)
                    st.add(v.memset(hmax8[:, :], -1e30))
                    v.wait_ge(l_loaded, 48)
                    for k, name in enumerate(("rT", "kT", "vT")):
                        hi, lo = lw[name]
                        if name == "vT":
                            st.link(v.tensor_scalar(lstg[:, k, :, :], lstg[:, k, :, :], 0.5, None, ALU.mult))
                        st.link(v.tensor_copy(hi[:, :, :], lstg[:, k, :, :]))
                        st.add(v.tensor_tensor(lo[:, :, :], lstg[:, k, :, :], hi[:, :, :].bitcast(F32), ALU.subtract))
                    v.wait_ge(acc_done, 1)
                    v.tensor_copy(acc_avg[:, :, :].rearrange("p c b -> p (c b)"), psum[3][:, 0:HC * B]).then_inc(acc_ready, 1)
                    v.wait_ge(acc_ready, 1)
                    base = st.n

                    def quant(n, at):
                        sel = lambda m: m[:, bass.ds(n, 1), :, :].rearrange("p o k t -> p (o k t)")
                        after(v, hq_done, n)
                        v.tensor_scalar(qy[:, :], sel(ff), inv[:, A_CAT:A_CAT + 1], ROUND, ALU.mult, ALU.add).then_inc(v_hid, 1)
                        v.wait_ge(v_hid, at + 1)
                        v.tensor_scalar(sel(qf), qy[:, :], ROUND, None, ALU.subtract).then_inc(hq_done, 1)

                    def body(n, ahead):
                        at = base + 1 + KH * n
                        if ahead:
                            quant(n + 1, at)
                        else:
                            v.wait_ge(v_hid, at)
                        for q in range(HC // 2):
                            v.wait_ge(h_done, 4 * n + q + 1)
                            v.tensor_reduce(hcur[:, 2 * q:2 * q + 2], psum[q][:, :].rearrange("p (c t) -> p c t", c=2), X, ALU.max).then_inc(h_red, 1)
                        v.wait_ge(h_red, 4 * n + 4)
                        at = at + (1 if ahead else 0)
                        v.tensor_tensor(hcur[:, :], hcur[:, :], acc_avg[:, :, bass.ds(n, 1)].rearrange("p c o -> p (c o)"), ALU.add).then_inc(v_hid, 1)
                        v.wait_ge(v_hid, at + 1)
                        v.tensor_tensor(hmax8[:, :], hmax8[:, :], hcur[:, :], ALU.max).then_inc(v_hid, 1)
                    quant(0, base)
                    body(0, True)
                    with v.Fori(1, B - 1) as n:
                        body(n, True)
                    body(B - 1, False)
                    end = base + 1 + KH * B - 1
                    v.wait_ge(v_hid, end)
                    st2 = Steps(v, v_hid, end)
                    st2.link(v.tensor_scalar(hmax8[:, :], hmax8[:, :], oscale[:, O_F1:O_F1 + 1], None, ALU.mult))
                    st2.link(v.tensor_tensor(hmax8[:, :], hmax8[:, :], cols[:, COLS["b_f1"][0]:COLS["b_f1"][0] + HC], ALU.add))
                    st2.link(v.tensor_reduce(tmax[:, :], hmax8[:, :], X, ALU.max))
                    st2.link(v.tensor_scalar(tmax[:, :], tmax[:, :], 0.0, None, ALU.max))
            stack.pop()

        hb = sb("hb", [P, HC, B])
        s1h = sb("s1h", [P, 1])

        def hidden_bias(v, st):
            st.link(v.tensor_scalar(hb[:, :, :], acc_avg[:, :, :], oscale[:, O_F1:O_F1 + 1], None, ALU.mult))
            st.add(v.tensor_tensor(s1h[:, :], oscale[:, O_F1:O_F1 + 1], inv[:, A_H:A_H + 1], ALU.mult))
            st.link(v.tensor_tensor(hb[:, :, :], hb[:, :, :],
                                    cols[:, COLS["b_f1"][0]:COLS["b_f1"][0] + HC].unsqueeze(2).broadcast_to([P, HC, B]), ALU.add))
            st.link(v.tensor_scalar(hb[:, :, :], hb[:, :, :], inv[:, A_H:A_H + 1], None, ALU.mult))

        scale_step(A_H, [(O_F2, W_F2, A_H)], hidden_bias)
        DEPTH = 4
        with ExitStack() as scope:
            space = ff[:, :, :, :].rearrange("p b k t -> p (b k t)")
            used = [0]

            def view(*shape):
                n = 1
                for q in shape:
                    n *= q
                at = used[0]
                used[0] += n
                assert used[0] <= B * KC * T
                flat_ = space[:, at:at + n]
                if len(shape) == 1:
                    return flat_
                return flat_.rearrange("p (a b) -> p a b", a=shape[0])

            stack.append(scope)
            xt = [view(NT, C) for _ in range(DEPTH)]
            xnn = view(NT, C)
            zd = view(KC, T)
            xr, xk = view(KC, T), view(KC, T)
            tr = [view(NT * C) for _ in range(2)]
            kr, ks = view(KC, T), view(KC, T)
            hr2 = view(2, T)
            yo = view(NT, C)
            zz = sb("zz", [P, KC, T + 1])
            hq = [sb(f"hq{l}", [P, HC, T], BF16) for l in range(2)]
            pr_, pk, pv = ((sb(f"{q}_hi", [P, KC, T], F32R), sb(f"{q}_lo", [P, KC, T], F32R)) for q in ("mix_r", "mix_k", "k_sq"))
            hbs = [sb(f"hbs{l}", [P, HC]) for l in range(2)]
            st6 = sb("st6", [P, NT, 6])
            me, va, vt, rr, nm = (sb("fin_" + q, [P, NT]) for q in ("mean", "var", "vtmp", "rs", "nmr"))
            fl_ = lambda ap: ap.rearrange("p a b -> p (a b)")
            xt_loaded, y_stored = ([sem(f"fin_{q}{l}") for l in range(DEPTH)] for q in ("x_loaded", "y_stored"))
            (hbs_ready, f1_done, hrelu_done, hround_done, f2_done, xb_ready, x4_ready, ve4, rs4, nm_ready, xn4, z_turned, z_ready,
             zd_ready, mixr_done, mixk_done, r_hi, r_lo, k_hi, k_lo, v_hi, v_lo, r_done, k_done, tr_ready, kr_ready, ksq_ready,
             v_done, y_ready, yo_done, v_fin) = (sem("fin_" + q) for q in (
                 "hbs_ready", "f1_done", "relu_done", "round_done", "f2_done", "xb_ready", "x4_ready", "ve", "rs", "nmr_ready",
                 "xn", "z_turned", "z_ready", "zd_ready", "mixr_done", "mixk_done", "mixr_hi", "mixr_lo", "mixk_hi", "mixk_lo",
                 "ksq_hi", "ksq_lo", "r_done", "k_done", "tanh_ready", "krelu_ready", "ksq_ready", "v_done", "y_ready",
                 "yo_done", "dve"))
            out_v = out.rearrange("b (t p) c -> b p t c", p=P)
            x3r_v = x3_dram.rearrange("b (t p) c -> b p t c", p=P)
            KF3 = 10
            f1_ps, f2k_ps, v_ps, rz_ps = psum

            def pipeline3(eng, iteration):
                for i in range(DEPTH):
                    iteration(i, i, 0)
                with eng.Fori(1, B // DEPTH) as j:
                    for l in range(DEPTH):
                        iteration(DEPTH * j + l, l, j)
                for i in range(B, B + 3):
                    iteration(i, i % DEPTH, B // DEPTH)

            def batch(i, l, d, piece):
                b = i - d if d else i
                if not isinstance(b, int) or 0 <= b < B:
                    piece(b, (l - d) % DEPTH)

            with nc.Block() as block:
                @block.sync
                def _(sp):
                    def load(b, l):
                        sp.dma_start(xt[l], one(x3r_v, b)).then_inc(xt_loaded[l], 16)

                    def store(b, l):
                        sp.wait_ge(y_ready, b + 1)
                        sp.dma_start(one(out_v, b), xt[l]).then_inc(y_stored[l], 16)

                    def round_(j, more=True):
                        for l in range(DEPTH):
                            store(DEPTH * j + l, l)
                            if more:
                                sp.wait_ge(y_stored[l], 16 * j + 16)
                                load(DEPTH * j + l + DEPTH, l)
                    for l in range(DEPTH):
                        load(l, l)
                    round_(0)
                    with sp.Fori(1, B // DEPTH - 1) as j:
                        round_(j)
                    round_(B // DEPTH - 1, more=False)
                    for l in range(DEPTH):
                        sp.wait_ge(y_stored[l], 16 * (B // DEPTH))

                @block.gpsimd
                def _(g):
                    def iteration(i, l, j):
                        def z_steps(b, _):
                            g.wait_ge(z_ready, b + 1)
                            g.tensor_tensor(zd, zz[:, :, 1:T + 1], zz[:, :, 0:T], ALU.subtract).then_inc(zd_ready, 1)

                        def rstd(b, _):
                            g.wait_ge(ve4, b + 1)
                            g.tensor_tensor(rr[:, :], va[:, :], neg_half[:, :], ALU.pow).then_inc(rs4, 1)

                        def bias(b, l_):
                            g.wait_ge(xt_loaded[l_], 16 * j + 16)
                            g.tensor_tensor(xt[l_], xt[l_], bf2_row.unsqueeze(1).broadcast_to([P, NT, C]), ALU.add).then_inc(xb_ready, 1)

                        def residual(b, l_):
                            g.wait_ge(yo_done, b + 1)
                            g.tensor_tensor(xt[l_], yo, xt[l_], ALU.add).then_inc(y_ready, 1)
                        batch(i, l, 2, z_steps)
                        batch(i, l, 1, rstd)
                        batch(i, l, 0, bias)
                        batch(i, l, 3, residual)
                    pipeline3(g, iteration)

                @block.scalar
                def _(s):
                    def iteration(i, l, _):
                        def relu(c0):
                            def piece(b, l_):
                                for c in (c0, c0 + 1):
                                    s.wait_ge(f1_done, HC * b + c + 1)
                                    if c == 0:
                                        s.wait_ge(hbs_ready, b + 1)
                                    after(s, hround_done, HC * b + c - 1)
                                    s.activation(hr2[:, c % 2, :], f1_ps[:, (c % 2) * T:(c % 2 + 1) * T], ACT.Relu,
                                                 bias=hbs[l_ % 2][:, c:c + 1], scale=s1h[:, :]).then_inc(hrelu_done, 1)
                            return piece

                        def z_out(b, _):
                            s.wait_ge(z_turned, b + 1)
                            after(s, mixk_done, b)
                            s.activation(zz[:, :, 1:T + 1], rz_ps[:, :].rearrange("p (k t) -> p k t", k=KC), ACT.Copy).then_inc(z_ready, 1)

                        def r_high(b, _):
                            s.wait_ge(mixr_done, b + 1)
                            after(s, r_done, b)
                            s.activation(pr_[0][:, :, :], xr, ACT.Copy).then_inc(r_hi, 1)

                        def k_high(b, _):
                            s.wait_ge(mixk_done, b + 1)
                            after(s, k_done, b)
                            s.activation(pk[0][:, :, :], xk, ACT.Copy).then_inc(k_hi, 1)

                        def ln(b, l_):
                            s.wait_ge(nm_ready, b + 1)
                            after(s, z_turned, b)
                            for t in range(NT):
                                last = s.activation(xnn[:, t, :], xt[l_][:, t, :], ACT.Identity, bias=nm[:, t:t + 1], scale=rr[:, t:t + 1])
                            last.then_inc(xn4, 1)

                        def tanh(b, l_):
                            s.wait_ge(r_done, b + 1)
                            after(s, yo_done, b - 1)
                            s.activation(tr[l_ % 2], rz_ps[:, :], ACT.Tanh, scale=0.5).then_inc(tr_ready, 1)

                        def key(b, _):
                            s.wait_ge(k_done, b + 1)
                            after(s, ksq_ready, b)
                            s.activation(fl_(kr), f2k_ps[:, :], ACT.Relu).then_inc(kr_ready, 1)
                            s.wait_ge(kr_ready, b + 1)
                            after(s, v_done, b)
                            s.activation(pv[0][:, :, :], kr, ACT.Square).then_inc(v_hi, 1)
                        batch(i, l, 2, z_out)
                        batch(i, l, 0, relu(0))
                        batch(i, l, 2, r_high)
                        batch(i, l, 2, k_high)
                        batch(i, l, 0, relu(2))
                        batch(i, l, 1, ln)
                        batch(i, l, 2, tanh)
                        batch(i, l, 0, relu(4))
                        batch(i, l, 2, key)
                        batch(i, l, 0, relu(6))
                    pipeline3(s, iteration)

                @block.tensor
                def _(pe):
                    sl = slice(None)

                    def iteration(i, l, _):
                        def f1(c0):
                            def piece(b, _):
                                for c in (c0, c0 + 1):
                                    after(pe, hrelu_done, HC * b + c - 1)
                                    for k in range(KC):
                                        last = pe.matmul(f1_ps[:, (c % 2) * T:(c % 2 + 1) * T], wf1[:, k, c * P:(c + 1) * P],
                                                         qf[:, bass.ds(b, 1), k, :].rearrange("p o t -> p (o t)"), start=(k == 0), stop=(k == KC - 1))
                                    last.then_inc(f1_done, 1)
                            return piece

                        def f2(b, l_):
                            pe.wait_ge(hround_done, HC * b + HC)
                            after(pe, kr_ready, b - 1)
                            for t in range(NT):
                                for c in range(HC):
                                    last = pe.matmul(f2k_ps[:, t * C:(t + 1) * C], hq[l_ % 2][:, c, t * P:(t + 1) * P], wf2[:, c, :],
                                                     start=(c == 0), stop=(c == HC - 1))
                            last.then_inc(f2_done, 1)

                        def turn(b, _):
                            pe.wait_ge(xn4, b + 1)
                            after(pe, tr_ready, b)
                            for c in range(KC):
                                for t in range(NT):
                                    last = pe.transpose(rz_ps[:, c * T + t * P:c * T + (t + 1) * P], xnn[:, t, c * P:(c + 1) * P], ident[:, :])
                            last.then_inc(z_turned, 1)

                        def by_token(dst, act_, name, done):
                            for t in range(NT):
                                for k in range(KC):
                                    last = mm3(pe, dst[:, t * C:(t + 1) * C], pair(act_, sl, k, slice(t * P, (t + 1) * P)),
                                               pair(lw[name], sl, k, sl), k == 0, k == KC - 1)
                            last.then_inc(done, 1)

                        def receptance(b, _):
                            pe.wait_ge(r_lo, b + 1)
                            by_token(rz_ps, pr_, "rT", r_done)

                        def key(b, _):
                            pe.wait_ge(k_lo, b + 1)
                            if not isinstance(b, int) or b + 1 < B:
                                pe.wait_ge(x4_ready, b + 2)
                            for c in range(KC):
                                for k in range(KC):
                                    last = mm3(pe, f2k_ps[:, c * T:(c + 1) * T], pair(lw["kT"], sl, k, slice(c * P, (c + 1) * P)),
                                               pair(pk, sl, k, sl), k == 0, k == KC - 1)
                            last.then_inc(k_done, 1)

                        def value(b, _):
                            pe.wait_ge(v_lo, b + 1)
                            after(pe, yo_done, b)
                            by_token(v_ps, pv, "vT", v_done)
                        batch(i, l, 0, f1(0))
                        batch(i, l, 1, f2)
                        batch(i, l, 3, value)
                        batch(i, l, 0, f1(2))
                        batch(i, l, 2, receptance)
                        batch(i, l, 0, f1(4))
                        batch(i, l, 2, key)
                        batch(i, l, 0, f1(6))
                        batch(i, l, 1, turn)
                    pipeline3(pe, iteration)

                @block.vector
                def _(v):
                    v.memset(zz[:, :, 0:1], 0.0)

                    def iteration(i, l, _):
                        def bias(b, l_):
                            after(v, hrelu_done, HC * (b - 1))
                            v.tensor_scalar(hbs[l_ % 2][:, :], hb[:, :, bass.ds(b, 1)].rearrange("p c o -> p (c o)"), 1.0, None, ALU.mult).then_inc(hbs_ready, 1)

                        def quantise(c0):
                            def piece(b, l_):
                                for c in (c0, c0 + 1):
                                    v.wait_ge(hrelu_done, HC * b + c + 1)
                                    if c == 0:
                                        after(v, f2_done, b - 1)
                                    v.tensor_scalar(hq[l_ % 2][:, c, :], hr2[:, c % 2, :], ROUND, ROUND, ALU.add, ALU.subtract).then_inc(hround_done, 1)
                            return piece

                        def mix(dst, mu, done):
                            for c in range(KC):
                                last = v.scalar_tensor_tensor(out=dst[:, c, :], in0=zd[:, c, :], scalar=col(mu, c), in1=zz[:, c, 0:T],
                                                              op0=ALU.mult, op1=ALU.add)
                            last.then_inc(done, 1)

                        def mix_r(b, _):
                            v.wait_ge(zd_ready, b + 1)
                            mix(xr, "mu_r", mixr_done)

                        def mix_k(b, _):
                            mix(xk, "mu_k", mixk_done)

                        def low(dst, src, hi_sem, lo_sem):
                            def piece(b, _):
                                v.wait_ge(hi_sem, b + 1)
                                if src is ks:
                                    v.wait_ge(ksq_ready, b + 1)
                                v.tensor_tensor(dst[1][:, :, :], src, dst[0][:, :, :].bitcast(F32), ALU.subtract).then_inc(lo_sem, 1)
                            return piece

                        def x4(b, l_):
                            v.wait_ge(f2_done, b + 1)
                            v.wait_ge(xb_ready, b + 1)
                            v.scalar_tensor_tensor(out=fl_(xt[l_]), in0=f2k_ps[:, :], scalar=oscale[:, O_F2:O_F2 + 1], in1=fl_(xt[l_]),
                                                   op0=ALU.mult, op1=ALU.add).then_inc(x4_ready, 1)

                        def moments(b, l_):
                            v.wait_ge(x4_ready, b + 1)
                            after(v, xn4, b)
                            st = Steps(v, v_fin, KF3 * b)
                            stats(st, xt[l_], st6, me, va, vt, ve4)
                            assert st.n == KF3, st.n

                        def scaled_mean(b, _):
                            v.wait_ge(rs4, b + 1)
                            v.scalar_tensor_tensor(out=nm[:, :], in0=me[:, :], scalar=-1.0, in1=rr[:, :], op0=ALU.mult, op1=ALU.mult).then_inc(nm_ready, 1)

                        def gate(b, l_):
                            v.wait_ge(v_done, b + 1)
                            v.wait_ge(tr_ready, b + 1)
                            after(v, y_ready, b)
                            v.scalar_tensor_tensor(out=fl_(yo), in0=tr[l_ % 2], scalar=1.0, in1=v_ps[:, :], op0=ALU.add, op1=ALU.mult).then_inc(yo_done, 1)

                        def square(b, _):
                            v.wait_ge(kr_ready, b + 1)
                            v.tensor_tensor(ks, kr, kr, ALU.mult).then_inc(ksq_ready, 1)
                        batch(i, l, 0, bias)
                        batch(i, l, 0, quantise(0))
                        batch(i, l, 2, mix_r)
                        batch(i, l, 1, x4)
                        batch(i, l, 2, low(pr_, xr, r_hi, r_lo))
                        batch(i, l, 2, mix_k)
                        batch(i, l, 1, moments)
                        batch(i, l, 2, low(pk, xk, k_hi, k_lo))
                        batch(i, l, 1, scaled_mean)
                        batch(i, l, 0, quantise(2))
                        batch(i, l, 3, gate)
                        batch(i, l, 0, quantise(4))
                        batch(i, l, 2, square)
                        batch(i, l, 0, quantise(6))
                        batch(i, l, 2, low(pv, ks, v_hi, v_lo))
                    pipeline3(v, iteration)
            stack.pop()
        ff_scope.close()
        stack.pop()
    return nc


def kernel(**inputs):
    import numpy as np
    import concourse.bacc as bacc
    from concourse.bass_utils import run_bass_kernel_spmd

    g = lambda name: np.asarray(inputs[name])
    c = np.ascontiguousarray
    chunks = lambda name: g(name).reshape(-1, P)
    arrays = {
        "x": c(g("x")),
        "ctxT": c(g("ctx_768").reshape(NCTX, D).T),
        "WkT": c(g("L0_xattn_Wk").T), "WvT": c(g("L0_xattn_Wv").T), "Wq": c(g("L0_xattn_Wq")),
        "Wr": c(g("L0_ffn_Wr")), "Wv": c(g("L0_ffn_Wv")), "Wo": c(g("L0_ffn_Wo")), "WsT": c(g("L0_ffn_Ws").T),
        "K": c(g("L0_ffn_K_rwkv").reshape(2 * C, H)), "V": c(g("L0_ffn_V_rwkv").reshape(2 * H, C)),
        "W1": c(g("L0_ffn_W1")), "W2": c(g("L0_ffn_W2")), "W3": c(g("L0_ffn_W3")),
        "wb": c(np.concatenate([g("L0_ffn_conf_rwkv").T, g("L0_ffn_conf_trans")[:, None],
                                g("L0_ffn_w_diff")[:, None], g("L0_ffn_W_aff")], axis=1)),
        "d2v": c(g("L1_xattn_W_d2v").T), "img": c(g("L1_xattn_W_img").T), "txt": c(g("L1_xattn_W_txt").T),
        "att": c(np.concatenate([g("L1_xattn_W_att0").T, g("L1_xattn_W_att1").T], axis=1)),
        "f1": c(g("L1_xattn_W_f1").T), "f2": c(g("L1_xattn_W_f2").T),
        "rT": c(g("L1_ffn_W_r").T), "kT": c(g("L1_ffn_W_k").T), "vT": c(g("L1_ffn_W_v").T),
        "rows": c(np.concatenate([g("L0_xattn_bv"), g("L1_xattn_b_f2"), g("L0_ffn_capital_shares")])),
    }
    packed = {"bq": "L0_xattn_bq", "bk": "L0_xattn_bk", "ln1_w": "L0_ffn_ln1_w", "ln1_b": "L0_ffn_ln1_b",
              "ln2_w": "L0_ffn_ln2_w", "ln2_b": "L0_ffn_ln2_b", "b_d2v": "L1_xattn_b_d2v", "b_img": "L1_xattn_b_img",
              "b_txt": "L1_xattn_b_txt", "b_att0": "L1_xattn_b_att0", "b_att1": "L1_xattn_b_att1",
              "b_f1": "L1_xattn_b_f1", "mu_r": "L1_ffn_mu_r", "mu_k": "L1_ffn_mu_k"}
    arrays["cols"] = c(np.concatenate([chunks(packed[name]) for name in COLS]).T)

    nc = bacc.Bacc("TRN2", target_bir_lowering=False, num_devices=1)
    aps = {n: nc.dram_tensor("in_" + n, v.shape, mybir.dt.from_np(v.dtype), kind="ExternalInput").ap()
           for n, v in arrays.items()}
    out = nc.dram_tensor("out_0", (B, T, C), F32, kind="ExternalOutput").ap()
    build(nc, aps, out)
    r = run_bass_kernel_spmd(nc, [{"in_" + n: v for n, v in arrays.items()}], core_ids=[0])
    return r.results[0]["out_0"]
```

```python
from contextlib import ExitStack

import concourse.bass as bass
from concourse import mybir

F32, F32R, BF16 = mybir.dt.float32, mybir.dt.float32r, mybir.dt.bfloat16
ALU = mybir.AluOpType
ACT = mybir.ActivationFunctionType
X, XY = mybir.AxisListType.X, mybir.AxisListType.XY
RED = bass.bass_isa.ReduceOp

P = 128
B, T, C = 16, 512, 256
NT = T // P
KC = C // P
S, D = 64, 192
H = 1024
HC = H // P
NCTX = B * S
EPS = 1e-5
ROUND = 12582912.0
INV_SQRT = 1.0 / 16.0
NCHUNK = 2 + 2 * HC
GROUP_END = {1: 0, 1 + HC: 1, 1 + 2 * HC: 2}
GROUP_START = (0, 2, 2 + HC)
GROUP_EXPERT = (2, 0, 1)

COLS = {}
for _name, _n in (("bq", 2), ("bk", 2), ("ln1_w", 2), ("ln1_b", 2), ("ln2_w", 2), ("ln2_b", 2), ("b_d2v", 2),
                  ("b_img", 2), ("b_txt", 2), ("b_att0", 1), ("b_att1", 1), ("b_f1", 8), ("mu_r", 2), ("mu_k", 2)):
    COLS[_name] = (sum(n for _, n in COLS.values()), _n)
NCOLS = sum(n for _, n in COLS.values())


class Steps:

    def __init__(self, eng, sem, base=0):
        self.eng, self.sem, self.base, self.n = eng, sem, base, 0

    def add(self, ins):
        ins.then_inc(self.sem, 1)
        self.n += 1

    def wait(self):
        self.eng.wait_ge(self.sem, self.base + self.n)

    def link(self, ins):
        self.add(ins)
        self.wait()


def after(eng, sem, value):
    if not isinstance(value, int) or value > 0:
        eng.wait_ge(sem, value)


def build(nc, a, out):
    x3_dram = nc.dram_tensor("x3_scratch", [B, T, C], F32, kind="Internal").ap()
    text_dram = nc.dram_tensor("text_scratch", [B, T, C], F32, kind="Internal").ap()
    ms_dram = nc.dram_tensor("ms_scratch", [B, P, KC * S], F32, kind="Internal").ap()
    vs_dram = nc.dram_tensor("vs_scratch", [B, S, C], F32, kind="Internal").ap()
    cs_dram = nc.dram_tensor("cs_scratch", [B, 1, S], F32, kind="Internal").ap()
    kv_dram = nc.dram_tensor("kv_scratch", [B, P, 2 * S], F32, kind="Internal").ap()
    kvt_dram = nc.dram_tensor("kvt_scratch", [B, S, 2 * P], F32, kind="Internal").ap()

    with ExitStack() as top:
        stack = [top]

        def sb(name, shape, dt=F32):
            return stack[-1].enter_context(nc.sbuf_tensor(name, shape, dt))

        def sem(name):
            return top.enter_context(nc.semaphore(name))

        psum = [top.enter_context(nc.psum_tensor(f"pair{k}", [P, 1024], F32)) for k in range(4)]
        up_ps, out_ps, tp_ps, g_ps = psum

        cols = sb("cols", [P, NCOLS])

        def col(name, k=0):
            at, n = COLS[name]
            assert k < n
            return cols[:, at + k:at + k + 1]

        rows = sb("rows", [P, 2 * C + 3])
        bv_row, bf2_row, cap = rows[:, 0:C], rows[:, C:2 * C], rows[:, 2 * C:2 * C + 3]
        ident = sb("ident", [P, P])
        ident_b = sb("ident_b", [P, P], BF16)
        ones = sb("ones", [1, P])
        neg_half2 = sb("neg_half", [P, 2, NT])
        neg_half = neg_half2[:, 0, :]
        wtxt = sb("wtxt", [P, KC, C], BF16)
        watt = sb("watt", [P, KC, 2, P], BF16)
        wf1 = sb("wf1", [P, 2 * KC, H], BF16)
        wf2 = sb("wf2", [P, HC, C], BF16)
        q_img = sb("q_img", [P, KC, NCTX], BF16)
        avg = sb("avg", [P, KC, B])
        NW = 7
        W_D2V, W_IMG, W_TXT, W_A0, W_A1, W_F1, W_F2 = range(NW)
        wabs = sb("wabs", [P, NW])
        wsum = sb("wsum", [P, NW])
        wscale = sb("wscale", [P, NW])
        thr = sb("thr", [P, 2, NW])
        NA_ = 6
        A_CTX, A_VIS, A_IMG, A_TXT, A_CAT, A_H = range(NA_)
        amax = sb("amax", [P, NA_])
        gmax = sb("gmax", [P, NA_])
        iscale = sb("iscale", [P, NA_])
        inv = sb("inv", [P, NA_])
        oscale = sb("oscale", [P, 8])
        tmax = sb("tmax", [P, 1])
        tcur = sb("tcur", [P, 1])

        O_TXT, O_A0, O_A1, O_F1, O_F2 = 2, 3, 4, 5, 6

        v_set, p_set = sem("setup_dve"), sem("setup_pool")

        kv_scope = ExitStack()
        stack.append(kv_scope)
        names = ("Wr", "W2s", "Wv", "Wo", "W1", "W3")
        w = {n: (sb(n + "_hi", [P, KC, C], F32R), sb(n + "_lo", [P, KC, C], F32R)) for n in names}
        kexp = (sb("kexp_hi", [P, 2 * KC, H], F32R), sb("kexp_lo", [P, 2 * KC, H], F32R))
        vexp = (sb("vexp_hi", [P, 2 * HC, C], F32R), sb("vexp_lo", [P, 2 * HC, C], F32R))
        wb = sb("wb", [P, KC, 7])

        def mm3(pe, dst, st, mv, start, stop):
            pe.matmul(dst, st[1], mv[0], start=start, stop=False, skip_group_check=True)
            pe.matmul(dst, st[0], mv[1], start=False, stop=False, skip_group_check=True)
            return pe.matmul(dst, st[0], mv[0], start=False, stop=stop, skip_group_check=True)

        def stats(st, src, stat, mean, var, tmp, ready):
            for t in range(NT):
                st.add(st.eng.bn_stats(stat[:, t, :], src[:, t, :]))
            st.wait()
            e = lambda q: stat[:, :, q:q + 1].rearrange("p t o -> p (t o)")
            st.add(st.eng.tensor_tensor(mean[:, :], e(1), e(4), ALU.add))
            st.add(st.eng.tensor_tensor(tmp[:, :], e(1), e(4), ALU.subtract))
            st.link(st.eng.tensor_tensor(var[:, :], e(2), e(5), ALU.add))
            st.add(st.eng.tensor_scalar(mean[:, :], mean[:, :], 0.5, None, ALU.mult))
            st.add(st.eng.tensor_tensor(tmp[:, :], tmp[:, :], tmp[:, :], ALU.mult))
            st.link(st.eng.tensor_scalar(var[:, :], var[:, :], 1.0 / C, EPS, ALU.mult, ALU.add))
            last = st.eng.scalar_tensor_tensor(out=var[:, :], in0=tmp[:, :], scalar=0.25, in1=var[:, :],
                                               op0=ALU.mult, op1=ALU.add)
            if ready is None:
                st.link(last)
            else:
                last.then_inc(ready, 1)

        def pair(t, *ix):
            return (t[0][ix], t[1][ix])

        with ExitStack() as scope:
            stack.append(scope)
            big = sb("big", [P, 4 * H])
            w_raw = sb("w_raw", [P, 5, KC * C])
            raw = sb("raw", [P, 4 * 512])
            ctx_k = sb("ctx_k", [P, KC, NCTX])
            key_w = sb("key_w", [P, 5, 2, C])
            ctx = sb("ctx", [P, 2, NCTX])
            act = sb("act", [P, KC, NCTX])
            qa = sb("qa", [P, KC, NCTX], BF16)
            wide = sb("wide", [P, B * C])
            rounded = wide[:, 0:2 * NCTX].rearrange("p (k n) -> p k n", k=2)
            ms_all = wide[:, 2 * NCTX:4 * NCTX].rearrange("p (k n) -> p k n", k=2)
            cs_all = ctx_k[0:1, 0, :]
            v_all = wide[0:S, :].rearrange("p (b c) -> p b c", b=B)
            kf = act
            kt = w_raw[:, 0:4, :].rearrange("p q n -> p (q n)").rearrange("p (a j f) -> p a j f", a=2, f=P)
            wd2v = sb("wd2v", [P, 2, C], BF16)
            wimg = sb("wimg", [P, KC, C], BF16)
            ta = sb("ta", [P, 1024], BF16)
            tb_ = sb("tb_", [P, 1024], BF16)
            first_loaded, big_loaded, big_used, f2_loaded, w_loaded, raw_used, hi_done = (sem(n) for n in (
                "first_loaded", "big_loaded", "big_used", "f2_loaded", "weights_loaded", "raw_used", "split_hi"))
            key_free, key_lin, key_ready, key_turned, key_t_ready, key_stored = (sem(n) for n in (
                "key_places_free", "key_lin", "key_ready", "key_turned", "key_t_ready", "key_stored"))
            FIRST_LOADED = 16 * 15
            stored, ms_stored = sem("setup_stored"), sem("ms_stored")
            kpn = lambda ap: ap.rearrange("(k p) n -> p k n", p=P)
            ternary = [("d2v", W_D2V, raw[:, 0:512], wd2v, D * C), ("img", W_IMG, raw[:, 512:1024], wimg, C * C),
                       ("txt", W_TXT, raw[:, 1024:1536], wtxt, C * C), ("att", W_A0, raw[:, 1536:2048], watt, C * P),
                       ("f1", W_F1, big[:, :], wf1, 2 * C * H), ("f2", W_F2, raw[:, :], wf2, H * C)]
            split_w = ("K", "V", "Wr", "Wv", "Wo", "W1", "W3")
            HALVED = ("Wo", "W3")

            def halves(name):
                flat = lambda t: t[:, :, :].rearrange("p k n -> p (k n)")
                hi, lo = {"K": kexp, "V": vexp}.get(name) or w[name]
                src = big[:, :] if name in ("K", "V") else w_raw[:, split_w.index(name) - 2, :] if name in split_w else None
                return flat(hi), src, flat(lo)

            with nc.Block() as block:
                @block.sync
                def _(sp):
                    sp.dma_start(cols[:, :], a["cols"]).then_inc(first_loaded, 16)
                    sp.dma_start(ctx[:, 0, :], a["ctxT"][0:P, :]).then_inc(first_loaded, 16)
                    sp.dma_start(ctx[0:D - P, 1, :], a["ctxT"][P:D, :]).then_inc(first_loaded, 16)
                    v0 = raw[:, 0:512].rearrange("p (k n) -> p k n", k=2)
                    sp.dma_start(v0[:, 0, :], a["d2v"][0:P, :]).then_inc(first_loaded, 16)
                    sp.dma_start(v0[0:D - P, 1, :], a["d2v"][P:D, :]).then_inc(first_loaded, 16)
                    for name, _, src, _, _ in ternary[1:4]:
                        sp.dma_start(src.rearrange("p (k n) -> p k n", k=2), kpn(a[name])).then_inc(first_loaded, 16)
                    for k, name in ((3, "WkT"), (4, "WvT")):
                        sp.dma_start(key_w[:, k, 0, :], a[name][0:P, :]).then_inc(first_loaded, 16)
                        sp.dma_start(key_w[0:D - P, k, 1, :], a[name][P:D, :]).then_inc(first_loaded, 16)
                    for k, name in enumerate(("WsT", "W2", "Wq")):
                        sp.dma_start(key_w[:, k, :, :], kpn(a[name])).then_inc(first_loaded, 16)
                    sp.dma_start(big[:, :].rearrange("p (k n) -> p k n", k=4), kpn(a["K"])).then_inc(big_loaded, 16)
                    sp.dma_start(rows[:, :], a["rows"].partition_broadcast(P)).then_inc(w_loaded, 16)
                    sp.dma_start(wb[:, :, :], kpn(a["wb"])).then_inc(w_loaded, 16)
                    for name in split_w[2:]:
                        sp.dma_start(halves(name)[1].rearrange("p (k n) -> p k n", k=KC), kpn(a[name])).then_inc(w_loaded, 16)
                    sp.wait_ge(raw_used, 4)
                    sp.dma_start(raw[:, :].rearrange("p (k n) -> p k n", k=HC), kpn(a["f2"])).then_inc(f2_loaded, 16)
                    sp.wait_ge(big_used, 1)
                    sp.dma_start(big[:, :].rearrange("p (k n) -> p k n", k=16), kpn(a["V"])).then_inc(big_loaded, 16)
                    sp.wait_ge(big_used, 2)
                    sp.dma_start(big[:, :].rearrange("p (k n) -> p k n", k=4), kpn(a["f1"])).then_inc(big_loaded, 16)
                    sp.wait_ge(key_ready, 2)
                    for a_ in range(2):
                        sp.dma_start(kv_dram.rearrange("b p (a s) -> a p b s", a=2)[a_],
                                     kf[:, a_, :].rearrange("p (b s) -> p b s", s=S)).then_inc(key_stored, 16)
                    sp.wait_ge(key_t_ready, 2)
                    for a_ in range(2):
                        for h in range(2):
                            sp.dma_start(kvt_dram.rearrange("(j h) s (a f) -> a h s j f", h=2, a=2)[a_, h],
                                         kt[h * S:(h + 1) * S, a_, :, :]).then_inc(key_stored, 16)
                    sp.wait_ge(key_stored, 96)
                W_LOADED = 16 * len(split_w)

                part_ready, all_ready = sem("partitions_ready"), sem("all_partitions_ready")
                JOBS = [("max", A_CTX), ("sum", W_D2V), ("sum", W_IMG), ("sum", W_TXT), ("sum", W_A0), ("sum", W_A1),
                        ("max", A_VIS), ("sum", W_F2), ("max", A_IMG), ("sum", W_F1)]
                q_ready, lin_done, f32_ready = sem("q_ready"), sem("lin_done"), sem("lin_f32")
                key_done, key_out, val_out = sem("key_done"), sem("key_out"), sem("values_out")
                K_KEYS, K_M, K_BQ, K_VALUES = 1, 2, 3, 4
                K_W2S = K_VALUES + B // 4

                @block.gpsimd
                def _(g):
                    g.memset(ctx[D - P:P, 1, :], 0.0).then_inc(p_set, 1)
                    g.memset(raw[D - P:P, 256:512], 0.0).then_inc(p_set, 1)
                    g.wait_ge(p_set, 2)
                    g.memset(tmax[:, :], 0.0).then_inc(p_set, 1)
                    g.memset(ident[:, :], 0.0).then_inc(p_set, 1)
                    g.memset(ident_b[:, :], 0.0).then_inc(p_set, 1)
                    g.memset(ones[:, :], 1.0).then_inc(p_set, 1)
                    g.memset(neg_half2[:, :, :], -0.5).then_inc(p_set, 1)
                    g.wait_ge(p_set, 7)
                    for m in (ident, ident_b):
                        g.affine_select(out=m[:, :], in_=m[:, :], compare_op=ALU.not_equal, fill=1.0, base=0,
                                        pattern=[[-1, P]], channel_multiplier=1).then_inc(p_set, 1)

                    for n, (kind, k) in enumerate(JOBS):
                        g.wait_ge(part_ready, n + 1)
                        to, of = (gmax, amax) if kind == "max" else (wsum, wabs)
                        g.partition_all_reduce(to[:, k:k + 1], of[:, k:k + 1], P, RED.max if kind == "max" else RED.add).then_inc(all_ready, 1)

                @block.vector
                def _(v):
                    st = Steps(v, v_set)

                    def act_max(k, src):
                        v.tensor_reduce(amax[:, k:k + 1], src, XY, ALU.max, apply_absolute_value=True).then_inc(part_ready, 1)

                    def act_scale(k):
                        v.wait_ge(all_ready, JOBS.index(("max", k)) + 1)
                        st.link(v.tensor_scalar(iscale[:, k:k + 1], gmax[:, k:k + 1], 1e-8, 1.0 / 127.0, ALU.max, ALU.mult))
                        st.link(v.reciprocal(inv[:, k:k + 1], iscale[:, k:k + 1]))
                        if k < A_IMG:
                            st.link(v.tensor_tensor(oscale[:, k:k + 1], wscale[:, k:k + 1], iscale[:, k:k + 1], ALU.mult))

                    def quantise(k, src, dst):
                        for c in range(2):
                            st.add(v.tensor_scalar(rounded[:, c, :], src[:, c, :], inv[:, k:k + 1], ROUND, ALU.mult, ALU.add))
                        st.wait()
                        for c in range(2):
                            last = v.tensor_scalar(dst[:, c, :], rounded[:, c, :], ROUND, None, ALU.subtract)
                        last.then_inc(q_ready, 1)

                    def make_ternary(n, loaded, count):
                        name, k0, flat, dst, weights = ternary[n]
                        v.wait_ge(loaded, count)
                        if name == "att":
                            f3 = flat.rearrange("p (k a n) -> p k a n", k=KC, a=2)
                            jobs = [(k0 + j, f3[:, :, j, :], f3[:, :, j, :], watt[:, :, j, :]) for j in range(2)]
                        else:
                            size = flat.shape[1]
                            out_ = dst[:, :, :].rearrange("p k n -> p (k n)")
                            half = min(size, 1024)
                            jobs = [(k0, flat if o == 0 else None, flat[:, o:o + half], out_[:, o:o + half]) for o in range(0, size, half)]
                        for k, whole, _, _ in jobs:
                            if whole is not None:
                                v.tensor_reduce(wabs[:, k:k + 1], whole, XY if name == "att" else X, ALU.add,
                                                apply_absolute_value=True).then_inc(part_ready, 1)
                        for k, whole, src, dst_ in jobs:
                            if whole is not None:
                                v.wait_ge(all_ready, JOBS.index(("sum", k)) + 1)
                                st.link(v.tensor_scalar(wscale[:, k:k + 1], wsum[:, k:k + 1], 1.0 / weights, 1e-5, ALU.mult, ALU.max))
                                st.add(v.tensor_scalar(thr[:, 0, k:k + 1], wscale[:, k:k + 1], 0.5, None, ALU.mult))
                                st.link(v.tensor_scalar(thr[:, 1, k:k + 1], wscale[:, k:k + 1], -0.5, None, ALU.mult))
                            if name == "att":
                                over = ta[:, 0:C].rearrange("p (k n) -> p k n", k=KC)
                                under = tb_[:, 0:C].rearrange("p (k n) -> p k n", k=KC)
                            else:
                                over, under = ta[:, 0:src.shape[1]], tb_[:, 0:src.shape[1]]
                            st.add(v.tensor_scalar(over, src, thr[:, 0, k:k + 1], None, ALU.is_gt))
                            st.link(v.tensor_scalar(under, src, thr[:, 1, k:k + 1], None, ALU.is_lt))
                            last = v.tensor_tensor(dst_, over, under, ALU.subtract)
                            if dst_ is jobs[-1][3]:
                                last.then_inc(raw_used, 1)
                            else:
                                st.link(last)

                    def split_low(n):
                        v.wait_ge(hi_done, n + 1)
                        hi, src, lo = halves(split_w[n])
                        last = v.scalar_tensor_tensor(out=lo, in0=src, scalar=0.5 if split_w[n] in HALVED else 1.0,
                                                      in1=hi.bitcast(F32), op0=ALU.mult, op1=ALU.subtract)
                        if n < 2:
                            last.then_inc(big_used, 1)
                        if n == len(split_w) - 1:
                            last.then_inc(key_free, 1)

                    def image_step(k, dst):
                        v.wait_ge(f32_ready, 4 * k)
                        act_max(k, act[:, :, :])
                        act_scale(k)
                        quantise(k, act, dst)

                    v.wait_ge(first_loaded, FIRST_LOADED)
                    v.wait_ge(p_set, 3)
                    act_max(A_CTX, ctx[:, :, :])
                    make_ternary(0, first_loaded, FIRST_LOADED)
                    act_scale(A_CTX)
                    quantise(A_CTX, ctx, qa)
                    make_ternary(1, first_loaded, FIRST_LOADED)
                    make_ternary(2, first_loaded, FIRST_LOADED)
                    make_ternary(3, first_loaded, FIRST_LOADED)
                    split_low(0)
                    image_step(A_VIS, qa)
                    make_ternary(5, f2_loaded, 16)
                    split_low(1)
                    image_step(A_IMG, q_img)
                    av = act[:, :, :].rearrange("p k (b s) -> p (k b) s", s=S)
                    st.link(v.tensor_reduce(avg[:, :, :].rearrange("p k b -> p (k b)"), av, X, ALU.add))
                    st.add(v.tensor_scalar(avg[:, :, :], avg[:, :, :], 1.0 / S, None, ALU.mult))
                    for o, k in ((O_A0, W_A0), (O_A1, W_A1)):
                        last = v.tensor_tensor(oscale[:, o:o + 1], wscale[:, k:k + 1], iscale[:, A_IMG:A_IMG + 1], ALU.mult)
                    last.then_inc(key_free, 1)
                    v.wait_ge(w_loaded, W_LOADED)
                    v.wait_ge(ms_stored, 32)
                    v.wait_ge(q_ready, 3)
                    for q in range(B // 4):
                        v.wait_ge(key_done, K_VALUES + q)
                        for b in range(4):
                            last = v.tensor_tensor(v_all[:, 4 * q + b, :], (out_ps, up_ps)[q % 2][0:S, b * C:(b + 1) * C],
                                                   bv_row[0:S, :], ALU.add)
                        last.then_inc(val_out, 1)
                        if q % 2:
                            for n in range(2 if q == 1 else 5, 5 if q == 1 else len(split_w)):
                                split_low(n)
                    make_ternary(4, big_loaded, 48)
                    v.wait_ge(hi_done, len(split_w) + 1)
                    hi, _, lo = halves("W2s")
                    v.tensor_tensor(lo, out_ps[:, 0:KC * C], hi.bitcast(F32), ALU.subtract)

                @block.scalar
                def _(s):
                    s.wait_ge(first_loaded, FIRST_LOADED)
                    s.wait_ge(key_done, K_KEYS)
                    for c, ps in ((0, up_ps), (1, out_ps)):
                        last = s.activation(ctx_k[:, c, :], ps[:, :], ACT.Identity, bias=col("bk", c))
                    last.then_inc(key_out, 1)

                    def image_linear(k, bias):
                        if k == 1:
                            s.wait_ge(q_ready, 2)
                        for c in range(2):
                            for h in range(2):
                                s.wait_ge(lin_done, 4 * k + 2 * c + h + 1)
                                s.activation(act[:, c, h * 512:(h + 1) * 512], (tp_ps, g_ps)[c][:, h * 512:(h + 1) * 512],
                                             ACT.Identity, bias=col(bias, c), scale=oscale[:, k:k + 1]).then_inc(f32_ready, 1)

                    def split_high(n):
                        hi, src, _ = halves(split_w[n])
                        if n < 2:
                            s.wait_ge(big_loaded, 16 * n + 16)
                        s.activation(hi, src, ACT.Copy, scale=0.5 if split_w[n] in HALVED else 1.0).then_inc(hi_done, 1)
                    image_linear(0, "b_d2v")
                    split_high(0)
                    s.wait_ge(key_done, K_M)
                    for c, ps in ((0, up_ps), (1, out_ps)):
                        last = s.activation(ms_all[:, c, :], ps[:, :], ACT.Copy, scale=INV_SQRT)
                    last.then_inc(key_out, 1)
                    s.wait_ge(key_out, 2)
                    for k in range(KC):
                        s.dma_start(ms_dram.rearrange("b p (k s) -> p k b s", k=KC)[:, k],
                                    ms_all[:, k, :].rearrange("p (b s) -> p b s", s=S)).then_inc(ms_stored, 16)
                    split_high(1)
                    image_linear(1, "b_img")
                    s.wait_ge(key_done, K_BQ)
                    s.activation(cs_all, up_ps[0:1, :], ACT.Copy, scale=INV_SQRT).then_inc(key_out, 1)
                    s.wait_ge(key_out, 3)
                    s.dma_start(cs_dram.rearrange("b o s -> o b s"), cs_all.rearrange("p (b s) -> p b s", s=S)).then_inc(stored, 16)
                    s.wait_ge(w_loaded, W_LOADED)
                    for n in range(2, len(split_w)):
                        split_high(n)
                    s.wait_ge(key_done, K_W2S)
                    s.activation(halves("W2s")[0], out_ps[:, 0:KC * C], ACT.Copy).then_inc(hi_done, 1)
                    s.wait_ge(val_out, B // 4)
                    s.dma_start(vs_dram.rearrange("b s c -> s b c"), v_all[:, :, :]).then_inc(stored, 16)
                    for a_ in range(2):
                        s.wait_ge(key_lin, a_ + 1)
                        s.wait_ge(key_free, 1)
                        s.activation(kf[:, a_, :], (tp_ps, g_ps)[a_][:, :], ACT.Identity, bias=col("b_att%d" % a_),
                                     scale=oscale[:, O_A0 + a_:O_A0 + a_ + 1]).then_inc(key_ready, 1)
                    for a_ in range(2):
                        s.wait_ge(key_turned, a_ + 1)
                        s.wait_ge(key_free, 2)
                        s.activation(kt[:, a_, :, :].rearrange("p j f -> p (j f)"), (tp_ps, g_ps)[a_][:, :], ACT.Copy).then_inc(key_t_ready, 1)
                    s.wait_ge(stored, 32)

                @block.tensor
                def _(pe):
                    ws, w2, wq, wk, wv = (key_w[:, k, :, :] for k in range(5))
                    pe.wait_ge(first_loaded, FIRST_LOADED)
                    for c, ps in ((0, up_ps), (1, out_ps)):
                        for h in range(2):
                            hs = slice(h * 512, (h + 1) * 512)
                            pe.matmul(ps[:, hs], wk[:, 0, c * P:(c + 1) * P], ctx[:, 0, hs], start=True, stop=False)
                            m = pe.matmul(ps[:, hs], wk[0:D - P, 1, c * P:(c + 1) * P], ctx[0:D - P, 1, hs], start=False, stop=True)
                    m.then_inc(key_done, 1)

                    def image_linear(k, wt):
                        pe.wait_ge(q_ready, k + 1)
                        if k == 1:
                            pe.wait_ge(f32_ready, 4)
                        for c in range(2):
                            for h in range(2):
                                for j in range(2):
                                    m = pe.matmul((tp_ps, g_ps)[c][:, h * 512:(h + 1) * 512], wt[:, j, c * P:(c + 1) * P],
                                                  qa[:, j, h * 512:(h + 1) * 512], start=(j == 0), stop=(j == 1))
                                m.then_inc(lin_done, 1)
                    image_linear(0, wd2v)
                    pe.wait_ge(key_out, 1)
                    for c, ps in ((0, up_ps), (1, out_ps)):
                        for h in range(2):
                            hs = slice(h * 512, (h + 1) * 512)
                            for j in range(2):
                                m = pe.matmul(ps[:, hs], wq[:, j, c * P:(c + 1) * P], ctx_k[:, j, hs], start=(j == 0), stop=(j == 1))
                    m.then_inc(key_done, 1)
                    image_linear(1, wimg)
                    pe.wait_ge(key_out, 2)
                    for h in range(2):
                        hs = slice(h * 512, (h + 1) * 512)
                        for j in range(2):
                            m = pe.matmul(up_ps[0:1, hs], col("bq", j), ctx_k[:, j, hs], start=(j == 0), stop=(j == 1))
                    m.then_inc(key_done, 1)
                    for q in range(B // 4):
                        if q == 1:
                            pe.wait_ge(key_out, 3)
                        if q >= 2:
                            pe.wait_ge(val_out, q - 1)
                        for b in range(4):
                            n = 4 * q + b
                            dst = (out_ps, up_ps)[q % 2][0:S, b * C:(b + 1) * C]
                            pe.matmul(dst, ctx[:, 0, n * S:(n + 1) * S], wv[:, 0, :], start=True, stop=False)
                            m = pe.matmul(dst, ctx[0:D - P, 1, n * S:(n + 1) * S], wv[0:D - P, 1, :], start=False, stop=True)
                        m.then_inc(key_done, 1)
                    pe.wait_ge(val_out, B // 4 - 1)
                    for c in range(2):
                        for j in range(2):
                            m = pe.matmul(out_ps[:, c * C:(c + 1) * C], ws[:, j, c * P:(c + 1) * P], w2[:, j, :],
                                          start=(j == 0), stop=(j == 1))
                    m.then_inc(key_done, 1)
                    pe.wait_ge(q_ready, 3)
                    pe.wait_ge(f32_ready, 8)
                    for a_ in range(2):
                        for h in range(2):
                            for k in range(KC):
                                m = pe.matmul((tp_ps, g_ps)[a_][:, h * 512:(h + 1) * 512], watt[:, k, a_, :],
                                              q_img[:, k, h * 512:(h + 1) * 512], start=(k == 0), stop=(k == KC - 1))
                        m.then_inc(key_lin, 1)
                    pe.wait_ge(p_set, 9)
                    for a_ in range(2):
                        pe.wait_ge(key_ready, a_ + 1)
                        for j in range(B // 2):
                            m = pe.transpose((tp_ps, g_ps)[a_][:, j * P:(j + 1) * P], kf[:, a_, j * P:(j + 1) * P], ident[:, :])
                        m.then_inc(key_turned, 1)
            stack.pop()

        with ExitStack() as scope:
            stack.append(scope)
            x_in = sb("x_in", [P, NT, C])
            x1 = sb("x1", [P, NT, C])
            x2 = sb("x2", [P, NT, C])
            xacc = sb("xacc", [P, NT, C])
            x3 = sb("x3", [P, NT, C])
            text = sb("text", [P, NT, C])
            xn = sb("xn", [P, NT, C])
            xn0 = sb("xn0", [P, NT, C])
            fm = sb("fm", [P, KC, T])
            act_p = (sb("act_hi", [P, KC, T], F32R), sb("act_lo", [P, KC, T], F32R))
            h_p = (sb("h_hi", [P, KC, T], F32R), sb("h_lo", [P, KC, T], F32R))
            t1 = xn
            t2 = sb("t2", [P, KC, T])
            probs = sb("probs", [P, NT // 2, 2, S])
            probs_t = sb("probs_t", [P, NT // 2, P])
            ms, vs, cs = sb("ms", [P, KC, S]), sb("vs", [P, C]), sb("cs", [1, S])
            hr_r = sb("hr_r", [P, 3, T])
            hr_sq = sb("hr_sq", [P, 2, T])
            RING, LAG = 6, 3
            hr_p = (sb("hr_hi", [P, RING, T], F32R), sb("hr_lo", [P, RING, T], F32R))
            stat = sb("stat", [P, NT, 6])
            mean, var, vtmp, rs, nmr = (sb(n, [P, NT]) for n in ("mean", "var", "vtmp", "rs", "nmr"))
            stat0 = sb("stat0", [P, NT, 6])
            mean0, var0, vtmp0, rs0 = (sb(n, [P, NT]) for n in ("mean0", "var0", "vtmp0", "rs0"))
            var1, rs1 = sb("var1", [P, 2, NT]), sb("rs1", [P, 2, NT])
            stat3 = sb("stat3", [P, NT, 6])
            mean3, var3, vtmp3, rs3, nmr3 = (sb(n, [P, NT]) for n in ("mean3", "var3", "vtmp3", "rs3", "nmr3"))
            smax, ssum = sb("smax", [P, NT]), sb("ssum", [P, NT])
            sig = sb("sig", [P, NT, 4])
            bid = sb("bid", [P, NT, 3])
            hot = sb("hot", [P, NT, 3])
            btmp = sb("btmp", [P, NT, 3])
            coef = sb("coef", [P, NT, 3])
            cap4 = sb("cap4", [P, NT, 3])

            x_loaded, small_loaded = sem("x_loaded"), sem("small_loaded")
            x3_stored, text_stored = sem("x3_stored"), sem("text_stored")
            ve_ready, rs_ready, ve3_ready, rs3_ready = (sem(n) for n in ("ve_ready", "rs_ready", "ve3_ready", "rs3_ready"))
            xn_ready, turned, turned_out = sem("xn_ready"), sem("turned"), sem("turned_out")
            scores_done, shifted, exp_done, probs_turned, probs_t_ready = (sem(n) for n in (
                "scores_done", "scores_shifted", "exp_done", "probs_turned", "probs_t_ready"))
            pv_done, x1_ready, x2_ready, xacc_ready = (sem(n) for n in ("pv_done", "x1_ready", "x2_ready", "xacc_ready"))
            hi_ready, lo_ready = sem("act_hi_ready"), sem("act_lo_ready")
            wr_done, w2s_done, wv_done, wo_done = (sem(n) for n in ("wr_done", "w2s_done", "wv_done", "wo_done"))
            t1_ready, t2_ready, g_ready = sem("t1_ready"), sem("t2_ready"), sem("gated_ready")
            h_hi_ready, h_ready = sem("h_hi_ready"), sem("h_ready")
            bids_done, bexp_done, coef_ready = sem("bids_done"), sem("bid_exp_done"), sem("coef_ready")
            up_done, relu_done, sq_done, hr_hi_done, hr_lo_done, evac_done = (sem(n) for n in (
                "up_done", "relu_done", "sq_done", "hr_hi_done", "hr_lo_done", "evac_done"))
            down_done = sem("down_done")
            ve0_ready, rs0_ready, ve1_ready, rs1_ready, xn0_ready, bid_ready = (sem(n) for n in (
                "ve0_ready", "rs0_ready", "ve1_ready", "rs1_ready", "xn0_ready", "bid_ready"))
            nmr_ready, x2ln_ready, nmr3_ready, text_ready, text_seen = (sem(n) for n in (
                "nmr_ready", "x2_ln_ready", "nmr3_ready", "text_ready", "text_seen"))
            v_first, v_front, v_bids, v_tail, a_front = sem("dve_first"), sem("dve_front"), sem("dve_bids"), sem("dve_tail"), sem("act_front")
            K0, KF, KB, KT = 10, 28, 13, 11

            x_v = a["x"].rearrange("b (t p) c -> b p t c", p=P)
            x3_v = x3_dram.rearrange("b (t p) c -> b p t c", p=P)
            text_v = text_dram.rearrange("b (t p) c -> b p t c", p=P)

            def one(ap, n):
                return ap[bass.ds(n, 1)].rearrange("o p t c -> p (o t) c")

            def one2(ap, n):
                return ap[bass.ds(n, 1)].rearrange("o p c -> (o p) c")

            def pipeline(eng, iteration):
                iteration(None, None, None, 0)
                iteration(None, None, 0, 1)
                iteration(None, 0, 1, 2)
                iteration(0, 1, 2, 3)
                with eng.Fori(2, B - 2) as i:
                    iteration(i - 1, i, i + 1, i + 2)
                iteration(B - 3, B - 2, B - 1, None)
                iteration(B - 2, B - 1, None, None)
                iteration(B - 1, None, None, None)

            flat = lambda b: b[:, :, :].rearrange("p a b -> p (a b)")

            with nc.Block() as block:
                @block.sync
                def _(sp):
                    def load(n):
                        after(sp, x1_ready, n)
                        sp.dma_start(x_in[:, :, :], one(x_v, n)).then_inc(x_loaded, 16)
                        after(sp, pv_done, n)
                        sp.dma_start(flat(ms), one2(ms_dram, n)).then_inc(small_loaded, 16)
                        for h in range(2):
                            sp.dma_start(vs[h * S:(h + 1) * S, :], one2(vs_dram, n)).then_inc(small_loaded, 16)
                        sp.dma_start(cs[:, :], one2(cs_dram, n)).then_inc(small_loaded, 16)

                    def store(t):
                        sp.wait_ge(evac_done, 3 * t + 3)
                        sp.dma_start(one(x3_v, t), x3[:, :, :]).then_inc(x3_stored, 16)
                        sp.wait_ge(text_ready, t + 1)
                        sp.dma_start(one(text_v, t), text[:, :, :]).then_inc(text_stored, 16)

                    load(0)
                    load(1)
                    load(2)
                    load(3)
                    with sp.Fori(4, B) as n:
                        store(n - 4)
                        load(n)
                    for t in range(B - 4, B):
                        store(t)
                    sp.wait_ge(x3_stored, 16 * B)
                    sp.wait_ge(text_stored, 16 * B)

                @block.gpsimd
                def _(g):
                    def iteration(t, i, n, m):
                        if i is not None:
                            g.wait_ge(x2_ready, i + 1)
                            after(g, evac_done, 3 * i)
                            g.tensor_tensor(xacc[:, :, :], x1[:, :, :], x2[:, :, :], ALU.add).then_inc(xacc_ready, 1)
                        if n is not None:
                            g.wait_ge(ve1_ready, n + 1)
                            g.tensor_tensor(rs1[:, :, :], var1[:, :, :], neg_half2[:, :, :], ALU.pow).then_inc(rs1_ready, 1)
                        if m is not None:
                            g.wait_ge(ve0_ready, m + 1)
                            g.tensor_tensor(rs0[:, :], var0[:, :], neg_half[:, :], ALU.pow).then_inc(rs0_ready, 1)
                        if t is not None:
                            g.wait_ge(ve3_ready, t + 1)
                            g.tensor_tensor(rs3[:, :], var3[:, :], neg_half[:, :], ALU.pow).then_inc(rs3_ready, 1)
                        if n is not None:
                            g.wait_ge(ve_ready, n + 1)
                            g.tensor_tensor(rs[:, :], var[:, :], neg_half[:, :], ALU.pow).then_inc(rs_ready, 1)
                    pipeline(g, iteration)

                @block.scalar
                def _(s):
                    def chunk(c, i):
                        up = up_ps[:, (c % 2) * T:(c % 2 + 1) * T]
                        hi = hr_p[0][:, c % RING, :]
                        if c < 2:
                            s.wait_ge(sq_done, NCHUNK * i + c + 1)
                            after(s, down_done, NCHUNK * i + c + 1 - RING)
                            s.activation(hi, hr_sq[:, c % 2, :], ACT.Copy).then_inc(hr_hi_done, 1)
                            return
                        s.wait_ge(up_done, NCHUNK * i + c + 1)
                        if c >= 5:
                            s.wait_ge(sq_done, NCHUNK * i + c - 2)
                        s.activation(hr_r[:, c % 3, :], up, ACT.Relu).then_inc(relu_done, 1)
                        s.wait_ge(relu_done, (NCHUNK - 2) * i + c - 1)
                        after(s, down_done, NCHUNK * i + c + 1 - RING)
                        s.activation(hi, hr_r[:, c % 3, :], ACT.Square).then_inc(hr_hi_done, 1)

                    def front(k, n):
                        if k == 0:
                            s.wait_ge(turned, 3 * n + 1)
                            after(s, bids_done, n)
                            after(s, h_ready, n)
                            s.activation(flat(fm), tp_ps[:, :], ACT.Copy).then_inc(turned_out, 1)
                        if k == 2:
                            s.wait_ge(shifted, n + 1)
                            s.activation(probs[:, :, :, :], probs[:, :, :, :], ACT.Exp).then_inc(exp_done, 1)
                        if k == 3:
                            s.wait_ge(probs_turned, n + 1)
                            after(s, pv_done, n)
                            s.activation(flat(probs_t), tp_ps[:, 0:T // 2], ACT.Copy).then_inc(probs_t_ready, 1)
                        if k == 7:
                            s.wait_ge(nmr_ready, n + 1)
                            for t in range(NT):
                                last = s.activation(x2[:, t, :], x1[:, t, :], ACT.Identity, bias=nmr[:, t:t + 1], scale=rs1[:, 0, t:t + 1])
                            last.then_inc(x2ln_ready, 1)
                        if k == 8:
                            s.wait_ge(turned, 3 * n + 2)
                            for c in range(KC):
                                s.activation(fm[:, c, :], tp_ps[:, c * T:(c + 1) * T], ACT.Identity,
                                             bias=col("ln1_b", c), scale=col("ln1_w", c)).then_inc(a_front, 1)
                            s.wait_ge(a_front, 2 * KC * n + KC)
                            after(s, wo_done, n)
                            s.activation(act_p[0][:, :, :], fm[:, :, :], ACT.Copy).then_inc(hi_ready, 1)
                        if k == 10:
                            s.wait_ge(wr_done, n + 1)
                            s.activation(flat(t1), g_ps[:, :], ACT.Tanh, scale=0.5).then_inc(t1_ready, 1)
                            s.wait_ge(w2s_done, n + 1)
                            if not isinstance(n, int) or n > 0:
                                s.wait_ge(sq_done, NCHUNK * n - NCHUNK + 2)
                            s.activation(flat(t2), tp_ps[:, :], ACT.Tanh, scale=0.5).then_inc(t2_ready, 1)
                        if k == 11:
                            s.wait_ge(g_ready, n + 1)
                            s.activation(act_p[0][:, :, :], fm[:, :, :], ACT.Copy).then_inc(hi_ready, 1)
                        if k == 16:
                            s.wait_ge(turned, 3 * n + 3)
                            s.wait_ge(lo_ready, 2 * n + 2)
                            for c in range(KC):
                                s.activation(fm[:, c, :], tp_ps[:, c * T:(c + 1) * T], ACT.Identity,
                                             bias=col("ln2_b", c), scale=col("ln2_w", c)).then_inc(a_front, 1)
                        if k == 17:
                            s.wait_ge(bids_done, n + 1)
                            after(s, bid_ready, n)
                            s.activation(sig[:, :, :], g_ps[:, 0:8 * NT].rearrange("p (t e) -> p t e", e=8)[:, :, 0:4],
                                         ACT.Exp, scale=-1.0).then_inc(bexp_done, 1)
                        if k == NCHUNK:
                            s.wait_ge(a_front, 2 * KC * n + 2 * KC)
                            after(s, up_done, NCHUNK * n)
                            s.activation(h_p[0][:, :, :], fm[:, :, :], ACT.Copy).then_inc(h_hi_ready, 1)

                    def iteration(t, i, n, m):
                        for k in range(NCHUNK):
                            if k == 12 and t is not None:
                                s.wait_ge(nmr3_ready, t + 1)
                                after(s, text_seen, t)
                                after(s, text_stored, 16 * t)
                                for q in range(NT):
                                    last = s.activation(text[:, q, :], x3[:, q, :], ACT.Identity, bias=nmr3[:, q:q + 1], scale=rs3[:, q:q + 1])
                                last.then_inc(text_ready, 1)
                            if n is not None:
                                front(k, n)
                            if i is not None:
                                chunk(k, i)
                        if n is not None:
                            front(NCHUNK, n)
                    pipeline(s, iteration)

                @block.tensor
                def _(pe):
                    def up(c, i):
                        dst = up_ps[:, (c % 2) * T:(c % 2 + 1) * T]
                        if c == 0:
                            pe.wait_ge(h_ready, i + 1)
                        if c in (2, 3):
                            pe.wait_ge(sq_done, NCHUNK * i + c - 1)
                        else:
                            after(pe, relu_done, (NCHUNK - 2) * i + (c - 1 if c < 2 else c - 3))
                        for k in range(KC):
                            if c < 2:
                                st = pair(w["W1"], slice(None), k, slice(c * P, (c + 1) * P))
                            else:
                                e, cc = divmod(c - 2, HC)
                                st = pair(kexp, slice(None), e * KC + k, slice(cc * P, (cc + 1) * P))
                            last = mm3(pe, dst, st, pair(h_p, slice(None), k, slice(None)), k == 0, k == KC - 1)
                        last.then_inc(up_done, 1)

                    def down(c, i):
                        first = c in GROUP_START
                        pe.wait_ge(hr_lo_done, NCHUNK * i + c + 1)
                        if first:
                            after(pe, evac_done, 3 * i + GROUP_START.index(c))
                        for t in range(NT):
                            st = pair(hr_p, slice(None), c % RING, slice(t * P, (t + 1) * P))
                            mv = pair(w["W3"], slice(None), c, slice(None)) if c < 2 else pair(vexp, slice(None), c - 2, slice(None))
                            last = mm3(pe, out_ps[:, t * C:(t + 1) * C], st, mv, first and t % 2 == 0, c in GROUP_END)
                        last.then_inc(down_done, 1)

                    def turn(xn):
                        for c in range(KC):
                            for t in range(NT):
                                last = pe.transpose(tp_ps[:, c * T + t * P:c * T + (t + 1) * P], xn[:, t, c * P:(c + 1) * P], ident[:, :])
                        last.then_inc(turned, 1)

                    def project(dst, name, done):
                        for c in range(KC):
                            for k in range(KC):
                                last = mm3(pe, dst[:, c * T:(c + 1) * T], pair(w[name], slice(None), k, slice(c * P, (c + 1) * P)),
                                           pair(act_p, slice(None), k, slice(None)), k == 0, k == KC - 1)
                        last.then_inc(done, 1)

                    def front(k, n):
                        if k == 1:
                            pe.wait_ge(turned_out, n + 1)
                            pe.wait_ge(small_loaded, 64 * n + 64)
                            after(pe, bid_ready, n)
                            for t in range(NT):
                                dst = g_ps[:, t * S:(t + 1) * S]
                                for c in range(KC):
                                    pe.matmul(dst, fm[:, c, t * P:(t + 1) * P], ms[:, c, :], start=(c == 0), stop=False)
                                last = pe.matmul(dst, ones[:, :], cs[:, :], start=False, stop=True)
                            last.then_inc(scores_done, 1)
                        if k == 2:
                            pe.wait_ge(exp_done, n + 1)
                            for j in range(NT // 2):
                                last = pe.transpose(tp_ps[:, j * P:(j + 1) * P], probs[:, j, :, :].rearrange("p h s -> p (h s)"), ident[:, :])
                            last.then_inc(probs_turned, 1)
                        if k == 4:
                            pe.wait_ge(probs_t_ready, n + 1)
                            for j in range(NT // 2):
                                for h in range(2):
                                    t, half = 2 * h + j, slice(h * S, (h + 1) * S)
                                    last = pe.matmul(g_ps[:, t * C:(t + 1) * C], probs_t[half, j, :], vs[half, :], start=True, stop=True)
                            last.then_inc(pv_done, 1)
                        if k == 7:
                            pe.wait_ge(xn_ready, 2 * n + 1)
                            turn(xn)
                        if k == 9:
                            pe.wait_ge(lo_ready, 2 * n + 1)
                            project(g_ps, "Wr", wr_done)
                            project(tp_ps, "W2s", w2s_done)
                        if k == 10:
                            pe.wait_ge(t1_ready, n + 1)
                            project(g_ps, "Wv", wv_done)
                        if k == 12:
                            pe.wait_ge(lo_ready, 2 * n + 2)
                            pe.wait_ge(t2_ready, n + 1)
                            for t in range(NT):
                                for c in range(KC):
                                    last = mm3(pe, tp_ps[:, t * C:(t + 1) * C], pair(act_p, slice(None), c, slice(t * P, (t + 1) * P)),
                                               pair(w["Wo"], slice(None), c, slice(None)), c == 0, c == KC - 1)
                            last.then_inc(wo_done, 1)
                        if k == 15:
                            pe.wait_ge(xn_ready, 2 * n + 2)
                            turn(xn)
                        if k == 16:
                            pe.wait_ge(a_front, 2 * KC * n + 2 * KC)
                            for t in range(NT):
                                for c in range(KC):
                                    last = pe.matmul(g_ps[:, 8 * t:8 * t + 7], fm[:, c, t * P:(t + 1) * P], wb[:, c, :],
                                                     start=(c == 0), stop=(c == KC - 1))
                            last.then_inc(bids_done, 1)

                    def iteration(t, i, n, m):
                        for k in range(NCHUNK):
                            opens = k - LAG in GROUP_START
                            if t is not None and k < LAG:
                                if k != 1:
                                    down(NCHUNK - LAG + k, t)
                                if k == 0:
                                    down(NCHUNK - LAG + 1, t)
                            if n is not None and k == 0:
                                pe.wait_ge(xn0_ready, n + 1)
                                after(pe, a_front, 2 * KC * n)
                                turn(xn0)
                            if i is not None:
                                if k >= LAG and not opens:
                                    down(k - LAG, i)
                                up(k, i)
                                if opens:
                                    down(k - LAG, i)
                            if n is not None:
                                front(k, n)
                    pipeline(pe, iteration)

                @block.vector
                def _(v):
                    for t in range(NT):
                        v.tensor_copy(cap4[:, t, :], cap)
                    v.memset(tmax[:, :], 0.0)

                    def chunk(c, i):
                        up = up_ps[:, (c % 2) * T:(c % 2 + 1) * T]
                        sq = hr_sq[:, c % 2, :]
                        if c < 2:
                            v.wait_ge(up_done, NCHUNK * i + c + 1)
                            v.wait_ge(t2_ready, i + 1)
                            v.scalar_tensor_tensor(out=sq, in0=t2[:, c, :], scalar=1.0, in1=up, op0=ALU.add, op1=ALU.mult).then_inc(sq_done, 1)
                        else:
                            v.wait_ge(relu_done, (NCHUNK - 2) * i + c - 1)
                            v.tensor_tensor(sq, hr_r[:, c % 3, :], hr_r[:, c % 3, :], ALU.mult).then_inc(sq_done, 1)
                        v.wait_ge(hr_hi_done, NCHUNK * i + c + 1)
                        v.wait_ge(sq_done, NCHUNK * i + c + 1)
                        v.tensor_tensor(hr_p[1][:, c % RING, :], sq, hr_p[0][:, c % RING, :].bitcast(F32), ALU.subtract).then_inc(hr_lo_done, 1)

                    def evacuate(c, i):
                        order = GROUP_END[c]
                        e = GROUP_EXPERT[order]
                        v.wait_ge(down_done, NCHUNK * i + c + 1)
                        v.wait_ge(xacc_ready, i + 1)
                        if order == 0:
                            v.wait_ge(coef_ready, i + 1)
                        else:
                            v.wait_ge(evac_done, 3 * i + order)
                        if order == 2:
                            after(v, x3_stored, 16 * i)
                            after(v, text_ready, i)
                        dst = x3 if order == 2 else xacc
                        for t in range(NT):
                            last = v.scalar_tensor_tensor(out=dst[:, t, :], in0=out_ps[:, t * C:(t + 1) * C], scalar=coef[:, t, e:e + 1],
                                                          in1=xacc[:, t, :], op0=ALU.mult, op1=ALU.add)
                        last.then_inc(evac_done, 1)

                    def first_ln(k, m, st):
                        if k == 9:
                            v.wait_ge(x_loaded, 16 * m + 16)
                            stats(st, x_in, stat0, mean0, var0, vtmp0, ve0_ready)
                        if k == 15:
                            v.wait_ge(rs0_ready, m + 1)
                            after(v, turned, 3 * m - 2)
                            for t in range(NT):
                                last = v.tensor_scalar(xn0[:, t, :], x_in[:, t, :], mean0[:, t:t + 1], rs0[:, t:t + 1], ALU.subtract, ALU.mult)
                            last.then_inc(xn0_ready, 1)

                    def front(k, n, st):
                        if k == 2:
                            v.wait_ge(scores_done, n + 1)
                            sc = g_ps[:, 0:NT * S].rearrange("p (t s) -> p t s", s=S)
                            sc4 = g_ps[:, 0:NT * S].rearrange("p (h j s) -> p h j s", h=2, s=S)
                            mx4 = smax[:, :].rearrange("p (h j) -> p h j", h=2).unsqueeze(3).broadcast_to([P, 2, NT // 2, S])
                            st.link(v.tensor_reduce(smax[:, :], sc, X, ALU.max))
                            after(v, probs_turned, n)
                            v.tensor_tensor(probs[:, :, :, :].rearrange("p j h s -> p h j s"), sc4, mx4, ALU.subtract).then_inc(shifted, 1)
                        if k == 3:
                            v.wait_ge(exp_done, n + 1)
                            st.link(v.tensor_reduce(ssum[:, :].rearrange("p (h j) -> p h j", h=2), probs[:, :, :, :].rearrange("p j h s -> p h j s"), X, ALU.add))
                            st.link(v.reciprocal(ssum[:, :], ssum[:, :]))
                        if k == 5:
                            v.wait_ge(pv_done, n + 1)
                            after(v, xacc_ready, n)
                            for t in range(NT):
                                last = v.scalar_tensor_tensor(out=x1[:, t, :], in0=g_ps[:, t * C:(t + 1) * C], scalar=ssum[:, t:t + 1],
                                                              in1=x_in[:, t, :], op0=ALU.mult, op1=ALU.add)
                            last.then_inc(x1_ready, 1)
                            v.wait_ge(x1_ready, n + 1)
                            after(v, x2ln_ready, n)
                            stats(st, x1, stat, mean, var1[:, 0, :], vtmp, None)
                            st.add(v.tensor_scalar(vtmp[:, :], var1[:, 0, :], EPS, None, ALU.subtract))
                            st.link(v.reciprocal(nmr[:, :], var1[:, 0, :]))
                            st.link(v.tensor_tensor(var1[:, 1, :], vtmp[:, :], nmr[:, :], ALU.mult))
                            v.tensor_scalar(var1[:, 1, :], var1[:, 1, :], EPS, None, ALU.add).then_inc(ve1_ready, 1)
                        if k == 6:
                            v.wait_ge(rs1_ready, n + 1)
                            st.add(v.tensor_tensor(vtmp[:, :], rs1[:, 0, :], rs1[:, 1, :], ALU.mult))
                            v.scalar_tensor_tensor(out=nmr[:, :], in0=mean[:, :], scalar=-1.0, in1=rs1[:, 0, :], op0=ALU.mult, op1=ALU.mult).then_inc(nmr_ready, 1)
                            st.wait()
                            after(v, turned, 3 * n)
                            for t in range(NT):
                                last = v.tensor_scalar(xn[:, t, :], x1[:, t, :], mean[:, t:t + 1], vtmp[:, t:t + 1], ALU.subtract, ALU.mult)
                            last.then_inc(xn_ready, 1)
                        if k == 8:
                            v.wait_ge(hi_ready, 2 * n + 1)
                            v.tensor_tensor(act_p[1][:, :, :], fm[:, :, :], act_p[0][:, :, :].bitcast(F32), ALU.subtract).then_inc(lo_ready, 1)
                        if k == 11:
                            v.wait_ge(wv_done, n + 1)
                            v.scalar_tensor_tensor(out=flat(fm), in0=flat(t1), scalar=1.0, in1=g_ps[:, :], op0=ALU.add, op1=ALU.mult).then_inc(g_ready, 1)
                            v.wait_ge(hi_ready, 2 * n + 2)
                            v.tensor_tensor(act_p[1][:, :, :], fm[:, :, :], act_p[0][:, :, :].bitcast(F32), ALU.subtract).then_inc(lo_ready, 1)
                        if k == 13:
                            v.wait_ge(wo_done, n + 1)
                            v.wait_ge(x2ln_ready, n + 1)
                            v.tensor_tensor(flat(x2), flat(x2), tp_ps[:, :], ALU.add).then_inc(x2_ready, 1)
                            v.wait_ge(x2_ready, n + 1)
                            v.wait_ge(xn_ready, 2 * n + 1)
                            stats(st, x2, stat, mean, var, vtmp, ve_ready)
                        if k == 14:
                            v.wait_ge(rs_ready, n + 1)
                            for t in range(NT):
                                last = v.tensor_scalar(xn[:, t, :], x2[:, t, :], mean[:, t:t + 1], rs[:, t:t + 1], ALU.subtract, ALU.mult)
                            last.then_inc(xn_ready, 1)

                    def bids(n):
                        st = Steps(v, v_bids, KB * n)
                        v.wait_ge(bexp_done, n + 1)
                        after(v, coef_ready, n)
                        conf = sig[:, :, 0:3]
                        ee = lambda m, q: m[:, :, q:q + 1]
                        st.link(v.tensor_scalar(sig[:, :, :], sig[:, :, :], 1.0, None, ALU.add))
                        st.link(v.reciprocal(sig[:, :, :], sig[:, :, :]))
                        st.add(v.tensor_tensor(bid[:, :, :], conf, cap4[:, :, :], ALU.mult))
                        st.link(v.tensor_scalar(btmp[:, :, :], conf, 1e-6, None, ALU.add))
                        st.link(v.tensor_tensor(bid[:, :, :], bid[:, :, :], ee(sig, 3).broadcast_to([P, NT, 3]), ALU.mult))
                        aff = g_ps[:, 0:8 * NT].rearrange("p (t e) -> p t e", e=8)[:, :, 4:7]
                        st.add(v.tensor_tensor(bid[:, :, :], bid[:, :, :], aff, ALU.add))
                        st.link(v.reciprocal(btmp[:, :, :], btmp[:, :, :]))
                        st.add(v.tensor_tensor(btmp[:, :, :], btmp[:, :, :], conf, ALU.mult))
                        st.add(v.tensor_tensor(ee(hot, 0), ee(bid, 1), ee(bid, 2), ALU.max))
                        st.link(v.tensor_tensor(ee(hot, 2), ee(bid, 0), ee(bid, 1), ALU.max))
                        st.add(v.tensor_tensor(ee(hot, 0), ee(bid, 0), ee(hot, 0), ALU.is_ge))
                        st.link(v.tensor_tensor(ee(hot, 2), ee(bid, 2), ee(hot, 2), ALU.is_gt))
                        st.link(v.tensor_tensor(ee(hot, 1), ee(hot, 0), ee(hot, 2), ALU.add))
                        v.tensor_scalar(ee(hot, 1), ee(hot, 1), -1.0, 1.0, ALU.mult, ALU.add).then_inc(bid_ready, 1)
                        assert st.n == KB, st.n

                    def tail(k, t, st):
                        if k == 9:
                            v.wait_ge(evac_done, 3 * t + 3)
                            stats(st, x3, stat3, mean3, var3, vtmp3, ve3_ready)
                        if k == 11:
                            v.wait_ge(rs3_ready, t + 1)
                            v.scalar_tensor_tensor(out=nmr3[:, :], in0=mean3[:, :], scalar=-1.0, in1=rs3[:, :], op0=ALU.mult, op1=ALU.mult).then_inc(nmr3_ready, 1)
                        if k == 14:
                            v.wait_ge(text_ready, t + 1)
                            v.tensor_reduce(tcur[:, :], text[:, :, :], XY, ALU.max, apply_absolute_value=True).then_inc(text_seen, 1)
                            v.wait_ge(text_seen, t + 1)
                            st.link(v.tensor_tensor(tmax[:, :], tmax[:, :], tcur[:, :], ALU.max))

                    def iteration(t, i, n, m):
                        st = Steps(v, v_front, 0 if n is None else KF * n)
                        st0 = Steps(v, v_first, 0 if m is None else K0 * m)
                        stt = Steps(v, v_tail, 0 if t is None else KT * t)
                        for k in range(NCHUNK):
                            if n is not None:
                                front(k, n, st)
                            if k == 2:
                                if t is not None:
                                    evacuate(NCHUNK - 1, t)
                                if i is not None:
                                    v.wait_ge(bid_ready, i + 1)
                                    after(v, evac_done, 3 * i)
                                    v.tensor_tensor(coef[:, :, :], btmp[:, :, :], hot[:, :, :], ALU.mult).then_inc(coef_ready, 1)
                            if i is not None and k - LAG in GROUP_END:
                                evacuate(k - LAG, i)
                            if i is not None:
                                chunk(k, i)
                            if m is not None:
                                first_ln(k, m, st0)
                            if t is not None:
                                tail(k, t, stt)
                        if n is not None:
                            v.wait_ge(h_hi_ready, n + 1)
                            v.tensor_tensor(h_p[1][:, :, :], fm[:, :, :], h_p[0][:, :, :].bitcast(F32), ALU.subtract).then_inc(h_ready, 1)
                            bids(n)
                            assert st.n == KF, st.n
                        assert (t is None or stt.n == KT) and (m is None or st0.n == K0), (stt.n, st0.n)
                    pipeline(v, iteration)
            stack.pop()

        kv_scope.close()
        stack.pop()

        scale_max, scale_steps = sem("scale_max"), sem("scale_steps")
        scales_made = [0, 0]

        def scale_step(which, products, extra=None):
            with nc.Block() as block:
                @block.gpsimd
                def _(g):
                    g.partition_all_reduce(gmax[:, which:which + 1], tmax[:, :], P, RED.max).then_inc(scale_max, 1)

                @block.vector
                def _(v):
                    st = Steps(v, scale_steps, scales_made[1])
                    scales_made[0] += 1
                    v.wait_ge(scale_max, scales_made[0])
                    st.link(v.tensor_scalar(iscale[:, which:which + 1], gmax[:, which:which + 1], 1e-8, 1.0 / 127.0, ALU.max, ALU.mult))
                    st.add(v.reciprocal(inv[:, which:which + 1], iscale[:, which:which + 1]))
                    for o, wk, ak in products:
                        st.add(v.tensor_tensor(oscale[:, o:o + 1], wscale[:, wk:wk + 1], iscale[:, ak:ak + 1], ALU.mult))
                    st.wait()
                    if extra is not None:
                        extra(v, st)
                    scales_made[1] += st.n
                    v.memset(tmax[:, :], 0.0)

        def first_then_loop(eng, body, n):
            body(0)
            with eng.Fori(1, n) as j:
                body(j)

        ff_scope = ExitStack()
        stack.append(ff_scope)
        ff = sb("ff", [P, B, KC, T])

        scale_step(A_TXT, [(O_TXT, W_TXT, A_TXT)])

        L = 4
        GROUPS = (GA, GB) = ((0, 1), (2, 3))
        with ExitStack() as scope:
            stack.append(scope)
            tx = [sb(f"tx{l}", [P, NT, C]) for l in range(L)]
            qt = [sb(f"qt{l}", [P, NT, C], BF16) for l in range(L)]
            qc = [sb(f"qc{l}", [P, KC, T], BF16) for l in range(L)]
            f = [sb(f"f{l}", [P, KC, T]) for l in range(L)]
            fs = [sb(f"fs{l}", [P, T]) for l in range(L)]
            pr = [sb(f"pr{l}", [P, NT // 2, 2, S]) for l in range(L)]
            prt = [sb(f"prt{l}", [P, NT // 2, P]) for l in range(L)]
            kv = [sb(f"kv{l}", [P, 2, S]) for l in range(L)]
            kvt = [sb(f"kvt{l}", [P, 2, P]) for l in range(L)]
            mx = [sb(f"mx{l}", [P, NT]) for l in range(L)]
            sm = [sb(f"sm{l}", [P, NT]) for l in range(L)]
            cur = [sb(f"cur{l}", [P, 1]) for l in range(L)]
            tx_loaded, kv_loaded, f_stored = ([sem(f"att_{n}{l}") for l in range(L)] for n in ("tx_loaded", "kv_loaded", "f_stored"))
            (quant_done, q_turned, qc_ready, txt_done, f_ready, fs_ready, sc_done, sc_shifted,
             e_done, norm_done, e_turned, prt_ready, o_done, f_updated, f_seen, v_att_a, v_att_b) = (sem("att_" + n) for n in (
                 "quant_done", "q_turned", "qc_ready", "txt_done", "f_ready", "fs_ready",
                 "scores_done", "shifted", "exp_done", "norm_done", "probs_turned", "probs_t_ready", "o_done",
                 "f_updated", "f_seen", "dve_a", "dve_b"))
            t_v = text_dram.rearrange("b (t p) c -> b p t c", p=P)
            NJ = B // L
            KV_ = 16

            def bank4(l):
                return psum[l][:, :].rearrange("p (h n) -> p h n", h=2)[:, :, 0:2 * P]

            def tok4(ap):
                return ap.rearrange("p (h n) -> p h n", h=2)

            def use(j, l, a_):
                first, last = isinstance(j, int) and j == 0, isinstance(j, int) and j == NJ - 1
                if l in GA:
                    at = 2 * L * j + 2 if a_ else (0 if first else 2 * L * j - 2)
                else:
                    at = 2 * L * j + L if a_ == 0 else 2 * L * j + (2 * L - 2 if last else 2 * L)
                return at + l % 2

            def after_last_use(eng, sem_, j, l, a_):
                if a_:
                    eng.wait_ge(sem_, use(j, l, 0) + 1)
                elif not (isinstance(j, int) and j == 0):
                    at = 2 * L * (j - 1) + 2 if l in GA else 2 * L * j
                    eng.wait_ge(sem_, at + l % 2 + 1)

            def turns(eng, turn):
                turn(0, True, False)
                with eng.Fori(1, NJ - 1) as j:
                    turn(j, True, True)
                turn(NJ - 1, True, True)
                turn(NJ, False, True)

            def work(j, now, before, plan):
                for piece, group, *rest in plan:
                    if group == "B-":
                        if before:
                            piece(j - 1, GB, *rest)
                    elif group == "A+":
                        if now and not (isinstance(j, int) and j == NJ - 1):
                            piece(j + 1, GA, *rest)
                    elif now:
                        piece(j, GA if group == "A" else GB, *rest)

            with nc.Block() as block:
                @block.sync
                def _(sp):
                    def text(j, lanes):
                        for l in lanes:
                            after(sp, quant_done, L * j + l + 1 - L)
                            sp.dma_start(tx[l][:, :, :], one(t_v, L * j + l)).then_inc(tx_loaded[l], 16)

                    def keys(j, lanes):
                        for l in lanes:
                            n = L * j + l
                            after_last_use(sp, o_done, j, l, 0)
                            sp.dma_start(kv[l][:, :, :].rearrange("p a s -> p (a s)"), one2(kv_dram, n)).then_inc(kv_loaded[l], 16)
                            for h in range(2):
                                sp.dma_start(kvt[l][h * S:(h + 1) * S, :, :].rearrange("p a f -> p (a f)"), one2(kvt_dram, n)).then_inc(kv_loaded[l], 16)

                    def store(j, lanes):
                        for l in lanes:
                            sp.wait_ge(f_updated, use(j, l, 1) + 1)
                            sp.dma_start(ff[:, bass.ds(L * j + l, 1), :, :].rearrange("p o k t -> p (o k t)"),
                                         f[l][:, :, :].rearrange("p k t -> p (k t)")).then_inc(f_stored[l], 16)

                    def turn(j, now, before):
                        if now:
                            text(j, GB)
                            if not (isinstance(j, int) and j == NJ - 1):
                                text(j + 1, GA)
                            keys(j, GB)
                        if before:
                            store(j - 1, GB)
                        if now:
                            if not (isinstance(j, int) and j == NJ - 1):
                                keys(j + 1, GA)
                            store(j, GA)
                    text(0, GA)
                    keys(0, GA)
                    turns(sp, turn)
                    for l in range(L):
                        sp.wait_ge(f_stored[l], 16 * NJ)

                @block.gpsimd
                def _(g):
                    def folded(j, lanes, a_):
                        for l in lanes:
                            if a_ == 0:
                                g.wait_ge(f_ready, L * j + l + 1)
                                after_last_use(g, sc_done, j, l, 0)
                            else:
                                g.wait_ge(f_updated, use(j, l, 0) + 1)
                            g.tensor_tensor(fs[l][:, :], f[l][:, 0, :], f[l][:, 1, :], ALU.add).then_inc(fs_ready, 1)
                    turns(g, lambda j, now, before: work(j, now, before, [
                        (folded, "A", 0), (folded, "B-", 1), (folded, "A", 1), (folded, "B", 0)]))

                @block.scalar
                def _(s):
                    def turned_text(j, lanes):
                        for l in lanes:
                            n = L * j + l
                            s.wait_ge(q_turned, n + 1)
                            after(s, txt_done, n + 1 - L)
                            s.activation(qc[l][:, :, :].rearrange("p k t -> p (k t)"), psum[l][:, 0:T].bitcast(BF16), ACT.Copy).then_inc(qc_ready, 1)

                    def fused(j, lanes):
                        for l in lanes:
                            s.wait_ge(txt_done, L * j + l + 1)
                            after(s, f_stored[l], 16 * j)
                            after(s, f_seen, L * j + l + 1 - L)
                            for c in range(KC):
                                last = s.activation(f[l][:, c, :], psum[l][:, c * T:(c + 1) * T], ACT.Identity, bias=col("b_txt", c),
                                                    scale=oscale[:, O_TXT:O_TXT + 1])
                            last.then_inc(f_ready, 1)

                    def exp(j, lanes, a_):
                        for l in lanes:
                            s.wait_ge(sc_shifted, use(j, l, a_) + 1)
                            s.activation(pr[l][:, :, :, :], pr[l][:, :, :, :], ACT.Exp, scale=INV_SQRT).then_inc(e_done, 1)

                    def turned_probs(j, lanes, a_):
                        for l in lanes:
                            s.wait_ge(e_turned, use(j, l, a_) + 1)
                            after_last_use(s, o_done, j, l, a_)
                            s.activation(prt[l][:, :, :].rearrange("p j t -> p (j t)"), psum[l][:, 0:2 * P], ACT.Copy).then_inc(prt_ready, 1)
                    turns(s, lambda j, now, before: work(j, now, before, [
                        (exp, "B-", 0), (turned_text, "A"), (turned_probs, "B-", 0), (fused, "A"), (exp, "A", 0),
                        (exp, "B-", 1), (turned_probs, "A", 0), (turned_probs, "B-", 1), (turned_text, "B"),
                        (exp, "A", 1), (fused, "B"), (turned_probs, "A", 1)]))

                @block.tensor
                def _(pe):
                    def turn_text(j, lanes):
                        for l in lanes:
                            pe.wait_ge(quant_done, L * j + l + 1)
                            after_last_use(pe, f_updated, j, l, 0)
                            qp = psum[l][:, 0:T].bitcast(BF16)
                            for c in range(KC):
                                for t in range(NT):
                                    last = pe.transpose(qp[:, c * T + t * P:c * T + (t + 1) * P], qt[l][:, t, c * P:(c + 1) * P], ident_b[:, :])
                            last.then_inc(q_turned, 1)

                    def linear(j, lanes):
                        for l in lanes:
                            pe.wait_ge(qc_ready, L * j + l + 1)
                            for c in range(KC):
                                for k in range(KC):
                                    last = pe.matmul(psum[l][:, c * T:(c + 1) * T], wtxt[:, k, c * P:(c + 1) * P], qc[l][:, k, :],
                                                     start=(k == 0), stop=(k == KC - 1))
                            last.then_inc(txt_done, 1)

                    def scores(j, lanes, a_):
                        for l in lanes:
                            if a_ == 0:
                                pe.wait_ge(kv_loaded[l], 48 * j + 48)
                            pe.wait_ge(fs_ready, use(j, l, a_) + 1)
                            for t in range(NT):
                                last = pe.matmul(psum[l][:, t * S:(t + 1) * S], fs[l][:, t * P:(t + 1) * P], kv[l][:, a_, :], start=True, stop=True)
                            last.then_inc(sc_done, 1)

                    def turn_probs(j, lanes, a_):
                        for l in lanes:
                            pe.wait_ge(norm_done, use(j, l, a_) + 1)
                            for q in range(NT // 2):
                                last = pe.transpose(psum[l][:, q * P:(q + 1) * P], pr[l][:, q, :, :].rearrange("p h s -> p (h s)"), ident[:, :])
                            last.then_inc(e_turned, 1)

                    def output(j, lanes, a_):
                        for l in lanes:
                            pe.wait_ge(prt_ready, use(j, l, a_) + 1)
                            for q in range(NT // 2):
                                for h in range(2):
                                    half = slice(h * S, (h + 1) * S)
                                    last = pe.matmul(psum[l][:, h * T + q * P:h * T + (q + 1) * P], kvt[l][half, a_, :],
                                                     prt[l][half, q, :], start=True, stop=True)
                            last.then_inc(o_done, 1)
                    turns(pe, lambda j, now, before: work(j, now, before, [
                        (turn_text, "A"), (turn_probs, "B-", 0), (linear, "A"), (output, "B-", 0), (scores, "A", 0),
                        (scores, "B-", 1), (turn_probs, "A", 0), (output, "A", 0), (turn_probs, "B-", 1),
                        (output, "B-", 1), (scores, "A", 1), (turn_text, "B"), (linear, "B"), (turn_probs, "A", 1),
                        (output, "A", 1), (scores, "B", 0)]))

                @block.vector
                def _(v):
                    def steps(j, lanes, at):
                        return Steps(v, v_att_a if lanes is GA else v_att_b, KV_ * j + at)

                    def quantise(j, lanes):
                        st = steps(j, lanes, 0 if isinstance(j, int) and j == 0 else -2)
                        for l in lanes:
                            v.wait_ge(tx_loaded[l], 16 * j + 16)
                            st.add(v.tensor_scalar(tx[l][:, :, :], tx[l][:, :, :], inv[:, A_TXT:A_TXT + 1], ROUND, ALU.mult, ALU.add))
                        st.wait()
                        for l in lanes:
                            after(v, q_turned, L * j + l + 1 - L)
                            v.tensor_scalar(qt[l][:, :, :], tx[l][:, :, :], ROUND, None, ALU.subtract).then_inc(quant_done, 1)

                    def shift(j, lanes, a_):
                        st = steps(j, lanes, 2 + 6 * a_)
                        for l in lanes:
                            v.wait_ge(sc_done, use(j, l, a_) + 1)
                            st.add(v.tensor_reduce(mx[l][:, :], psum[l][:, 0:NT * S].rearrange("p (t s) -> p t s", s=S), X, ALU.max))
                        st.wait()
                        for l in lanes:
                            after_last_use(v, e_turned, j, l, a_)
                            v.tensor_tensor(pr[l][:, :, :, :].rearrange("p j h s -> p h j s"),
                                            psum[l][:, 0:NT * S].rearrange("p (h j s) -> p h j s", h=2, s=S),
                                            mx[l][:, :].rearrange("p (h j) -> p h j", h=2).unsqueeze(3).broadcast_to([P, 2, NT // 2, S]),
                                            ALU.subtract).then_inc(sc_shifted, 1)

                    def normalise(j, lanes, a_):
                        st = steps(j, lanes, 4 + 6 * a_)
                        for l in lanes:
                            v.wait_ge(e_done, use(j, l, a_) + 1)
                            st.add(v.tensor_reduce(sm[l][:, :].rearrange("p (j h) -> p j h", h=2), pr[l][:, :, :, :], X, ALU.add))
                        st.wait()
                        for l in lanes:
                            st.add(v.reciprocal(sm[l][:, :], sm[l][:, :]))
                        st.wait()
                        for l in lanes:
                            v.tensor_tensor(pr[l][:, :, :, :], pr[l][:, :, :, :],
                                            sm[l][:, :].rearrange("p (j h) -> p j h", h=2).unsqueeze(3).broadcast_to([P, NT // 2, 2, S]),
                                            ALU.mult).then_inc(norm_done, 1)

                    def update(j, lanes, a_):
                        for l in lanes:
                            v.wait_ge(o_done, use(j, l, a_) + 1)
                            for c in range(KC):
                                last = v.scalar_tensor_tensor(out=tok4(f[l][:, c, :]), in0=bank4(l), scalar=0.1, in1=tok4(f[l][:, c, :]),
                                                              op0=ALU.mult, op1=ALU.add)
                            last.then_inc(f_updated, 1)

                    def largest(j, lanes):
                        st = steps(j, lanes, 14 if isinstance(j, int) and j == NJ - 1 else 16)
                        for l in lanes:
                            v.wait_ge(f_updated, use(j, l, 1) + 1)
                            v.tensor_reduce(cur[l][:, :], f[l][:, :, :], XY, ALU.max, apply_absolute_value=True).then_inc(f_seen, 1)
                        for l in lanes:
                            v.wait_ge(f_seen, L * j + l + 1)
                            st.link(v.tensor_tensor(tmax[:, :], tmax[:, :], cur[l][:, :], ALU.max))
                    quantise(0, GA)
                    turns(v, lambda j, now, before: work(j, now, before, [
                        (shift, "B-", 0), (normalise, "B-", 0), (update, "B-", 0), (shift, "A", 0), (normalise, "A", 0),
                        (shift, "B-", 1), (normalise, "B-", 1), (update, "A", 0), (quantise, "B"), (update, "B-", 1),
                        (shift, "A", 1), (largest, "B-"), (normalise, "A", 1), (quantise, "A+"), (update, "A", 1),
                        (largest, "A")]))
                    st = Steps(v, v_att_a, KV_ * NJ)
                    st.link(v.tensor_reduce(tcur[:, :], avg[:, :, :], XY, ALU.max, apply_absolute_value=True))
                    st.link(v.tensor_tensor(tmax[:, :], tmax[:, :], tcur[:, :], ALU.max))
            stack.pop()

        qf = sb("qf", [P, B, KC, T], BF16)
        lw = {n: (sb(n + "_hi", [P, KC, C], F32R), sb(n + "_lo", [P, KC, C], F32R)) for n in ("rT", "kT", "vT")}
        qavg = sb("qavg", [P, KC, B], BF16)
        acc_avg = sb("acc_avg", [P, HC, B])
        hmax8, hcur = sb("hmax8", [P, HC]), sb("hcur", [P, HC])
        scale_step(A_CAT, [(O_F1, W_F1, A_CAT)])
        qy = sb("qy", [P, KC * T])
        with ExitStack() as scope:
            stack.append(scope)
            lstg = sb("lstg", [P, 3, KC, C])
            l_loaded, qavg_ready, acc_done, acc_ready, v_hid = (sem(n) for n in ("l1_loaded", "qavg_ready", "acc_avg_done", "acc_avg_ready", "dve_hidden"))
            hy_done, hq_done, h_done, h_red = sem("hid_rounded"), sem("hid_quant"), sem("hid_f1"), sem("hid_reduced")
            neg_round = sb("neg_round", [P, 1])
            KH = 2
            with nc.Block() as block:
                @block.sync
                def _(sp):
                    for k, name in enumerate(("rT", "kT", "vT")):
                        sp.dma_start(lstg[:, k, :, :], a[name].rearrange("(k p) n -> p k n", p=P)).then_inc(l_loaded, 16)

                @block.tensor
                def _(pe):
                    pe.wait_ge(qavg_ready, 1)
                    for c in range(HC):
                        for k in range(KC):
                            last = pe.matmul(psum[3][:, c * B:(c + 1) * B], wf1[:, KC + k, c * P:(c + 1) * P], qavg[:, k, :],
                                             start=(k == 0), stop=(k == KC - 1))
                    last.then_inc(acc_done, 1)
                    pe.wait_ge(acc_ready, 1)

                    def body(n):
                        for q in range(HC // 2):
                            if q == 0:
                                pe.wait_ge(hq_done, n + 1)
                            after(pe, h_red, 4 * n + q - 3)
                            for c in (2 * q, 2 * q + 1):
                                for k in range(KC):
                                    last = pe.matmul(psum[q][:, (c % 2) * T:(c % 2 + 1) * T], wf1[:, k, c * P:(c + 1) * P],
                                                     qf[:, bass.ds(n, 1), k, :].rearrange("p o t -> p (o t)"), start=(k == 0), stop=(k == KC - 1))
                            last.then_inc(h_done, 1)
                    first_then_loop(pe, body, B)

                @block.scalar
                def _(s):
                    def body(n):
                        s.wait_ge(hy_done, n + 1)
                        s.wait_ge(acc_done, 1)
                        s.activation(qf[:, bass.ds(n, 1), :, :].rearrange("p o k t -> p (o k t)"), qy[:, :],
                                     ACT.Identity, bias=neg_round[:, :]).then_inc(hq_done, 1)
                    first_then_loop(s, body, B)

                @block.vector
                def _(v):
                    st = Steps(v, v_hid)
                    st.add(v.memset(neg_round[:, :], -ROUND))
                    st.link(v.tensor_scalar(lstg_avg := qy[:, 0:KC * B].rearrange("p (k b) -> p k b", k=KC), avg[:, :, :], inv[:, A_CAT:A_CAT + 1], ROUND, ALU.mult, ALU.add))
                    v.tensor_scalar(qavg[:, :, :], lstg_avg, ROUND, None, ALU.subtract).then_inc(qavg_ready, 1)
                    st.add(v.memset(hmax8[:, :], -1e30))
                    v.wait_ge(l_loaded, 48)
                    for k, name in enumerate(("rT", "kT", "vT")):
                        hi, lo = lw[name]
                        if name == "vT":
                            st.link(v.tensor_scalar(lstg[:, k, :, :], lstg[:, k, :, :], 0.5, None, ALU.mult))
                        st.link(v.tensor_copy(hi[:, :, :], lstg[:, k, :, :]))
                        st.add(v.tensor_tensor(lo[:, :, :], lstg[:, k, :, :], hi[:, :, :].bitcast(F32), ALU.subtract))
                    v.wait_ge(acc_done, 1)
                    v.tensor_copy(acc_avg[:, :, :].rearrange("p c b -> p (c b)"), psum[3][:, 0:HC * B]).then_inc(acc_ready, 1)
                    v.wait_ge(acc_ready, 1)
                    base = st.n

                    def quant(n):
                        sel = lambda m: m[:, bass.ds(n, 1), :, :].rearrange("p o k t -> p (o k t)")
                        after(v, hq_done, n)
                        v.tensor_scalar(qy[:, :], sel(ff), inv[:, A_CAT:A_CAT + 1], ROUND, ALU.mult, ALU.add).then_inc(hy_done, 1)

                    def body(n, ahead):
                        at = base + KH * n
                        if ahead:
                            quant(n + 1)
                        v.wait_ge(v_hid, at)
                        for q in range(HC // 2):
                            v.wait_ge(h_done, 4 * n + q + 1)
                            v.tensor_reduce(hcur[:, 2 * q:2 * q + 2], psum[q][:, :].rearrange("p (c t) -> p c t", c=2), X, ALU.max).then_inc(h_red, 1)
                        v.wait_ge(h_red, 4 * n + 4)
                        v.tensor_tensor(hcur[:, :], hcur[:, :], acc_avg[:, :, bass.ds(n, 1)].rearrange("p c o -> p (c o)"), ALU.add).then_inc(v_hid, 1)
                        v.wait_ge(v_hid, at + 1)
                        v.tensor_tensor(hmax8[:, :], hmax8[:, :], hcur[:, :], ALU.max).then_inc(v_hid, 1)
                    quant(0)
                    body(0, True)
                    with v.Fori(1, B - 1) as n:
                        body(n, True)
                    body(B - 1, False)
                    end = base + KH * B
                    v.wait_ge(v_hid, end)
                    st2 = Steps(v, v_hid, end)
                    st2.link(v.tensor_scalar(hmax8[:, :], hmax8[:, :], oscale[:, O_F1:O_F1 + 1], None, ALU.mult))
                    st2.link(v.tensor_tensor(hmax8[:, :], hmax8[:, :], cols[:, COLS["b_f1"][0]:COLS["b_f1"][0] + HC], ALU.add))
                    st2.link(v.tensor_reduce(tmax[:, :], hmax8[:, :], X, ALU.max))
                    st2.link(v.tensor_scalar(tmax[:, :], tmax[:, :], 0.0, None, ALU.max))
            stack.pop()

        hb = sb("hb", [P, HC, B])
        s1h = sb("s1h", [P, 1])

        def hidden_bias(v, st):
            st.link(v.tensor_scalar(hb[:, :, :], acc_avg[:, :, :], oscale[:, O_F1:O_F1 + 1], None, ALU.mult))
            st.add(v.tensor_tensor(s1h[:, :], oscale[:, O_F1:O_F1 + 1], inv[:, A_H:A_H + 1], ALU.mult))
            st.link(v.tensor_tensor(hb[:, :, :], hb[:, :, :],
                                    cols[:, COLS["b_f1"][0]:COLS["b_f1"][0] + HC].unsqueeze(2).broadcast_to([P, HC, B]), ALU.add))
            st.link(v.tensor_scalar(hb[:, :, :], hb[:, :, :], inv[:, A_H:A_H + 1], None, ALU.mult))

        scale_step(A_H, [(O_F2, W_F2, A_H)], hidden_bias)
        DEPTH = 4
        with ExitStack() as scope:
            space = ff[:, :, :, :].rearrange("p b k t -> p (b k t)")
            used = [0]

            def view(*shape):
                n = 1
                for q in shape:
                    n *= q
                at = used[0]
                used[0] += n
                assert used[0] <= B * KC * T
                flat_ = space[:, at:at + n]
                if len(shape) == 1:
                    return flat_
                return flat_.rearrange("p (a b) -> p a b", a=shape[0])

            stack.append(scope)
            xt = [view(NT, C) for _ in range(DEPTH)]
            xnn = view(NT, C)
            zd = view(KC, T)
            xr, xk = view(KC, T), view(KC, T)
            tr = [view(NT * C) for _ in range(2)]
            kr, ks = view(KC, T), view(KC, T)
            hr4 = view(4, T)
            yo = view(NT, C)
            zz = sb("zz", [P, KC, T + 1])
            hq = [sb(f"hq{l}", [P, HC, T], BF16) for l in range(2)]
            pr_, pk, pv = ((sb(f"{q}_hi", [P, KC, T], F32R), sb(f"{q}_lo", [P, KC, T], F32R)) for q in ("mix_r", "mix_k", "k_sq"))
            hbs = [sb(f"hbs{l}", [P, HC]) for l in range(2)]
            st6 = sb("st6", [P, NT, 6])
            me, va, vt, rr, nm = (sb("fin_" + q, [P, NT]) for q in ("mean", "var", "vtmp", "rs", "nmr"))
            fl_ = lambda ap: ap.rearrange("p a b -> p (a b)")
            xt_loaded, y_stored = ([sem(f"fin_{q}{l}") for l in range(DEPTH)] for q in ("x_loaded", "y_stored"))
            (hbs_ready, f1_done, hrelu_done, hround_done, f2_done, xb_ready, x4_ready, ve4, rs4, nm_ready, xn4, z_turned, z_ready,
             zd_ready, mix_done, rk_hi, rk_lo, v_hi, v_lo, rk_done, tr_ready, kr_ready, ksq_ready,
             v_done, y_ready, yo_done, v_fin) = (sem("fin_" + q) for q in (
                 "hbs_ready", "f1_done", "relu_done", "round_done", "f2_done", "xb_ready", "x4_ready", "ve", "rs", "nmr_ready",
                 "xn", "z_turned", "z_ready", "zd_ready", "mix_done", "mix_hi", "mix_lo",
                 "ksq_hi", "ksq_lo", "receptance_key_done", "tanh_ready", "krelu_ready", "ksq_ready", "v_done", "y_ready",
                 "yo_done", "dve"))
            out_v = out.rearrange("b (t p) c -> b p t c", p=P)
            x3r_v = x3_dram.rearrange("b (t p) c -> b p t c", p=P)
            KF3 = 10
            f1_ps, f2k_ps, v_ps, rz_ps = psum

            def pipeline3(eng, iteration):
                for i in range(DEPTH):
                    iteration(i, i, 0)
                with eng.Fori(1, B // DEPTH) as j:
                    for l in range(DEPTH):
                        iteration(DEPTH * j + l, l, j)
                for i in range(B, B + 3):
                    iteration(i, i % DEPTH, B // DEPTH)

            def batch(i, l, d, piece):
                b = i - d if d else i
                if not isinstance(b, int) or 0 <= b < B:
                    piece(b, (l - d) % DEPTH)

            with nc.Block() as block:
                @block.sync
                def _(sp):
                    def load(b, l):
                        sp.dma_start(xt[l], one(x3r_v, b)).then_inc(xt_loaded[l], 16)

                    def store(b, l):
                        sp.wait_ge(y_ready, b + 1)
                        sp.dma_start(one(out_v, b), xt[l]).then_inc(y_stored[l], 16)

                    def round_(j, more=True):
                        for l in range(DEPTH):
                            store(DEPTH * j + l, l)
                            if more:
                                sp.wait_ge(y_stored[l], 16 * j + 16)
                                load(DEPTH * j + l + DEPTH, l)
                    for l in range(DEPTH):
                        load(l, l)
                    round_(0)
                    with sp.Fori(1, B // DEPTH - 1) as j:
                        round_(j)
                    round_(B // DEPTH - 1, more=False)
                    for l in range(DEPTH):
                        sp.wait_ge(y_stored[l], 16 * (B // DEPTH))

                @block.gpsimd
                def _(g):
                    def iteration(i, l, j):
                        def z_steps(b, _):
                            g.wait_ge(z_ready, b + 1)
                            g.tensor_tensor(zd, zz[:, :, 1:T + 1], zz[:, :, 0:T], ALU.subtract).then_inc(zd_ready, 1)

                        def rstd(b, _):
                            g.wait_ge(ve4, b + 1)
                            g.tensor_tensor(rr[:, :], va[:, :], neg_half[:, :], ALU.pow).then_inc(rs4, 1)

                        def bias(b, l_):
                            g.wait_ge(xt_loaded[l_], 16 * j + 16)
                            g.tensor_tensor(xt[l_], xt[l_], bf2_row.unsqueeze(1).broadcast_to([P, NT, C]), ALU.add).then_inc(xb_ready, 1)

                        def residual(b, l_):
                            g.wait_ge(yo_done, b + 1)
                            g.tensor_tensor(xt[l_], yo, xt[l_], ALU.add).then_inc(y_ready, 1)
                        batch(i, l, 2, z_steps)
                        batch(i, l, 1, rstd)
                        batch(i, l, 0, bias)
                        batch(i, l, 3, residual)
                    pipeline3(g, iteration)

                @block.scalar
                def _(s):
                    def iteration(i, l, _):
                        def relu(*chunks):
                            def piece(b, l_):
                                for c in chunks:
                                    s.wait_ge(f1_done, HC * b + c + 1)
                                    if c == 0:
                                        s.wait_ge(hbs_ready, b + 1)
                                    after(s, hround_done, HC * b + c - 3)
                                    s.activation(hr4[:, c % 4, :], f1_ps[:, (c % 2) * T:(c % 2 + 1) * T], ACT.Relu,
                                                 bias=hbs[l_ % 2][:, c:c + 1], scale=s1h[:, :]).then_inc(hrelu_done, 1)
                            return piece

                        def z_out(b, _):
                            s.wait_ge(z_turned, b + 1)
                            after(s, mix_done, 2 * b)
                            s.activation(zz[:, :, 1:T + 1], rz_ps[:, :].rearrange("p (k t) -> p k t", k=KC), ACT.Copy).then_inc(z_ready, 1)

                        def r_high(b, _):
                            s.wait_ge(mix_done, 2 * b + 1)
                            after(s, rk_done, 2 * b - 1)
                            s.activation(pr_[0][:, :, :], xr, ACT.Copy).then_inc(rk_hi, 1)

                        def k_high(b, _):
                            s.wait_ge(mix_done, 2 * b + 2)
                            after(s, rk_done, 2 * b)
                            s.activation(pk[0][:, :, :], xk, ACT.Copy).then_inc(rk_hi, 1)

                        def ln(b, l_):
                            s.wait_ge(nm_ready, b + 1)
                            after(s, z_turned, b)
                            for t in range(NT):
                                last = s.activation(xnn[:, t, :], xt[l_][:, t, :], ACT.Identity, bias=nm[:, t:t + 1], scale=rr[:, t:t + 1])
                            last.then_inc(xn4, 1)

                        def tanh(b, l_):
                            s.wait_ge(rk_done, 2 * b + 1)
                            after(s, yo_done, b - 1)
                            s.activation(tr[l_ % 2], rz_ps[:, :], ACT.Tanh, scale=0.5).then_inc(tr_ready, 1)

                        def key_relu(b, _):
                            s.wait_ge(rk_done, 2 * b + 2)
                            after(s, ksq_ready, b)
                            s.activation(fl_(kr), f2k_ps[:, :], ACT.Relu).then_inc(kr_ready, 1)

                        def key_high(b, _):
                            s.wait_ge(kr_ready, b + 1)
                            after(s, v_done, b)
                            s.activation(pv[0][:, :, :], kr, ACT.Square).then_inc(v_hi, 1)
                        batch(i, l, 2, z_out)
                        batch(i, l, 0, relu(0, 1))
                        batch(i, l, 2, r_high)
                        batch(i, l, 0, relu(2, 3))
                        batch(i, l, 2, k_high)
                        batch(i, l, 0, relu(4, 5))
                        batch(i, l, 2, tanh)
                        batch(i, l, 0, relu(6, 7))
                        batch(i, l, 1, ln)
                        batch(i, l, 2, key_relu)
                        batch(i, l, 2, key_high)
                    pipeline3(s, iteration)

                @block.tensor
                def _(pe):
                    sl = slice(None)

                    def iteration(i, l, _):
                        def f1(*chunks):
                            def piece(b, _):
                                for c in chunks:
                                    after(pe, hrelu_done, HC * b + c - 1)
                                    for k in range(KC):
                                        last = pe.matmul(f1_ps[:, (c % 2) * T:(c % 2 + 1) * T], wf1[:, k, c * P:(c + 1) * P],
                                                         qf[:, bass.ds(b, 1), k, :].rearrange("p o t -> p (o t)"), start=(k == 0), stop=(k == KC - 1))
                                    last.then_inc(f1_done, 1)
                            return piece

                        def f2(b, l_):
                            pe.wait_ge(hround_done, HC * b + HC)
                            after(pe, kr_ready, b - 1)
                            for t in range(NT):
                                for c in range(HC):
                                    last = pe.matmul(f2k_ps[:, t * C:(t + 1) * C], hq[l_ % 2][:, c, t * P:(t + 1) * P], wf2[:, c, :],
                                                     start=(c == 0), stop=(c == HC - 1))
                            last.then_inc(f2_done, 1)

                        def turn(b, _):
                            pe.wait_ge(xn4, b + 1)
                            after(pe, tr_ready, b)
                            for c in range(KC):
                                for t in range(NT):
                                    last = pe.transpose(rz_ps[:, c * T + t * P:c * T + (t + 1) * P], xnn[:, t, c * P:(c + 1) * P], ident[:, :])
                            last.then_inc(z_turned, 1)

                        def by_token(dst, act_, name, done):
                            for t in range(NT):
                                for k in range(KC):
                                    last = mm3(pe, dst[:, t * C:(t + 1) * C], pair(act_, sl, k, slice(t * P, (t + 1) * P)),
                                               pair(lw[name], sl, k, sl), k == 0, k == KC - 1)
                            last.then_inc(done, 1)

                        def receptance(b, _):
                            pe.wait_ge(rk_lo, 2 * b + 1)
                            by_token(rz_ps, pr_, "rT", rk_done)

                        def key(b, _):
                            pe.wait_ge(rk_lo, 2 * b + 2)
                            if not isinstance(b, int) or b + 1 < B:
                                pe.wait_ge(x4_ready, b + 2)
                            for c in range(KC):
                                for k in range(KC):
                                    last = mm3(pe, f2k_ps[:, c * T:(c + 1) * T], pair(lw["kT"], sl, k, slice(c * P, (c + 1) * P)),
                                               pair(pk, sl, k, sl), k == 0, k == KC - 1)
                            last.then_inc(rk_done, 1)

                        def value(b, _):
                            pe.wait_ge(v_lo, b + 1)
                            after(pe, yo_done, b)
                            by_token(v_ps, pv, "vT", v_done)
                        batch(i, l, 0, f1(0, 1))
                        batch(i, l, 1, f2)
                        batch(i, l, 0, f1(2, 3))
                        batch(i, l, 3, value)
                        batch(i, l, 0, f1(4, 5))
                        batch(i, l, 2, receptance)
                        batch(i, l, 0, f1(6, 7))
                        batch(i, l, 2, key)
                        batch(i, l, 1, turn)
                    pipeline3(pe, iteration)

                @block.vector
                def _(v):
                    v.memset(zz[:, :, 0:1], 0.0)

                    def iteration(i, l, _):
                        def bias(b, l_):
                            after(v, hrelu_done, HC * (b - 1))
                            v.tensor_scalar(hbs[l_ % 2][:, :], hb[:, :, bass.ds(b, 1)].rearrange("p c o -> p (c o)"), 1.0, None, ALU.mult).then_inc(hbs_ready, 1)

                        def quantise(*chunks):
                            def piece(b, l_):
                                for c in chunks:
                                    v.wait_ge(hrelu_done, HC * b + c + 1)
                                    if c == 0:
                                        after(v, f2_done, b - 1)
                                    v.tensor_scalar(hq[l_ % 2][:, c, :], hr4[:, c % 4, :], ROUND, ROUND, ALU.add, ALU.subtract).then_inc(hround_done, 1)
                            return piece

                        def mix(dst, mu):
                            for c in range(KC):
                                last = v.scalar_tensor_tensor(out=dst[:, c, :], in0=zd[:, c, :], scalar=col(mu, c), in1=zz[:, c, 0:T],
                                                              op0=ALU.mult, op1=ALU.add)
                            last.then_inc(mix_done, 1)

                        def mix_r(b, _):
                            v.wait_ge(zd_ready, b + 1)
                            mix(xr, "mu_r")

                        def mix_k(b, _):
                            mix(xk, "mu_k")

                        def low(dst, src, hi_sem, lo_sem, uses, nth):
                            def piece(b, _):
                                v.wait_ge(hi_sem, uses * b + nth)
                                if src is ks:
                                    v.wait_ge(ksq_ready, b + 1)
                                v.tensor_tensor(dst[1][:, :, :], src, dst[0][:, :, :].bitcast(F32), ALU.subtract).then_inc(lo_sem, 1)
                            return piece

                        def x4(b, l_):
                            v.wait_ge(f2_done, b + 1)
                            v.wait_ge(xb_ready, b + 1)
                            v.scalar_tensor_tensor(out=fl_(xt[l_]), in0=f2k_ps[:, :], scalar=oscale[:, O_F2:O_F2 + 1], in1=fl_(xt[l_]),
                                                   op0=ALU.mult, op1=ALU.add).then_inc(x4_ready, 1)

                        def moments(b, l_):
                            v.wait_ge(x4_ready, b + 1)
                            after(v, xn4, b)
                            st = Steps(v, v_fin, KF3 * b)
                            stats(st, xt[l_], st6, me, va, vt, ve4)
                            assert st.n == KF3, st.n

                        def scaled_mean(b, _):
                            v.wait_ge(rs4, b + 1)
                            v.scalar_tensor_tensor(out=nm[:, :], in0=me[:, :], scalar=-1.0, in1=rr[:, :], op0=ALU.mult, op1=ALU.mult).then_inc(nm_ready, 1)

                        def gate(b, l_):
                            v.wait_ge(v_done, b + 1)
                            v.wait_ge(tr_ready, b + 1)
                            after(v, y_ready, b)
                            v.scalar_tensor_tensor(out=fl_(yo), in0=tr[l_ % 2], scalar=1.0, in1=v_ps[:, :], op0=ALU.add, op1=ALU.mult).then_inc(yo_done, 1)

                        def square(b, _):
                            v.wait_ge(kr_ready, b + 1)
                            v.tensor_tensor(ks, kr, kr, ALU.mult).then_inc(ksq_ready, 1)
                        batch(i, l, 0, bias)
                        batch(i, l, 0, quantise(0, 1))
                        batch(i, l, 2, mix_r)
                        batch(i, l, 2, mix_k)
                        batch(i, l, 2, low(pr_, xr, rk_hi, rk_lo, 2, 1))
                        batch(i, l, 1, x4)
                        batch(i, l, 0, quantise(2))
                        batch(i, l, 2, low(pk, xk, rk_hi, rk_lo, 2, 2))
                        batch(i, l, 1, moments)
                        batch(i, l, 0, quantise(3))
                        batch(i, l, 1, scaled_mean)
                        batch(i, l, 0, quantise(4, 5))
                        batch(i, l, 0, quantise(6, 7))
                        batch(i, l, 3, gate)
                        batch(i, l, 2, square)
                        batch(i, l, 2, low(pv, ks, v_hi, v_lo, 1, 1))
                    pipeline3(v, iteration)
            stack.pop()
        ff_scope.close()
        stack.pop()
    return nc


def kernel(**inputs):
    import numpy as np
    import concourse.bacc as bacc
    from concourse.bass_utils import run_bass_kernel_spmd

    g = lambda name: np.asarray(inputs[name])
    c = np.ascontiguousarray
    chunks = lambda name: g(name).reshape(-1, P)
    arrays = {
        "x": c(g("x")),
        "ctxT": c(g("ctx_768").reshape(NCTX, D).T),
        "WkT": c(g("L0_xattn_Wk").T), "WvT": c(g("L0_xattn_Wv").T), "Wq": c(g("L0_xattn_Wq")),
        "Wr": c(g("L0_ffn_Wr")), "Wv": c(g("L0_ffn_Wv")), "Wo": c(g("L0_ffn_Wo")), "WsT": c(g("L0_ffn_Ws").T),
        "K": c(g("L0_ffn_K_rwkv").reshape(2 * C, H)), "V": c(g("L0_ffn_V_rwkv").reshape(2 * H, C)),
        "W1": c(g("L0_ffn_W1")), "W2": c(g("L0_ffn_W2")), "W3": c(g("L0_ffn_W3")),
        "wb": c(np.concatenate([g("L0_ffn_conf_rwkv").T, g("L0_ffn_conf_trans")[:, None],
                                g("L0_ffn_w_diff")[:, None], g("L0_ffn_W_aff")], axis=1)),
        "d2v": c(g("L1_xattn_W_d2v").T), "img": c(g("L1_xattn_W_img").T), "txt": c(g("L1_xattn_W_txt").T),
        "att": c(np.concatenate([g("L1_xattn_W_att0").T, g("L1_xattn_W_att1").T], axis=1)),
        "f1": c(g("L1_xattn_W_f1").T), "f2": c(g("L1_xattn_W_f2").T),
        "rT": c(g("L1_ffn_W_r").T), "kT": c(g("L1_ffn_W_k").T), "vT": c(g("L1_ffn_W_v").T),
        "rows": c(np.concatenate([g("L0_xattn_bv"), g("L1_xattn_b_f2"), g("L0_ffn_capital_shares")])),
    }
    packed = {"bq": "L0_xattn_bq", "bk": "L0_xattn_bk", "ln1_w": "L0_ffn_ln1_w", "ln1_b": "L0_ffn_ln1_b",
              "ln2_w": "L0_ffn_ln2_w", "ln2_b": "L0_ffn_ln2_b", "b_d2v": "L1_xattn_b_d2v", "b_img": "L1_xattn_b_img",
              "b_txt": "L1_xattn_b_txt", "b_att0": "L1_xattn_b_att0", "b_att1": "L1_xattn_b_att1",
              "b_f1": "L1_xattn_b_f1", "mu_r": "L1_ffn_mu_r", "mu_k": "L1_ffn_mu_k"}
    arrays["cols"] = c(np.concatenate([chunks(packed[name]) for name in COLS]).T)

    nc = bacc.Bacc("TRN2", target_bir_lowering=False, num_devices=1)
    aps = {n: nc.dram_tensor("in_" + n, v.shape, mybir.dt.from_np(v.dtype), kind="ExternalInput").ap()
           for n, v in arrays.items()}
    out = nc.dram_tensor("out_0", (B, T, C), F32, kind="ExternalOutput").ap()
    build(nc, aps, out)
    r = run_bass_kernel_spmd(nc, [{"in_" + n: v for n, v in arrays.items()}], core_ids=[0])
    return r.results[0]["out_0"]
```
